# Optimizing a Trainium2 kernel written in Bass

```python
import numpy as np
import jax
import jax.numpy as jnp

def _softmax(x, axis=-1):
    return jax.nn.softmax(x, axis=axis)

def _gelu(x):
    return jax.nn.gelu(x, approximate=True)

def _silu(x):
    return jax.nn.silu(x)

def _sigmoid(x):
    return jax.nn.sigmoid(x)

def _layernorm(x, axis=-1, eps=1e-05):
    m = jnp.mean(x, axis=axis, keepdims=True)
    v = jnp.var(x, axis=axis, keepdims=True)
    return (x - m) / jnp.sqrt(v + eps)

def _scatter_add(tgt, idx, src, axis=0):
    return tgt.at[idx].add(src)

def _segment_sum(src, seg, n):
    return jax.ops.segment_sum(src, seg, n)
kernel_name = 'mk_adaln_d1_jaxref_r8_baebe2'

def setup_inputs(seed: int=0):
    np.random.seed(seed)
    _w = jnp.asarray

    def _L0_attn_setup():
        import jax, jax.numpy as jnp
        import numpy as np
        B, S, HID = (4, 256, 128)
        E, K, H = (8, 2, 8)
        DK = HID // H
        DV = HID // H
        CAP = int(S * 1.0)
        CHUNK = 64
        EPS = 1e-05

        def chunk_linear_attn(q, k, v):
            Bt, T, Hh, Dk = q.shape
            Dv = v.shape[-1]
            nc = T // CHUNK
            q = q * Dk ** (-0.5)
            qc = q.reshape(Bt, nc, CHUNK, Hh, Dk).transpose(1, 0, 2, 3, 4)
            kc = k.reshape(Bt, nc, CHUNK, Hh, Dk).transpose(1, 0, 2, 3, 4)
            vc = v.reshape(Bt, nc, CHUNK, Hh, Dv).transpose(1, 0, 2, 3, 4)
            causal = jnp.tril(jnp.ones((CHUNK, CHUNK), q.dtype))

            def step(Sst, qkv):
                qb, kb, vb = qkv
                attn = jnp.einsum('bihd,bjhd->bhij', qb, kb) * causal
                intra = jnp.einsum('bhij,bjhe->bihe', attn, vb)
                inter = jnp.einsum('bihd,bhde->bihe', qb, Sst)
                Sst = Sst + jnp.einsum('bjhd,bjhe->bhde', kb, vb)
                return (Sst, intra + inter)
            S0 = jnp.zeros((Bt, Hh, Dk, Dv), q.dtype)
            _, o = jax.lax.scan(step, S0, (qc, kc, vc))
            return o.transpose(1, 0, 2, 3, 4).reshape(Bt, T, Hh, Dv)

        def _forward(x, gate_w, q_w, k_w, v_w, fmq1_w, fmq2_w, fmk1_w, fmk2_w, norm_w, o_w):
            b, s0, d = x.shape
            logits = jnp.einsum('bsd,ed->bse', x, gate_w)
            scores = jax.nn.softmax(logits.astype(jnp.float32), axis=-1)
            rw, sel = jax.lax.top_k(scores, K)
            rw = (rw / rw.sum(-1, keepdims=True)).astype(x.dtype)
            routing_mask = jax.nn.one_hot(sel, E, dtype=jnp.int32).sum(2)
            s = s0 * K
            x_rep = jnp.repeat(x, K, axis=1).reshape(b * s, d)
            sel_flat = sel.reshape(b * s).astype(jnp.int32)
            batch_idx = jnp.repeat(jnp.arange(b, dtype=jnp.int32), s)
            combined = batch_idx * E + sel_flat
            sorted_indices = jnp.argsort(combined)
            x_sorted = x_rep[sorted_indices]
            tokens = routing_mask.sum(axis=1)
            flat_off = (jnp.cumsum(tokens, axis=1) + (jnp.arange(b, dtype=jnp.int32) * s)[:, None]).reshape(-1)
            starts = jnp.concatenate([jnp.zeros((1,), flat_off.dtype), flat_off[:-1]])
            idx = starts[:, None] + jnp.arange(CAP, dtype=flat_off.dtype)[None, :]
            shift = jnp.maximum(tokens.reshape(-1) - CAP, 0)
            tidx = idx + shift[:, None]
            dmask = tidx < flat_off[:, None]
            tidx = jnp.where(dmask, tidx, 0)
            xe = x_sorted[tidx.reshape(-1)].reshape(b * E, CAP, d) * dmask[..., None].astype(x.dtype)
            xe = xe.reshape(b, E, CAP, d).transpose(1, 0, 2, 3)
            q = jnp.einsum('ebtc,kc->ebtk', xe, q_w).reshape(E, b, CAP, H, DK)
            k = jnp.einsum('ebtc,ekc->ebtk', xe, k_w).reshape(E, b, CAP, H, DK)
            v = jnp.einsum('ebtc,ekc->ebtk', xe, v_w).reshape(E, b, CAP, H, DV)
            q = jnp.einsum('...d,kd->...k', q, fmq1_w) * jnp.einsum('...d,kd->...k', q, fmq2_w)
            k = jnp.einsum('...d,kd->...k', k, fmk1_w) * jnp.einsum('...d,kd->...k', k, fmk2_w)
            o = chunk_linear_attn(q.reshape(E * b, CAP, H, DK), k.reshape(E * b, CAP, H, DK), v.reshape(E * b, CAP, H, DV))
            oflat = o.reshape(E, b, CAP, H, DV).transpose(1, 0, 2, 3, 4).reshape(b * E * CAP, H, DV)
            oflat = oflat * dmask.reshape(-1)[:, None, None].astype(o.dtype)
            res = jnp.zeros((b * s, H, DV), o.dtype).at[tidx.reshape(-1)].add(oflat)
            inv = jnp.argsort(sorted_indices)
            restored = res[inv].reshape(b, s0, K, H, DV)
            out = (restored * rw[..., None, None]).sum(axis=2)
            out = out * jax.lax.rsqrt(jnp.mean(out * out, axis=-1, keepdims=True) + EPS) * norm_w
            out = out.reshape(b, s0, H * DV)
            return jnp.einsum('bsv,dv->bsd', out, o_w)
        key = jax.random.key(seed)
        ks = jax.random.split(key, 12)
        std = 0.02
        return {'x': jax.random.normal(ks[0], (B, S, HID), jnp.float32), 'gate_w': jax.random.normal(ks[1], (E, HID), jnp.float32) * std, 'q_w': jax.random.normal(ks[2], (HID, HID), jnp.float32) * std, 'k_w': jax.random.normal(ks[3], (E, HID, HID), jnp.float32) * std, 'v_w': jax.random.normal(ks[4], (E, HID, HID), jnp.float32) * std, 'fmq1_w': jax.random.normal(ks[5], (DK, DK), jnp.float32) * std, 'fmq2_w': jax.random.normal(ks[6], (DK, DK), jnp.float32) * std, 'fmk1_w': jax.random.normal(ks[7], (DK, DK), jnp.float32) * std, 'fmk2_w': jax.random.normal(ks[8], (DK, DK), jnp.float32) * std, 'norm_w': jnp.ones((DV,), jnp.float32), 'o_w': jax.random.normal(ks[9], (HID, HID), jnp.float32) * std}
    _L0_attn_in = _L0_attn_setup()

    def _L0_ffn_setup():
        import jax, jax.numpy as jnp
        import numpy as np
        B, S, D = (2, 256, 128)
        E, K, H = (8, 4, 128)
        SH = 2 * H

        def _silu(x):
            return x * jax.nn.sigmoid(x)

        def _swiglu(x, w1, b1, w2, b2):
            return _silu(x @ w1 + b1) * (x @ w2 + b2)

        def _moe(x, gate_w, exp_w1, exp_w3, exp_w2, sh_w1, sh_w3, sh_w2):
            b, s, d = x.shape
            t = b * s
            xt = x.reshape(t, d)
            scores = jax.nn.softmax(xt @ gate_w.T, axis=-1)
            topv, topi = jax.lax.top_k(scores, K)
            topv = topv / jnp.sum(topv, axis=-1, keepdims=True)
            combine = jnp.zeros((t, E), xt.dtype).at[jnp.arange(t)[:, None], topi].set(topv)
            g = _silu(jnp.einsum('td,edh->eth', xt, exp_w1))
            u = jnp.einsum('td,edh->eth', xt, exp_w3)
            yexp = jnp.einsum('eth,ehd->etd', g * u, exp_w2)
            routed = jnp.einsum('te,etd->td', combine, yexp)
            shared = _silu(xt @ sh_w1) * (xt @ sh_w3) @ sh_w2
            return (routed + shared).reshape(b, s, d)
        key = jax.random.key(seed)
        ks = jax.random.split(key, 24)
        f = lambda k, shape: jax.random.normal(k, shape, dtype=jnp.float32) * 0.02
        return {'x': jax.random.normal(ks[0], (B, S, D), dtype=jnp.float32), 'lin0_w': f(ks[1], (D, D)), 'lin0_b': f(ks[2], (D,)), 'swi1_w1': f(ks[3], (D, D)), 'swi1_b1': f(ks[4], (D,)), 'swi1_w2': f(ks[5], (D, D)), 'swi1_b2': f(ks[6], (D,)), 'gate_w': f(ks[7], (E, D)), 'exp_w1': f(ks[8], (E, D, H)), 'exp_w3': f(ks[9], (E, D, H)), 'exp_w2': f(ks[10], (E, H, D)), 'sh_w1': f(ks[11], (D, SH)), 'sh_w3': f(ks[12], (D, SH)), 'sh_w2': f(ks[13], (SH, D)), 'lin1_w': f(ks[14], (D, D)), 'lin1_b': f(ks[15], (D,)), 'swi2_w1': f(ks[16], (D, D)), 'swi2_b1': f(ks[17], (D,)), 'swi2_w2': f(ks[18], (D, D)), 'swi2_b2': f(ks[19], (D,))}
    _L0_ffn_in = _L0_ffn_setup()
    _L0_c = _w((lambda *s: np.random.randn(*s).astype(np.float32) * 0.05)(16, 128))
    _L0_wmod = _w((lambda *s: np.random.randn(*s).astype(np.float32) * 0.05)(128, 6 * 128) * 128 ** (-0.5))
    _d = {'L0_attn_x': _L0_attn_in['x'], 'L0_attn_gate_w': _L0_attn_in['gate_w'], 'L0_attn_q_w': _L0_attn_in['q_w'], 'L0_attn_k_w': _L0_attn_in['k_w'], 'L0_attn_v_w': _L0_attn_in['v_w'], 'L0_attn_fmq1_w': _L0_attn_in['fmq1_w'], 'L0_attn_fmq2_w': _L0_attn_in['fmq2_w'], 'L0_attn_fmk1_w': _L0_attn_in['fmk1_w'], 'L0_attn_fmk2_w': _L0_attn_in['fmk2_w'], 'L0_attn_norm_w': _L0_attn_in['norm_w'], 'L0_attn_o_w': _L0_attn_in['o_w'], 'L0_ffn_lin0_w': _L0_ffn_in['lin0_w'], 'L0_ffn_lin0_b': _L0_ffn_in['lin0_b'], 'L0_ffn_swi1_w1': _L0_ffn_in['swi1_w1'], 'L0_ffn_swi1_b1': _L0_ffn_in['swi1_b1'], 'L0_ffn_swi1_w2': _L0_ffn_in['swi1_w2'], 'L0_ffn_swi1_b2': _L0_ffn_in['swi1_b2'], 'L0_ffn_gate_w': _L0_ffn_in['gate_w'], 'L0_ffn_exp_w1': _L0_ffn_in['exp_w1'], 'L0_ffn_exp_w3': _L0_ffn_in['exp_w3'], 'L0_ffn_exp_w2': _L0_ffn_in['exp_w2'], 'L0_ffn_sh_w1': _L0_ffn_in['sh_w1'], 'L0_ffn_sh_w3': _L0_ffn_in['sh_w3'], 'L0_ffn_sh_w2': _L0_ffn_in['sh_w2'], 'L0_ffn_lin1_w': _L0_ffn_in['lin1_w'], 'L0_ffn_lin1_b': _L0_ffn_in['lin1_b'], 'L0_ffn_swi2_w1': _L0_ffn_in['swi2_w1'], 'L0_ffn_swi2_b1': _L0_ffn_in['swi2_b1'], 'L0_ffn_swi2_w2': _L0_ffn_in['swi2_w2'], 'L0_ffn_swi2_b2': _L0_ffn_in['swi2_b2'], 'L0_c': _L0_c, 'L0_wmod': _L0_wmod}
    _x0 = _d['L0_attn_x']
    _d['L0_attn_x'] = jax.random.normal(jax.random.fold_in(jax.random.key(seed), 1), (16, 512, 128), dtype=_x0.dtype)
    del _x0
    return _d

def reference(L0_attn_x, L0_attn_gate_w, L0_attn_q_w, L0_attn_k_w, L0_attn_v_w, L0_attn_fmq1_w, L0_attn_fmq2_w, L0_attn_fmk1_w, L0_attn_fmk2_w, L0_attn_norm_w, L0_attn_o_w, L0_ffn_lin0_w, L0_ffn_lin0_b, L0_ffn_swi1_w1, L0_ffn_swi1_b1, L0_ffn_swi1_w2, L0_ffn_swi1_b2, L0_ffn_gate_w, L0_ffn_exp_w1, L0_ffn_exp_w3, L0_ffn_exp_w2, L0_ffn_sh_w1, L0_ffn_sh_w3, L0_ffn_sh_w2, L0_ffn_lin1_w, L0_ffn_lin1_b, L0_ffn_swi2_w1, L0_ffn_swi2_b1, L0_ffn_swi2_w2, L0_ffn_swi2_b2, L0_c, L0_wmod):

    def _L0_attn_ref(x, gate_w, q_w, k_w, v_w, fmq1_w, fmq2_w, fmk1_w, fmk2_w, norm_w, o_w):
        import jax, jax.numpy as jnp
        import numpy as np
        B, S, HID = (4, 256, 128)
        E, K, H = (8, 2, 8)
        DK = HID // H
        DV = HID // H
        CAP = int(S * 1.0)
        CHUNK = 64
        EPS = 1e-05

        def chunk_linear_attn(q, k, v):
            Bt, T, Hh, Dk = q.shape
            Dv = v.shape[-1]
            nc = T // CHUNK
            q = q * Dk ** (-0.5)
            qc = q.reshape(Bt, nc, CHUNK, Hh, Dk).transpose(1, 0, 2, 3, 4)
            kc = k.reshape(Bt, nc, CHUNK, Hh, Dk).transpose(1, 0, 2, 3, 4)
            vc = v.reshape(Bt, nc, CHUNK, Hh, Dv).transpose(1, 0, 2, 3, 4)
            causal = jnp.tril(jnp.ones((CHUNK, CHUNK), q.dtype))

            def step(Sst, qkv):
                qb, kb, vb = qkv
                attn = jnp.einsum('bihd,bjhd->bhij', qb, kb) * causal
                intra = jnp.einsum('bhij,bjhe->bihe', attn, vb)
                inter = jnp.einsum('bihd,bhde->bihe', qb, Sst)
                Sst = Sst + jnp.einsum('bjhd,bjhe->bhde', kb, vb)
                return (Sst, intra + inter)
            S0 = jnp.zeros((Bt, Hh, Dk, Dv), q.dtype)
            _, o = jax.lax.scan(step, S0, (qc, kc, vc))
            return o.transpose(1, 0, 2, 3, 4).reshape(Bt, T, Hh, Dv)

        def _forward(x, gate_w, q_w, k_w, v_w, fmq1_w, fmq2_w, fmk1_w, fmk2_w, norm_w, o_w):
            b, s0, d = x.shape
            logits = jnp.einsum('bsd,ed->bse', x, gate_w)
            scores = jax.nn.softmax(logits.astype(jnp.float32), axis=-1)
            rw, sel = jax.lax.top_k(scores, K)
            rw = (rw / rw.sum(-1, keepdims=True)).astype(x.dtype)
            routing_mask = jax.nn.one_hot(sel, E, dtype=jnp.int32).sum(2)
            s = s0 * K
            x_rep = jnp.repeat(x, K, axis=1).reshape(b * s, d)
            sel_flat = sel.reshape(b * s).astype(jnp.int32)
            batch_idx = jnp.repeat(jnp.arange(b, dtype=jnp.int32), s)
            combined = batch_idx * E + sel_flat
            sorted_indices = jnp.argsort(combined)
            x_sorted = x_rep[sorted_indices]
            tokens = routing_mask.sum(axis=1)
            flat_off = (jnp.cumsum(tokens, axis=1) + (jnp.arange(b, dtype=jnp.int32) * s)[:, None]).reshape(-1)
            starts = jnp.concatenate([jnp.zeros((1,), flat_off.dtype), flat_off[:-1]])
            idx = starts[:, None] + jnp.arange(CAP, dtype=flat_off.dtype)[None, :]
            shift = jnp.maximum(tokens.reshape(-1) - CAP, 0)
            tidx = idx + shift[:, None]
            dmask = tidx < flat_off[:, None]
            tidx = jnp.where(dmask, tidx, 0)
            xe = x_sorted[tidx.reshape(-1)].reshape(b * E, CAP, d) * dmask[..., None].astype(x.dtype)
            xe = xe.reshape(b, E, CAP, d).transpose(1, 0, 2, 3)
            q = jnp.einsum('ebtc,kc->ebtk', xe, q_w).reshape(E, b, CAP, H, DK)
            k = jnp.einsum('ebtc,ekc->ebtk', xe, k_w).reshape(E, b, CAP, H, DK)
            v = jnp.einsum('ebtc,ekc->ebtk', xe, v_w).reshape(E, b, CAP, H, DV)
            q = jnp.einsum('...d,kd->...k', q, fmq1_w) * jnp.einsum('...d,kd->...k', q, fmq2_w)
            k = jnp.einsum('...d,kd->...k', k, fmk1_w) * jnp.einsum('...d,kd->...k', k, fmk2_w)
            o = chunk_linear_attn(q.reshape(E * b, CAP, H, DK), k.reshape(E * b, CAP, H, DK), v.reshape(E * b, CAP, H, DV))
            oflat = o.reshape(E, b, CAP, H, DV).transpose(1, 0, 2, 3, 4).reshape(b * E * CAP, H, DV)
            oflat = oflat * dmask.reshape(-1)[:, None, None].astype(o.dtype)
            res = jnp.zeros((b * s, H, DV), o.dtype).at[tidx.reshape(-1)].add(oflat)
            inv = jnp.argsort(sorted_indices)
            restored = res[inv].reshape(b, s0, K, H, DV)
            out = (restored * rw[..., None, None]).sum(axis=2)
            out = out * jax.lax.rsqrt(jnp.mean(out * out, axis=-1, keepdims=True) + EPS) * norm_w
            out = out.reshape(b, s0, H * DV)
            return jnp.einsum('bsv,dv->bsd', out, o_w)
        return _forward(x, gate_w, q_w, k_w, v_w, fmq1_w, fmq2_w, fmk1_w, fmk2_w, norm_w, o_w)

    def _L0_ffn_ref(x, lin0_w, lin0_b, swi1_w1, swi1_b1, swi1_w2, swi1_b2, gate_w, exp_w1, exp_w3, exp_w2, sh_w1, sh_w3, sh_w2, lin1_w, lin1_b, swi2_w1, swi2_b1, swi2_w2, swi2_b2):
        import jax, jax.numpy as jnp
        import numpy as np
        B, S, D = (2, 256, 128)
        E, K, H = (8, 4, 128)
        SH = 2 * H

        def _silu(x):
            return x * jax.nn.sigmoid(x)

        def _swiglu(x, w1, b1, w2, b2):
            return _silu(x @ w1 + b1) * (x @ w2 + b2)

        def _moe(x, gate_w, exp_w1, exp_w3, exp_w2, sh_w1, sh_w3, sh_w2):
            b, s, d = x.shape
            t = b * s
            xt = x.reshape(t, d)
            scores = jax.nn.softmax(xt @ gate_w.T, axis=-1)
            topv, topi = jax.lax.top_k(scores, K)
            topv = topv / jnp.sum(topv, axis=-1, keepdims=True)
            combine = jnp.zeros((t, E), xt.dtype).at[jnp.arange(t)[:, None], topi].set(topv)
            g = _silu(jnp.einsum('td,edh->eth', xt, exp_w1))
            u = jnp.einsum('td,edh->eth', xt, exp_w3)
            yexp = jnp.einsum('eth,ehd->etd', g * u, exp_w2)
            routed = jnp.einsum('te,etd->td', combine, yexp)
            shared = _silu(xt @ sh_w1) * (xt @ sh_w3) @ sh_w2
            return (routed + shared).reshape(b, s, d)
        h = x @ lin0_w + lin0_b
        h = _swiglu(h, swi1_w1, swi1_b1, swi1_w2, swi1_b2)
        h = _moe(h, gate_w, exp_w1, exp_w3, exp_w2, sh_w1, sh_w3, sh_w2)
        h = h @ lin1_w + lin1_b
        h = _swiglu(h, swi2_w1, swi2_b1, swi2_w2, swi2_b2)
        return h
    x = L0_attn_x
    mod = (_silu(L0_c) @ L0_wmod).reshape(L0_c.shape[0], 6, 1, -1)
    sa, ca, ga, sb, cb, gb = (mod[:, 0], mod[:, 1], mod[:, 2], mod[:, 3], mod[:, 4], mod[:, 5])
    ga = (2 * (ga >= 0) - 1) * jnp.maximum(jnp.abs(ga), 0.25)
    gb = (2 * (gb >= 0) - 1) * jnp.maximum(jnp.abs(gb), 0.25)
    h = _layernorm(x, axis=-1) * (1 + ca) + sa
    x = x + ga * _L0_attn_ref(h, L0_attn_gate_w, L0_attn_q_w, L0_attn_k_w, L0_attn_v_w, L0_attn_fmq1_w, L0_attn_fmq2_w, L0_attn_fmk1_w, L0_attn_fmk2_w, L0_attn_norm_w, L0_attn_o_w)
    h = _layernorm(x, axis=-1) * (1 + cb) + sb
    x = x + gb * _L0_ffn_ref(h, L0_ffn_lin0_w, L0_ffn_lin0_b, L0_ffn_swi1_w1, L0_ffn_swi1_b1, L0_ffn_swi1_w2, L0_ffn_swi1_b2, L0_ffn_gate_w, L0_ffn_exp_w1, L0_ffn_exp_w3, L0_ffn_exp_w2, L0_ffn_sh_w1, L0_ffn_sh_w3, L0_ffn_sh_w2, L0_ffn_lin1_w, L0_ffn_lin1_b, L0_ffn_swi2_w1, L0_ffn_swi2_b1, L0_ffn_swi2_w2, L0_ffn_swi2_b2)
    return x

_drawn_inputs = setup_inputs


def setup_inputs(seed=0):
    import zlib

    import numpy as np

    out = dict(_drawn_inputs(seed))
    spreads = {'L0_attn_norm_w': (1.0, 0.2)}
    factors = {}
    for name, (base, spread) in spreads.items():
        noise = np.random.default_rng([zlib.crc32(name.encode()), seed]).standard_normal(out[name].shape)
        drawn = base * np.exp(spread * noise) if base else spread * noise
        out[name] = jnp.asarray(drawn.astype(out[name].dtype))
    for name, factor in factors.items():
        out[name] = (out[name] * factor).astype(out[name].dtype)
    return out
```

```python
from contextlib import ExitStack

import concourse.bass as bass
from concourse import mybir

ALU = mybir.AluOpType
ACT = mybir.ActivationFunctionType
AX = mybir.AxisListType
F32 = mybir.dt.float32
BF16 = mybir.dt.bfloat16
U32 = mybir.dt.uint32

P = 128
D = 128
NB = 16
S = 512
NT = S // P
TILES = NB * NT
E = 8
TOPA = 2
TOPF = 4
CAP = 256
H = 8
DK = 16
C = 64
NCH = CAP // C
ROW = 2 * D
G = NB * E
SH = 2
EPS = 1e-5
FAR = 1.0e6
LOW = -1.0e30


def bcast(ap, shape):
    return ap.to_broadcast(shape) if hasattr(ap, "to_broadcast") else ap.broadcast_to(shape)


def adaln_block(nc, x, gate_wT, q_w, k_w, v_wT, fmT, norm_c, o_wT, lin0, lin0_b, s1w1, s1b1, s1w2, s1b2, fgateT,
                ew1, ew3, ew2, shw1, shw3, shw2, lin1, lin1_b, s2w1, s2b1, s2w2, s2b2, cT, wmod, out):
    ctx = ExitStack()
    with ctx:
        def sb(name, shape, dt=F32):
            return ctx.enter_context(nc.sbuf_tensor(name, shape, dt))

        def sem(name):
            return ctx.enter_context(nc.semaphore(name))

        hs = nc.dram_tensor("routed_rows", [(G + 1) * CAP, ROW], F32, kind="Internal").ap()
        osd = nc.dram_tensor("attended_rows", [G * CAP, D], F32, kind="Internal").ap()

        bank = [ctx.enter_context(nc.psum_tensor(f"bank{i}", [P, 512], F32)) for i in range(8)]

        x_all = sb("x_all", [P, TILES, D])
        hq = sb("hq", [P, TILES, ROW])
        ident = sb("ident", [P, P])
        identb = sb("identb", [P, P], BF16)
        headm = sb("headm", [P, P])
        parity = sb("parity", [P, 2])
        causal = sb("causal", [P, C])
        tri = sb("tri", [P, P], BF16)
        ones = sb("ones", [P, P], BF16)
        sel24 = sb("sel24", [3 * E, E, P], BF16)
        eslot = sb("eslot", [P, E])
        erow = sb("erow", [P, NB, E])
        mods = sb("mods", [P, 6, NB])
        k1T = sb("k1T", [P, E, P])
        k2T = sb("k2T", [P, E, P])
        q1T = sb("q1T", [P, P])
        q2T = sb("q2T", [P, P])
        vT = sb("vT", [P, E, P])
        oT = sb("oT", [P, P])
        gA = sb("gA", [P, E])
        gF = sb("gF", [P, E])
        mat = sb("mat", [P, 6, P])
        bias = sb("bias", [P, 6])
        w1s = sb("w1s", [P, E + SH, P])
        w3s = sb("w3s", [P, E + SH, P])
        w2s = sb("w2s", [P, E + SH, P])
        stats = sb("stats", [P, TILES, 6])
        mean = sb("mean", [P, TILES])
        rstd = sb("rstd", [P, TILES])
        lg = sb("lg", [P, TILES, E])
        wslot = sb("wslot", [P, TILES, TOPA])
        idxs = sb("idxs", [P, TILES, TOPA], U32)
        idxg = sb("idxg", [P, TILES, TOPA], U32)
        w24 = sb("w24", [P, TILES, 3 * E], BF16)

        ph = ExitStack()
        zero = ph.enter_context(nc.sbuf_tensor("zero", [P, CAP * E // P * ROW], F32))
        kw_raw = ph.enter_context(nc.sbuf_tensor("kw_raw", [P, E, P], F32))
        q_raw = ph.enter_context(nc.sbuf_tensor("q_raw", [P, P], F32))
        fm = ph.enter_context(nc.sbuf_tensor("fm", [P, 4, P], F32))
        cT_s = ph.enter_context(nc.sbuf_tensor("cT_s", [P, NB], F32))
        wmod_s = ph.enter_context(nc.sbuf_tensor("wmod_s", [P, 6 * P], F32))
        normc = ph.enter_context(nc.sbuf_tensor("normc", [P, 1], F32))
        sgn = ph.enter_context(nc.sbuf_tensor("sgn", [P, NB], F32))
        xh = ph.enter_context(nc.sbuf_tensor("xh", [P, 2, NT, D], F32))
        hT = ph.enter_context(nc.sbuf_tensor("hT", [P, 2, S], F32))
        q1s = ph.enter_context(nc.sbuf_tensor("q1s", [P, 2, S], F32))
        qT = ph.enter_context(nc.sbuf_tensor("qT", [P, 2, S], F32))
        tw = [ph.enter_context(nc.sbuf_tensor(f"tw{i}", [P, TILES, E], F32)) for i in range(4)]
        ta = [ph.enter_context(nc.sbuf_tensor(f"ta{i}", [P, TILES], F32)) for i in range(3)]
        selp = ph.enter_context(nc.sbuf_tensor("selp", [P, TILES, E], F32))
        selb = ph.enter_context(nc.sbuf_tensor("selb", [P, TILES, E], BF16))

        MASKS = 18
        NW = 8 + 6 + 6 + 8

        s_x = [sem(f"x_loaded{i}") for i in range(4)]
        s_w = sem("weights_loaded")
        s_mask = sem("masks_made")
        s_pmask = sem("parity_made")
        s_zero = sem("zero_made")
        s_zfill = sem("rows_zeroed")
        s_silu = sem("c_silu")
        s_mod = sem("mod_product")
        s_fold = sem("kq_folded")
        s_wcopy = sem("folded_copied")
        s_bd = sem("features_masked")
        s_ch = sem("vector_chain")
        s_var = sem("variance_ready")
        s_sq = sem("deviation_ready")
        s_mods = sem("mods_ready")
        s_xh = sem("normalised")
        s_xT = sem("normalised_turned")
        s_hT = sem("modulated")
        s_qp = sem("q_products")
        s_q1 = sem("q1_copied")
        s_qf = sem("q_features")
        s_hb = sem("h_and_logits")
        s_hqh = sem("h_rows_kept")
        s_lg = sem("logits_kept")
        s_qb = sem("q_turned")
        s_hqq = sem("q_rows_kept")
        s_e0 = sem("exponent_in")
        s_e1 = sem("exponent_out")
        s_selb = sem("selection_ready")
        s_cnt = sem("counts_ready")

        def newton(dve, link, dev, var, y, t):
            link(dve.reciprocal(y, dev))
            link(dve.tensor_tensor(t, y, y, ALU.mult))
            link(dve.tensor_tensor(t, t, var, ALU.mult))
            link(dve.tensor_scalar(t, t, -0.5, 1.5, ALU.mult, ALU.add))
            link(dve.tensor_tensor(y, y, t, ALU.mult))

        def norm_stats(dve, link, var, t):
            link(dve.tensor_tensor(mean[:, :], stats[:, :, 1], stats[:, :, 4], ALU.add))
            link(dve.tensor_scalar(mean[:, :], mean[:, :], 0.5, None, ALU.mult))
            link(dve.tensor_tensor(t, stats[:, :, 1], stats[:, :, 4], ALU.subtract))
            link(dve.tensor_tensor(t, t, t, ALU.mult))
            link(dve.tensor_scalar(t, t, 0.25, EPS, ALU.mult, ALU.add))
            link(dve.tensor_tensor(var, stats[:, :, 2], stats[:, :, 5], ALU.add))
            link(dve.scalar_tensor_tensor(out=var, in0=var, scalar=1.0 / D, in1=t, op0=ALU.mult, op1=ALU.add))

        def pick(dve, link, left, first, t, m):
            link(dve.tensor_reduce(m, left, AX.X, ALU.max))
            mb = m.unsqueeze(2).to_broadcast([P, TILES, E])
            link(dve.tensor_tensor(t, left, mb, ALU.is_equal))
            link(dve.tensor_tensor(t, t, eslot[:, :].unsqueeze(1).to_broadcast([P, TILES, E]), ALU.mult))
            link(dve.tensor_reduce(m, t, AX.X, ALU.max))
            link(dve.tensor_tensor(first, t, mb, ALU.is_equal))

        with nc.Block() as block:
            @block.sync
            def _(sp):
                xv = x.rearrange("b (i p) d -> p (b i) d", p=P)
                q = TILES // 4
                for n in range(4):
                    sp.dma_start(x_all[:, n * q:(n + 1) * q, :], xv[:, n * q:(n + 1) * q, :]).then_inc(s_x[n], 16)
                    if n == 0:
                        for dst, src in ((cT_s[:, :], cT), (wmod_s[:, :], wmod), (q_raw[:, :], q_w),
                                         (fm[:, :, :], fmT.rearrange("f k c -> k f c")), (gA[:, :], gate_wT),
                                         (normc[:, :], norm_c), (kw_raw[:, :, :], k_w.rearrange("e k c -> k e c")),
                                         (oT[:, :], o_wT)):
                            sp.dma_start(dst, src).then_inc(s_w, 16)
                for n, src in enumerate((lin0, s1w1, s1w2, lin1, s2w1, s2w2)):
                    sp.dma_start(mat[:, n, :], src).then_inc(s_w, 16)
                for n, src in enumerate((lin0_b, s1b1, s1b2, lin1_b, s2b1, s2b2)):
                    sp.dma_start(bias[:, n:n + 1], src).then_inc(s_w, 16)
                for dst, src in ((gF[:, :], fgateT), (vT[:, :, :], v_wT.rearrange("e c k -> c e k")),
                                 (w1s[:, 0:E, :], ew1.rearrange("e d h -> d e h")),
                                 (w3s[:, 0:E, :], ew3.rearrange("e d h -> d e h")),
                                 (w2s[:, 0:E, :], ew2.rearrange("e h d -> h e d")),
                                 (w1s[:, E:E + SH, :], shw1.rearrange("d (s h) -> d s h", s=SH)),
                                 (w3s[:, E:E + SH, :], shw3.rearrange("d (s h) -> d s h", s=SH)),
                                 (w2s[:, E:E + SH, :], shw2.rearrange("(s h) d -> h s d", s=SH))):
                    sp.dma_start(dst, src).then_inc(s_w, 16)
                sp.wait_ge(s_w, 16 * NW)
                sp.wait_ge(s_zero, 1)
                zrow = CAP * E // P
                for b in range(NB):
                    sp.dma_start(hs[b * CAP * E:(b + 1) * CAP * E, :].rearrange("(p r) w -> p (r w)", r=zrow),
                                 zero[:, :]).then_inc(s_zfill, 16)
                sp.dma_start(hs[G * CAP:(G + 1) * CAP, :].rearrange("(p r) w -> p (r w)", p=P),
                             zero[:, 0:CAP // P * ROW]).then_inc(s_zfill, 16)
                sp.wait_ge(s_zfill, 16 * (NB + 1))

            @block.gpsimd
            def _(pool):
                made = [0]

                def link(ins):
                    made[0] += 1
                    ins.then_inc(s_mask, 1)
                    pool.wait_ge(s_mask, made[0])

                pool.memset(zero[:, :], 0.0).then_inc(s_zero, 1)
                link(pool.memset(ident[:, :], 0.0))
                link(pool.affine_select(out=ident[:, :], in_=ident[:, :], compare_op=ALU.not_equal, fill=1.0, base=0,
                                        pattern=[[-1, P]], channel_multiplier=1))
                link(pool.tensor_copy(identb[:, :], ident[:, :]))
                link(pool.memset(headm[:, :], 1.0))
                hv = headm[:, :].rearrange("p (h d) -> p h d", d=DK)
                link(pool.affine_select(out=hv, in_=hv, compare_op=ALU.is_ge, fill=0.0, base=0,
                                        pattern=[[-DK, H], [0, DK]], channel_multiplier=1))
                link(pool.affine_select(out=hv, in_=hv, compare_op=ALU.is_ge, fill=0.0, base=DK - 1,
                                        pattern=[[DK, H], [0, DK]], channel_multiplier=-1))
                link(pool.memset(causal[:, :], 1.0))
                link(pool.affine_select(out=causal[:, :], in_=causal[:, :], compare_op=ALU.is_ge, fill=0.0, base=C,
                                        pattern=[[1, C]], channel_multiplier=-1))
                link(pool.affine_select(out=causal[0:C, :], in_=causal[0:C, :], compare_op=ALU.is_ge, fill=0.0,
                                        base=0, pattern=[[1, C]], channel_multiplier=-1))
                link(pool.memset(tri[:, :], 1.0))
                link(pool.affine_select(out=tri[:, :], in_=tri[:, :], compare_op=ALU.is_ge, fill=0.0, base=0,
                                        pattern=[[-1, P]], channel_multiplier=1))
                link(pool.memset(ones[:, :], 1.0))
                link(pool.memset(sel24[:, :, :], 0.0))
                for part in range(3):
                    link(pool.affine_select(out=sel24[:, :, :], in_=sel24[:, :, :], compare_op=ALU.not_equal, fill=1.0,
                                            base=-part * E, pattern=[[-1, E], [0, P]], channel_multiplier=1))
                link(pool.iota(eslot[:, :], [[-1, E]], base=E, channel_multiplier=0,
                               allow_small_or_imprecise_dtypes=True))
                link(pool.iota(erow[:, :, :], [[E * CAP, NB], [CAP, E]], base=CAP, channel_multiplier=0,
                               allow_small_or_imprecise_dtypes=True))
                assert made[0] == MASKS

            @block.scalar
            def _(act):
                act.wait_ge(s_w, 16 * NW)
                act.activation(cT_s[:, :], cT_s[:, :], ACT.Silu).then_inc(s_silu, 1)
                act.wait_ge(s_fold, 1)
                act.activation(q1T[:, :], bank[7][:, 256:384], ACT.Copy).then_inc(s_wcopy, 1)
                act.activation(q2T[:, :], bank[7][:, 384:512], ACT.Copy).then_inc(s_wcopy, 1)
                for e in range(E):
                    act.wait_ge(s_fold, 2 + e)
                    act.activation(k1T[:, e, :], bank[e % 4][:, 0:P], ACT.Copy)
                    act.activation(k2T[:, e, :], bank[e % 4][:, P:2 * P], ACT.Copy).then_inc(s_wcopy, 1)
                act.wait_ge(s_var, 1)
                act.activation(ta[1][:, :], ta[0][:, :], ACT.Sqrt).then_inc(s_sq, 1)
                act.wait_ge(s_mods, 1)
                with act.Fori(0, NB // 2) as bb:
                    for u in range(2):
                        b = 2 * bb + u
                        act.wait_ge(s_xT, b + 1)
                        act.activation(hT[:, u, :], bank[u][:, :], ACT.Identity, bias=mods[:, 0, bass.ds(b, 1)],
                                       scale=mods[:, 1, bass.ds(b, 1)]).then_inc(s_hT, 1)
                        act.wait_ge(s_qp, b + 1)
                        act.activation(q1s[:, u, :], bank[2][:, :], ACT.Copy).then_inc(s_q1, 1)
                        act.wait_ge(s_hb, b + 1)
                        act.activation(hq[:, bass.ds(b * NT, NT), 0:D],
                                       bank[5][:, :].rearrange("p (i d) -> p i d", d=D), ACT.Copy).then_inc(s_hqh, 1)
                        act.wait_ge(s_qb, b + 1)
                        act.activation(hq[:, bass.ds(b * NT, NT), D:ROW],
                                       bank[6][:, :].rearrange("p (i d) -> p i d", d=D), ACT.Copy).then_inc(s_hqq, 1)
                act.wait_ge(s_e0, 1)
                act.activation(tw[2][:, :, :], tw[2][:, :, :], ACT.Exp).then_inc(s_e1, 1)

            @block.tensor
            def _(pe):
                pe.wait_ge(s_w, 16 * NW)
                pe.wait_ge(s_silu, 1)
                for j in range(6):
                    mm = pe.matmul(bank[7][:, j * NB:(j + 1) * NB], wmod_s[:, j * P:(j + 1) * P], cT_s[:, :],
                                   start=True, stop=True)
                mm.then_inc(s_mod, 1)
                pe.wait_ge(s_bd, 1)
                pe.wait_ge(s_mods, 1)
                mm = pe.matmul(bank[7][:, 256:512], q_raw[:, :], fm[:, 0:2, :].rearrange("p f c -> p (f c)"),
                               start=True, stop=True)
                mm.then_inc(s_fold, 1)
                for e in range(E):
                    if e >= 4:
                        pe.wait_ge(s_wcopy, 2 + e - 3)
                    pe.matmul(bank[e % 4][:, 0:2 * P], kw_raw[:, e, :], fm[:, 2:4, :].rearrange("p f c -> p (f c)"),
                              start=True, stop=True).then_inc(s_fold, 1)
                pe.wait_ge(s_wcopy, 2 + E)
                pe.wait_ge(s_mask, MASKS)
                with pe.Fori(0, NB // 2) as bb:
                    for u in range(2):
                        b = 2 * bb + u
                        pe.wait_ge(s_xh, b + 1)
                        for i in range(NT):
                            mm = pe.transpose(bank[u][:, i * P:(i + 1) * P], xh[:, u, i, :], ident[:, :])
                        mm.then_inc(s_xT, 1)
                        pe.wait_ge(s_hT, b + 1)
                        pe.wait_ge(s_qf, b)
                        pe.matmul(bank[2][:, :], q1T[:, :], hT[:, u, :], start=True, stop=True)
                        pe.matmul(bank[3][:, :], q2T[:, :], hT[:, u, :], start=True, stop=True).then_inc(s_qp, 1)
                        pe.wait_ge(s_lg, b)
                        pe.wait_ge(s_hqh, b)
                        for i in range(NT):
                            pe.matmul(bank[4][:, i * E:(i + 1) * E], hT[:, u, i * P:(i + 1) * P], gA[:, :],
                                      start=True, stop=True)
                        for i in range(NT):
                            mm = pe.transpose(bank[5][:, i * P:(i + 1) * P], hT[:, u, i * P:(i + 1) * P], ident[:, :])
                        mm.then_inc(s_hb, 1)
                        pe.wait_ge(s_qf, b + 1)
                        pe.wait_ge(s_hqq, b)
                        for i in range(NT):
                            mm = pe.transpose(bank[6][:, i * P:(i + 1) * P], qT[:, u, i * P:(i + 1) * P], ident[:, :])
                        mm.then_inc(s_qb, 1)
                pe.wait_ge(s_selb, 1)
                flat = selb[:, :, :].rearrange("p t e -> p (t e)")
                pe.matmul(bank[0][:, :], tri[:, :], flat, start=True, stop=True)
                pe.matmul(bank[1][:, :], ones[:, :], flat, start=True, stop=True).then_inc(s_cnt, 1)

            @block.vector
            def _(dve):
                count = [0]

                def link(ins):
                    count[0] += 1
                    ins.then_inc(s_ch, 1)
                    dve.wait_ge(s_ch, count[0])

                dve.wait_ge(s_w, 16 * NW)
                dve.wait_ge(s_mask, MASKS)
                for f in range(4):
                    ins = dve.tensor_tensor(fm[:, f, :], fm[:, f, :], headm[:, :], ALU.mult)
                ins.then_inc(s_bd, 1)
                for par in range(2):
                    link(dve.tensor_reduce(parity[:, par:par + 1],
                                           headm[:, :].rearrange("p (h r) -> p h r", r=2 * DK)[:, :, par * DK],
                                           AX.X, ALU.add))
                link(dve.tensor_scalar(oT[:, :], oT[:, :], normc[:, 0:1], None, ALU.mult))
                dve.wait_ge(s_mod, 1)
                link(dve.tensor_copy(mods[:, :, :], bank[7][:, 0:6 * NB].rearrange("p (j b) -> p j b", b=NB)))
                for j in (1, 4):
                    link(dve.tensor_scalar(mods[:, j, :], mods[:, j, :], 1.0, None, ALU.add))
                for j in (2, 5):
                    link(dve.tensor_scalar(sgn[:, :], mods[:, j, :], 0.0, 2.0, ALU.is_ge, ALU.mult))
                    link(dve.tensor_scalar(sgn[:, :], sgn[:, :], -1.0, None, ALU.add))
                    link(dve.tensor_tensor(mods[:, j, :], mods[:, j, :], sgn[:, :], ALU.mult))
                    link(dve.tensor_scalar(mods[:, j, :], mods[:, j, :], 0.25, None, ALU.max))
                    link(dve.tensor_tensor(mods[:, j, :], mods[:, j, :], sgn[:, :], ALU.mult))
                dve.sem_inc(s_mods, 1)
                q = TILES // 4
                base = count[0]
                for n in range(4):
                    dve.wait_ge(s_x[n], 16)
                    with dve.Fori(n * q // NT, (n + 1) * q // NT) as tt:
                        for i in range(NT):
                            dve.bn_stats(stats[:, NT * tt + i, :], x_all[:, NT * tt + i, :]).then_inc(s_ch, 1)
                count[0] = base + TILES
                dve.wait_ge(s_ch, count[0])
                norm_stats(dve, link, ta[0][:, :], ta[2][:, :])
                dve.sem_inc(s_var, 1)
                dve.wait_ge(s_sq, 1)
                newton(dve, link, ta[1][:, :], ta[0][:, :], rstd[:, :], ta[2][:, :])
                with dve.Fori(0, NB // 2) as bb:
                    for u in range(2):
                        b = 2 * bb + u
                        if u == 0:
                            dve.wait_ge(s_xT, 2 * bb)
                        for i in range(NT):
                            t = b * NT + i
                            ins = dve.tensor_scalar(xh[:, u, i, :], x_all[:, t, :], mean[:, bass.ds(t, 1)],
                                                    rstd[:, bass.ds(t, 1)], ALU.subtract, ALU.mult)
                        ins.then_inc(s_xh, 1)
                    for u in range(2):
                        b = 2 * bb + u
                        dve.wait_ge(s_hb, b + 1)
                        dve.tensor_copy(lg[:, bass.ds(b * NT, NT), :],
                                        bank[4][:, 0:NT * E].rearrange("p (i e) -> p i e", e=E)).then_inc(s_lg, 1)
                        dve.wait_ge(s_q1, b + 1)
                        dve.scalar_tensor_tensor(out=qT[:, u, :], in0=bank[3][:, :], scalar=DK ** -0.5,
                                                 in1=q1s[:, u, :], op0=ALU.mult, op1=ALU.mult).then_inc(s_qf, 1)
                dve.wait_ge(s_lg, NB)
                one, two, left, t = (v[:, :, :] for v in (tw[0], tw[1], tw[3], tw[2]))
                m = ta[0][:, :]
                pick(dve, link, lg[:, :, :], one, t, m)
                link(dve.scalar_tensor_tensor(out=left, in0=one, scalar=LOW, in1=lg[:, :, :], op0=ALU.mult, op1=ALU.add))
                pick(dve, link, left, two, t, m)
                link(dve.tensor_reduce(m, lg[:, :, :], AX.X, ALU.max))
                link(dve.tensor_tensor(t, lg[:, :, :], m.unsqueeze(2).to_broadcast([P, TILES, E]), ALU.subtract))
                dve.sem_inc(s_e0, 1)
                link(dve.tensor_tensor(left, one, two, ALU.add))
                link(dve.tensor_copy(selb[:, :, :], left))
                dve.sem_inc(s_selb, 1)
                dve.wait_ge(s_e1, 1)
                link(dve.tensor_tensor(t, t, left, ALU.mult))
                link(dve.tensor_reduce(m, t, AX.X, ALU.add))
                link(dve.reciprocal(ta[1][:, :], m))
                link(dve.tensor_tensor(t, t, ta[1][:, :].unsqueeze(2).to_broadcast([P, TILES, E]), ALU.mult))
                dve.wait_ge(s_cnt, 1)
                cnt = lg[:, :, :]
                cb = lg[:, :, :].rearrange("p (b i) e -> p b i e", i=NT)
                tot = left.rearrange("p (b i) e -> p b i e", i=NT)
                link(dve.tensor_copy(cnt, bank[0][:, :].rearrange("p (t e) -> p t e", e=E)))
                link(dve.tensor_copy(left, bank[1][:, :].rearrange("p (t e) -> p t e", e=E)))
                for i in range(NT - 2, -1, -1):
                    link(dve.tensor_tensor(cb[:, :, i, :], cb[:, :, i, :], tot[:, :, i + 1, :], ALU.add))
                    if i:
                        link(dve.tensor_tensor(tot[:, :, i, :], tot[:, :, i, :], tot[:, :, i + 1, :], ALU.add))
                keep = left
                link(dve.tensor_scalar(keep, cnt, float(CAP), None, ALU.is_le))
                for i in range(NT):
                    link(dve.tensor_tensor(cb[:, :, i, :], erow[:, :, :], cb[:, :, i, :], ALU.subtract))
                for s, oh in enumerate((one, two)):
                    link(dve.tensor_tensor(oh, oh, keep, ALU.mult))
                    kept, row = ta[1][:, :], ta[2][:, :]
                    link(dve.tensor_reduce(kept, oh, AX.X, ALU.add))
                    prod = selp[:, :, :]
                    link(dve.tensor_tensor(prod, oh, t, ALU.mult))
                    link(dve.tensor_reduce(wslot[:, :, s], prod, AX.X, ALU.add))
                    link(dve.tensor_tensor(prod, oh, cnt, ALU.mult))
                    link(dve.tensor_reduce(row, prod, AX.X, ALU.add))
                    link(dve.tensor_copy(idxg[:, :, s], row))
                    link(dve.tensor_scalar(kept, kept, -FAR, FAR, ALU.mult, ALU.add))
                    link(dve.tensor_tensor(row, row, kept, ALU.add))
                    link(dve.tensor_copy(idxs[:, :, s], row))

        ph.close()

        ph = ExitStack()

        def tb(name, shape, dt=F32):
            return ph.enter_context(nc.sbuf_tensor(name, shape, dt))

        RING = 4
        srow = tb("srow", [P, NT, ROW])
        sidx = tb("sidx", [P, NT * TOPA], U32)
        rows = tb("rows", [P, RING, 2, ROW])
        turned = tb("turned", [P, 2, 2, 2 * P])
        qx = tb("qx", [P, 2, 2 * P])
        k1s = tb("k1s", [P, 2 * P])
        kT = tb("kT", [P, 2 * P])
        vk = tb("vk", [P, 2, 4, P])
        att = tb("att", [P, 4, 2, 2, C])
        st = tb("st", [P, 3, P])
        ob = tb("ob", [P, 2, 2, P])

        s_scat = sem("rows_scattered")
        s_ld = [sem(f"rows_loaded{i}") for i in range(RING)]
        s_t = sem("rows_turned")
        s_te = sem("turned_copied")
        s_qx = sem("q_split")
        s_k = sem("k_products")
        s_ke = sem("k1_copied")
        s_kf = sem("k_features")
        s_vk = sem("v_and_k_ready")
        s_vke = sem("v_and_k_copied")
        s_s = sem("scores_ready")
        s_a = sem("scores_masked")
        s_st = sem("states_ready")
        s_ste = sem("states_masked")
        s_o = sem("attended")
        s_oe = sem("attended_copied")
        s_os = [sem("attended_stored0"), sem("attended_stored1")]

        with nc.Block() as block:
            @block.gpsimd
            def _(pool):
                with pool.Fori(0, NB) as b:
                    pool.wait_ge(s_scat, 16 * NT * TOPA * b)
                    pool.tensor_copy(srow[:, :, :], hq[:, bass.ds(b * NT, NT), :])
                    pool.tensor_copy(sidx[:, :], idxs[:, bass.ds(b * NT, NT), :]
                                     .rearrange("p i s -> p (i s)"))
                    pool.drain()
                    for i in range(NT):
                        for s in range(TOPA):
                            k = i * TOPA + s
                            pool.indirect_dma_start(hs, bass.IndirectOffsetOnAxis(sidx[:, k:k + 1], 0),
                                                    srow[:, i, :], None, bounds_check=G * CAP - 1,
                                                    oob_is_err=False).then_inc(s_scat, 16)
                pool.wait_ge(s_scat, 16 * NT * TOPA * NB)

            @block.sync
            def _(sp):
                hv = hs.rearrange("(g a p) w -> g p a w", a=2, p=P)
                ov = osd.rearrange("(g a p) d -> g p a d", a=2, p=P)

                def load(g, slot):
                    sp.dma_start(rows[:, slot, :, :], hv[g]).then_inc(s_ld[slot], 16)

                def batch(b, last):
                    for e in range(E):
                        g = b * E + e
                        if not last or e < E - RING:
                            sp.wait_ge(s_t, g + 1)
                            if e == E - RING:
                                sp.wait_ge(s_scat, 16 * NT * TOPA * (b + 2))
                            load(g + RING, e % RING)
                        sp.wait_ge(s_oe, g + 1)
                        sp.dma_start(ov[g], ob[:, e % 2, :, :]).then_inc(s_os[e % 2], 16)

                sp.wait_ge(s_scat, 16 * NT * TOPA)
                for e in range(RING):
                    load(e, e)
                with sp.Fori(0, NB - 1) as b:
                    batch(b, False)
                batch(NB - 1, True)
                for i in range(2):
                    sp.wait_ge(s_os[i], 16 * G // 2)

            @block.scalar
            def _(act):
                def turn(n, e):
                    act.wait_ge(s_t, n + 1)
                    act.activation(turned[:, e % 2, :, :].rearrange("p a c -> p (a c)"), bank[4][:, :],
                                   ACT.Copy).then_inc(s_te, 1)

                def first_k(n):
                    act.wait_ge(s_k, n + 1)
                    act.wait_ge(s_kf, n)
                    act.activation(k1s[:, :], bank[5][:, 0:2 * P], ACT.Copy).then_inc(s_ke, 1)

                def keep_vk(n, e):
                    act.wait_ge(s_vk, n + 1)
                    act.activation(vk[:, e % 2, :, :].rearrange("p a c -> p (a c)"), bank[6][:, :],
                                   ACT.Copy).then_inc(s_vke, 1)

                def outputs(g, b, e):
                    act.wait_ge(s_o, g + 1)
                    act.wait_ge(s_os[e % 2], 16 * (b * (E // 2) + e // 2))
                    for c in range(2):
                        ins = act.activation(ob[c * C:(c + 1) * C, e % 2, :, :].rearrange("p a c -> p (a c)"),
                                             bank[4 + c][c * C:(c + 1) * C, 0:2 * P], ACT.Copy)
                    ins.then_inc(s_oe, 1)

                def batch(b, last):
                    for e in range(E):
                        g = b * E + e
                        if not last or e < E - 1:
                            turn(g + 1, e + 1)
                            first_k(g + 1)
                            keep_vk(g + 1, e + 1)
                        outputs(g, b, e)

                turn(0, 0)
                first_k(0)
                keep_vk(0, 0)
                with act.Fori(0, NB - 1) as b:
                    batch(b, False)
                batch(NB - 1, True)

            @block.tensor
            def _(pe):
                def turn(n, e, b, en):
                    pe.wait_ge(s_ld[e % RING], 16 * (b * (E // RING) + en // RING + 1))
                    for part in range(2):
                        for a in range(2):
                            mm = pe.transpose(bank[4][:, part * 2 * P + a * P:part * 2 * P + (a + 1) * P],
                                              rows[:, e % RING, a, part * D:(part + 1) * D], ident[:, :])
                    mm.then_inc(s_t, 1)

                def keys(n, e):
                    e = e % E
                    pe.wait_ge(s_te, n + 1)
                    hT2 = turned[:, e % 2, 0, :]
                    pe.matmul(bank[5][:, 0:2 * P], k1T[:, e, :], hT2, start=True, stop=True)
                    pe.matmul(bank[5][:, 2 * P:4 * P], k2T[:, e, :], hT2, start=True, stop=True).then_inc(s_k, 1)

                def values(n, e):
                    e = e % E
                    pe.wait_ge(s_vke, n)
                    for a in range(2):
                        pe.matmul(bank[6][:, a * P:(a + 1) * P], turned[:, e % 2, 0, a * P:(a + 1) * P],
                                  vT[:, e, :], start=True, stop=True)

                def turn_k(n):
                    pe.wait_ge(s_kf, n + 1)
                    for a in range(2):
                        mm = pe.transpose(bank[6][:, (2 + a) * P:(3 + a) * P], kT[:, a * P:(a + 1) * P], ident[:, :])
                    mm.then_inc(s_vk, 1)

                def scores(g, e):
                    pe.wait_ge(s_qx, g + 1)
                    pe.wait_ge(s_kf, g + 1)
                    pe.wait_ge(s_a, g)
                    for a in range(2):
                        for c in range(2):
                            t0 = a * P + c * C
                            for p in range(4):
                                r = slice(32 * p, 32 * p + 32)
                                mm = pe.matmul(bank[p][c * C:(c + 1) * C, a * 2 * C:(a + 1) * 2 * C],
                                               kT[r, t0:t0 + C], qx[r, :, t0:t0 + C], start=True, stop=True)
                    mm.then_inc(s_s, 1)

                def states(g, e):
                    pe.wait_ge(s_vke, g + 1)
                    pe.wait_ge(s_ste, g)
                    v, k = vk[:, e % 2, 0:2, :], vk[:, e % 2, 2:4, :]
                    pe.matmul(bank[7][:, 0:P], k[0:C, 0, :], v[0:C, 0, :], start=True, stop=True)
                    pe.matmul(bank[7][:, P:2 * P], k[:, 0, :], v[:, 0, :], start=True, stop=True)
                    pe.matmul(bank[7][:, 2 * P:3 * P], k[:, 0, :], v[:, 0, :], start=True, stop=False)
                    pe.matmul(bank[7][:, 2 * P:3 * P], k[0:C, 1, :], v[0:C, 1, :], start=False,
                              stop=True).then_inc(s_st, 1)

                def attend(g, e, last):
                    pe.wait_ge(s_a, g + 1)
                    pe.wait_ge(s_ste, g + 1)
                    if not last:
                        pe.wait_ge(s_te, g + 2)
                        pe.wait_ge(s_kf, g + 2)
                    v, qT2 = vk[:, e % 2, 0:2, :], turned[:, e % 2, 1, :]
                    for c in (1, 0):
                        r = slice(c * C, (c + 1) * C)
                        for a in range(2):
                            n = 2 * a + c
                            if n:
                                pe.matmul(bank[4 + c][r, a * P:(a + 1) * P], qT2[:, n * C:(n + 1) * C],
                                          st[:, n - 1, :], start=True, stop=True, skip_group_check=True)
                            for h in range(H):
                                mm = pe.matmul(bank[4 + c][r, a * P + h * DK:a * P + (h + 1) * DK],
                                               att[r, h // 2, a, h % 2, :], v[r, a, h * DK:(h + 1) * DK],
                                               start=(n == 0), stop=True, skip_group_check=True)
                    mm.then_inc(s_o, 1)

                def batch(b, last):
                    for e in range(E):
                        g = b * E + e
                        scores(g, e)
                        end = last and e == E - 1
                        pe.wait_ge(s_oe, g)
                        if not end:
                            turn(g + 1, (e + 1) % E, b, e + 1)
                            keys(g + 1, e + 1)
                            values(g + 1, e + 1)
                        states(g, e)
                        if not end:
                            turn_k(g + 1)
                        attend(g, e, end)

                turn(0, 0, 0, 0)
                keys(0, 0)
                values(0, 0)
                turn_k(0)
                with pe.Fori(0, NB - 1) as b:
                    batch(b, False)
                batch(NB - 1, True)

            @block.vector
            def _(dve):
                def split_q(n, e):
                    dve.wait_ge(s_te, n + 1)
                    for par in range(2):
                        ins = dve.tensor_scalar(qx[:, par, :], turned[:, e % 2, 1, :], parity[:, par:par + 1], None,
                                                ALU.mult)
                    ins.then_inc(s_qx, 1)

                def k_features(n):
                    dve.wait_ge(s_ke, n + 1)
                    dve.tensor_tensor(kT[:, :], bank[5][:, 2 * P:4 * P], k1s[:, :], ALU.mult).then_inc(s_kf, 1)

                def mask_scores(g):
                    dve.wait_ge(s_s, g + 1)
                    for p in range(4):
                        ins = dve.tensor_tensor(att[:, p, :, :, :].rearrange("p a h t -> p (a h) t"),
                                                bank[p][:, 0:4 * C].rearrange("p (x t) -> p x t", t=C),
                                                causal[:, :].unsqueeze(1).to_broadcast([P, 4, C]), ALU.mult)
                    ins.then_inc(s_a, 1)

                def mask_states(g):
                    dve.wait_ge(s_st, g + 1)
                    dve.tensor_tensor(st[:, :, :], bank[7][:, 0:3 * P].rearrange("p (n d) -> p n d", d=P),
                                      headm[:, :].unsqueeze(1).to_broadcast([P, 3, P]), ALU.mult).then_inc(s_ste, 1)

                def batch(b, last):
                    for e in range(E):
                        g = b * E + e
                        mask_scores(g)
                        if not last or e < E - 1:
                            split_q(g + 1, e + 1)
                            k_features(g + 1)
                        mask_states(g)

                split_q(0, 0)
                k_features(0)
                with dve.Fori(0, NB - 1) as b:
                    batch(b, False)
                batch(NB - 1, True)
        ph.close()

        ph = ExitStack()
        gst = tb("gst", [P, 2, NT * TOPA, D])
        gidx = tb("gidx", [P, 2, NT * TOPA], U32)
        sqs = tb("sqs", [P, NT, D])
        ss = tb("ss", [P, NB * NT * H])
        dev = tb("dev", [P, NB * NT * H])
        rr = tb("rr", [P, NB * NT * H])
        tt = tb("tt", [P, NB * NT * H])
        on = tb("on", [P, 2, NT, D])
        onT = tb("onT", [P, 2, S])
        aT = tb("aT", [P, 2, S])

        s_g = [sem("rows_gathered0"), sem("rows_gathered1")]
        s_gm = sem("gathered_weighed")
        s_c1 = sem("combine_chain")
        s_v1 = sem("head_variance")
        s_v2 = sem("head_deviation")
        s_on = sem("heads_normalised")
        s_onT = sem("heads_turned")
        s_onc = sem("heads_copied")
        s_y = sem("projected")
        s_yc = sem("gated")
        s_yT = sem("gated_turned")
        s_x2 = sem("residual_added")
        s_v3 = sem("norm_variance")
        s_v4 = sem("norm_deviation")
        o_all = hq[:, :, 0:D]

        with nc.Block() as block:
            @block.gpsimd
            def _(pool):
                with pool.Fori(0, NB // 2) as bb:
                    for u in range(2):
                        b = 2 * bb + u
                        if u == 0:
                            pool.wait_ge(s_gm, 2 * bb)
                        pool.tensor_copy(gidx[:, u, :], idxg[:, bass.ds(b * NT, NT), :]
                                         .rearrange("p i s -> p (i s)"))
                        pool.drain()
                        for k in range(NT * TOPA):
                            pool.indirect_dma_start(gst[:, u, k, :], None, osd,
                                                    bass.IndirectOffsetOnAxis(gidx[:, u, k:k + 1], 0),
                                                    bounds_check=G * CAP - 1, oob_is_err=False).then_inc(s_g[u], 16)

            @block.scalar
            def _(act):
                act.wait_ge(s_v1, 1)
                act.activation(dev[:, :], ss[:, :], ACT.Sqrt).then_inc(s_v2, 1)
                with act.Fori(0, NB // 2) as bb:
                    for u in range(2):
                        b = 2 * bb + u
                        act.wait_ge(s_onT, b + 1)
                        act.activation(onT[:, u, :], bank[u][:, :], ACT.Copy).then_inc(s_onc, 1)
                        act.wait_ge(s_y, b + 1)
                        act.activation(aT[:, u, :], bank[2 + u][:, :], ACT.Copy,
                                       scale=mods[:, 2, bass.ds(b, 1)]).then_inc(s_yc, 1)
                act.wait_ge(s_v3, 1)
                act.activation(dev[:, 0:TILES], ss[:, 0:TILES], ACT.Sqrt).then_inc(s_v4, 1)

            @block.tensor
            def _(pe):
                with pe.Fori(0, NB // 2) as bb:
                    for u in range(2):
                        b = 2 * bb + u
                        pe.wait_ge(s_on, b + 1)
                        for i in range(NT):
                            mm = pe.transpose(bank[u][:, i * P:(i + 1) * P], on[:, u, i, :], ident[:, :])
                        mm.then_inc(s_onT, 1)
                        pe.wait_ge(s_onc, b + 1)
                        pe.matmul(bank[2 + u][:, :], oT[:, :], onT[:, u, :], start=True, stop=True).then_inc(s_y, 1)
                        pe.wait_ge(s_yc, b + 1)
                        if u == 0:
                            pe.wait_ge(s_x2, 2 * bb)
                        for i in range(NT):
                            mm = pe.transpose(bank[4 + u][:, i * P:(i + 1) * P], aT[:, u, i * P:(i + 1) * P],
                                              ident[:, :])
                        mm.then_inc(s_yT, 1)

            @block.vector
            def _(dve):
                count = [0]

                def link(ins):
                    count[0] += 1
                    ins.then_inc(s_c1, 1)
                    dve.wait_ge(s_c1, count[0])

                with dve.Fori(0, NB // 2) as bb:
                    for u in range(2):
                        b = 2 * bb + u
                        dve.wait_ge(s_g[u], 16 * NT * TOPA * (bb + 1))
                        w = wslot[:, bass.ds(b * NT, NT), :].rearrange("p i s -> p (i s)").unsqueeze(2)
                        dve.tensor_tensor(gst[:, u, :, :], gst[:, u, :, :], w.to_broadcast([P, NT * TOPA, D]),
                                          ALU.mult).then_inc(s_c1, 1)
                        dve.wait_ge(s_c1, 4 * b + 1)
                        gv = gst[:, u, :, :].rearrange("p (i s) d -> p i s d", s=TOPA)
                        o = o_all[:, bass.ds(b * NT, NT), :]
                        dve.tensor_tensor(o, gv[:, :, 0, :], gv[:, :, 1, :], ALU.add).then_inc(s_c1, 1)
                        dve.wait_ge(s_c1, 4 * b + 2)
                        dve.tensor_tensor(sqs[:, :, :], o, o, ALU.mult).then_inc(s_c1, 1)
                        dve.wait_ge(s_c1, 4 * b + 3)
                        dve.tensor_reduce(ss[:, bass.ds(b * NT * H, NT * H)],
                                          sqs[:, :, :].rearrange("p i (h d) -> p (i h) d", d=DK), AX.X,
                                          ALU.add).then_inc(s_c1, 1)
                        dve.wait_ge(s_c1, 4 * b + 4)
                        dve.sem_inc(s_gm, 1)
                count[0] = 4 * NB
                link(dve.tensor_scalar(ss[:, :], ss[:, :], 1.0 / DK, EPS, ALU.mult, ALU.add))
                dve.sem_inc(s_v1, 1)
                dve.wait_ge(s_v2, 1)
                newton(dve, link, dev[:, :], ss[:, :], rr[:, :], tt[:, :])

                def normalise(b, u):
                    o = o_all[:, bass.ds(b * NT, NT), :].rearrange("p i (h d) -> p i h d", d=DK)
                    r = rr[:, bass.ds(b * NT * H, NT * H)].rearrange("p (i h) -> p i h", h=H)
                    dve.tensor_tensor(on[:, u, :, :].rearrange("p i (h d) -> p i h d", d=DK), o,
                                      r.unsqueeze(3).to_broadcast([P, NT, H, DK]), ALU.mult).then_inc(s_on, 1)

                base = count[0]
                with dve.Fori(0, NB // 2) as bb:
                    dve.wait_ge(s_onT, 2 * bb)
                    for u in range(2):
                        normalise(2 * bb + u, u)
                    for u in range(2):
                        b = 2 * bb + u
                        dve.wait_ge(s_yT, b + 1)
                        xb = x_all[:, bass.ds(b * NT, NT), :]
                        dve.tensor_tensor(xb, bank[4 + u][:, :].rearrange("p (i d) -> p i d", d=D), xb,
                                          ALU.add).then_inc(s_x2, 1)
                        dve.wait_ge(s_x2, b + 1)
                        for i in range(NT):
                            dve.bn_stats(stats[:, NT * b + i, :], x_all[:, NT * b + i, :]).then_inc(s_c1, 1)
                count[0] = base + TILES
                dve.wait_ge(s_c1, count[0])
                norm_stats(dve, link, ss[:, 0:TILES], tt[:, 0:TILES])
                dve.sem_inc(s_v3, 1)
                dve.wait_ge(s_v4, 1)
                newton(dve, link, dev[:, 0:TILES], ss[:, 0:TILES], rstd[:, :], tt[:, 0:TILES])
        ph.close()

        ph = ExitStack()
        fxh = tb("fxh", [P, 2, NT, D])
        fhT = tb("fhT", [P, 2, S])
        l0 = tb("l0", [P, 2, S])
        sg = tb("sg", [P, 2, S])
        h2 = tb("h2", [P, 2, S])
        fw = [tb(f"fw{i}", [P, TILES, E]) for i in range(4)]
        fa = [tb(f"fa{i}", [P, TILES]) for i in range(2)]
        h_all = hq[:, :, D:ROW]

        s_fx = sem("ff_normalised")
        s_fT = sem("ff_turned")
        s_fh = sem("ff_modulated")
        s_l0 = sem("ff_linear")
        s_l0c = sem("ff_linear_copied")
        s_sw = sem("ff_glu_products")
        s_sg = sem("ff_glu_gate")
        s_h2 = sem("ff_hidden")
        s_rl = sem("router_products")
        s_rlc = sem("router_copied")
        s_hk = sem("ff_hidden_kept")
        s_c2 = sem("router_chain")
        s_x0 = sem("router_exponent_in")
        s_x1 = sem("router_exponent_out")

        with nc.Block() as block:
            @block.scalar
            def _(act):
                with act.Fori(0, NB // 2) as bb:
                    for u in range(2):
                        b = 2 * bb + u
                        act.wait_ge(s_fT, b + 1)
                        act.activation(fhT[:, u, :], bank[u][:, :], ACT.Identity, bias=mods[:, 3, bass.ds(b, 1)],
                                       scale=mods[:, 4, bass.ds(b, 1)]).then_inc(s_fh, 1)
                        act.wait_ge(s_l0, b + 1)
                        act.activation(l0[:, u, :], bank[2][:, :], ACT.Identity,
                                       bias=bias[:, 0:1]).then_inc(s_l0c, 1)
                        act.wait_ge(s_sw, 2 * b + 1)
                        act.activation(sg[:, u, :], bank[3][:, :], ACT.Silu, bias=bias[:, 1:2]).then_inc(s_sg, 1)
                act.wait_ge(s_x0, 1)
                act.activation(fw[2][:, :, :], fw[2][:, :, :], ACT.Exp).then_inc(s_x1, 1)

            @block.gpsimd
            def _(pool):
                with pool.Fori(0, NB // 2) as bb:
                    for u in range(2):
                        b = 2 * bb + u
                        pool.wait_ge(s_h2, b + 1)
                        pool.tensor_copy(h_all[:, bass.ds(b * NT, NT), :],
                                         h2[:, u, :].rearrange("p (i d) -> p i d", d=D)).then_inc(s_hk, 1)

            @block.tensor
            def _(pe):
                with pe.Fori(0, NB // 2) as bb:
                    for u in range(2):
                        b = 2 * bb + u
                        pe.wait_ge(s_fx, b + 1)
                        for i in range(NT):
                            mm = pe.transpose(bank[u][:, i * P:(i + 1) * P], fxh[:, u, i, :], ident[:, :])
                        mm.then_inc(s_fT, 1)
                        pe.wait_ge(s_fh, b + 1)
                        pe.matmul(bank[2][:, :], mat[:, 0, :], fhT[:, u, :], start=True, stop=True).then_inc(s_l0, 1)
                        pe.wait_ge(s_l0c, b + 1)
                        pe.matmul(bank[3][:, :], mat[:, 1, :], l0[:, u, :], start=True, stop=True).then_inc(s_sw, 1)
                        pe.wait_ge(s_h2, b)
                        pe.matmul(bank[4][:, :], mat[:, 2, :], l0[:, u, :], start=True, stop=True).then_inc(s_sw, 1)
                        pe.wait_ge(s_h2, b + 1)
                        pe.wait_ge(s_rlc, b)
                        for i in range(NT):
                            mm = pe.matmul(bank[5][:, i * E:(i + 1) * E], h2[:, u, i * P:(i + 1) * P], gF[:, :],
                                           start=True, stop=True)
                        mm.then_inc(s_rl, 1)

            @block.vector
            def _(dve):
                count = [0]

                def link(ins):
                    count[0] += 1
                    ins.then_inc(s_c2, 1)
                    dve.wait_ge(s_c2, count[0])

                with dve.Fori(0, NB // 2) as bb:
                    dve.wait_ge(s_fT, 2 * bb)
                    for u in range(2):
                        for i in range(NT):
                            t = (2 * bb + u) * NT + i
                            ins = dve.tensor_scalar(fxh[:, u, i, :], x_all[:, t, :], mean[:, bass.ds(t, 1)],
                                                    rstd[:, bass.ds(t, 1)], ALU.subtract, ALU.mult)
                        ins.then_inc(s_fx, 1)
                    for u in range(2):
                        b = 2 * bb + u
                        dve.wait_ge(s_sg, b + 1)
                        dve.wait_ge(s_sw, 2 * b + 2)
                        if u == 0:
                            dve.wait_ge(s_hk, 2 * bb)
                        dve.scalar_tensor_tensor(out=h2[:, u, :], in0=bank[4][:, :], scalar=bias[:, 2:3],
                                                 in1=sg[:, u, :], op0=ALU.add, op1=ALU.mult).then_inc(s_h2, 1)
                        dve.wait_ge(s_rl, b + 1)
                        dve.tensor_copy(lg[:, bass.ds(b * NT, NT), :],
                                        bank[5][:, 0:NT * E].rearrange("p (i e) -> p i e", e=E)).then_inc(s_rlc, 1)
                dve.wait_ge(s_rlc, NB)
                left, one, t, w = (v[:, :, :] for v in fw)
                m = fa[0][:, :]
                for k in range(TOPF):
                    src = lg[:, :, :] if k == 0 else left
                    pick(dve, link, src, one, t, m)
                    link(dve.scalar_tensor_tensor(out=left, in0=one, scalar=LOW, in1=src, op0=ALU.mult, op1=ALU.add))
                    if k == 0:
                        link(dve.tensor_copy(w, one))
                    else:
                        link(dve.tensor_tensor(w, w, one, ALU.add))
                link(dve.tensor_reduce(m, lg[:, :, :], AX.X, ALU.max))
                link(dve.tensor_tensor(t, lg[:, :, :], m.unsqueeze(2).to_broadcast([P, TILES, E]), ALU.subtract))
                dve.sem_inc(s_x0, 1)
                dve.wait_ge(s_x1, 1)
                link(dve.tensor_tensor(w, w, t, ALU.mult))
                link(dve.tensor_reduce(m, w, AX.X, ALU.add))
                link(dve.reciprocal(fa[1][:, :], m))
                link(dve.tensor_tensor(w, w, fa[1][:, :].unsqueeze(2).to_broadcast([P, TILES, E]), ALU.mult))
                for part in range(3):
                    piece = w24[:, :, part * E:(part + 1) * E]
                    link(dve.tensor_copy(piece, w))
                    if part < 2:
                        link(dve.tensor_tensor(w, w, piece, ALU.subtract))
        ph.close()

        ph = ExitStack()
        wst = tb("wst", [P, 2, NT, 3 * E], BF16)
        wTs = tb("wTs", [3 * E, 2, S], BF16)
        eg = tb("eg", [P, 2, S])
        ep = tb("ep", [P, 2, S])
        ys = tb("ys", [P, S])
        l1 = tb("l1", [P, S])
        tg = tb("tg", [P, S])
        t2 = tb("t2", [P, S])
        t3 = tb("t3", [P, S])
        fin = tb("fin", [P, 2, NT, D])
        TAIL = (2, 4, 6, 8)
        NU = E + SH

        s_ws = sem("weights_staged")
        s_wt = sem("weights_turned")
        s_wtc = sem("weights_copied")
        s_eg = sem("expert_products")
        s_es = sem("expert_gate")
        s_eu = sem("expert_gated")
        s_ep = sem("expert_hidden")
        s_ey = sem("expert_sum_parts")
        s_yk = sem("expert_sum_copied")
        s_t1 = sem("tail_linear")
        s_t1c = sem("tail_linear_copied")
        s_t2 = sem("tail_gate_product")
        s_t2c = sem("tail_gate")
        s_t3 = sem("tail_up_product")
        s_t3c = sem("tail_hidden")
        s_t4 = sem("tail_scaled")
        s_t5 = sem("tail_turned")
        s_fin = sem("result_ready")
        s_out = [sem("result_stored0"), sem("result_stored1")]

        w_ps = bank[7][0:3 * E, 0:S // 2].bitcast(BF16)

        with nc.Block() as block:
            def pairs(eng, batch):
                for u in range(2):
                    batch(u, u, u == 0)
                with eng.Fori(1, NB // 2) as bb:
                    for u in range(2):
                        batch(2 * bb + u, u, False)

            @block.gpsimd
            def _(pool):
                def batch(b, u, first):
                    if u == 0:
                        pool.wait_ge(s_wt, b)
                    pool.tensor_copy(wst[:, u, :, :], w24[:, bass.ds(b * NT, NT), :]).then_inc(s_ws, 1)

                pairs(pool, batch)

            @block.sync
            def _(sp):
                ov = out.rearrange("b (i p) d -> b p i d", p=P)

                def batch(b, u):
                    sp.wait_ge(s_fin, b + 1)
                    sp.dma_start(ov[b], fin[:, u, :, :]).then_inc(s_out[u], 16)

                with sp.Fori(0, NB // 2) as bb:
                    for u in range(2):
                        batch(2 * bb + u, u)
                for u in range(2):
                    sp.wait_ge(s_out[u], 16 * (NB // 2))

            @block.tensor
            def _(pe):
                def turn_weights(b, u, first):
                    pe.wait_ge(s_ws, b + 1)
                    if not first or u:
                        pe.wait_ge(s_fin, b - 1)
                        pe.wait_ge(s_wtc, b)
                    for i in range(NT):
                        mm = pe.transpose(w_ps[:, i * P:(i + 1) * P], wst[:, u, i, :], identb[:, :])
                    mm.then_inc(s_wt, 1)

                def up(b, u, n, free):
                    k = NU * b + n
                    r = h_all[:, bass.ds(b * NT, NT), :]
                    if free:
                        pe.wait_ge(s_ep, k - 1)
                    pe.matmul(bank[1 + n % 2][:, :], w1s[:, n, :], r, start=True, stop=True)
                    mm = pe.matmul(bank[3 + n % 2][:, :], w3s[:, n, :], r, start=True, stop=True)
                    if n < E:
                        pe.wait_ge(s_wtc, b + 1)
                        mm = pe.matmul(bank[5 + n % 2][:, :], sel24[:, n, :], wTs[:, u, :], start=True, stop=True)
                    mm.then_inc(s_eg, 1)

                def down(b, n):
                    pe.wait_ge(s_ep, NU * b + n + 1)
                    pe.matmul(bank[0][:, :], w2s[:, n, :], ep[:, n % 2, :], start=(n == 0),
                              stop=(n == NU - 1)).then_inc(s_ey, 1)

                def tail(b, step):
                    if step == 0:
                        pe.wait_ge(s_yk, b + 1)
                        pe.matmul(bank[7][:, :], mat[:, 3, :], ys[:, :], start=True, stop=True).then_inc(s_t1, 1)
                    elif step == 1:
                        pe.wait_ge(s_t1c, b + 1)
                        pe.matmul(bank[7][:, :], mat[:, 4, :], l1[:, :], start=True, stop=True).then_inc(s_t2, 1)
                    elif step == 2:
                        pe.wait_ge(s_t2c, b + 1)
                        pe.matmul(bank[7][:, :], mat[:, 5, :], l1[:, :], start=True, stop=True).then_inc(s_t3, 1)
                    else:
                        pe.wait_ge(s_t4, b + 1)
                        for i in range(NT):
                            mm = pe.transpose(bank[7][:, i * P:(i + 1) * P], t3[:, i * P:(i + 1) * P], ident[:, :])
                        mm.then_inc(s_t5, 1)

                def batch(b, u, first):
                    turn_weights(b, u, first)
                    for n in range(NU):
                        up(b, u, n, not first or n >= 2)
                        if n:
                            if n == 1 and not first:
                                pe.wait_ge(s_yk, b)
                            down(b, n - 1)
                        elif not first:
                            down(b - 1, NU - 1)
                        if n in TAIL and not first:
                            tail(b - 1, TAIL.index(n))

                pairs(pe, batch)
                down(NB - 1, NU - 1)
                for step in range(4):
                    tail(NB - 1, step)

            @block.scalar
            def _(act):
                def gate(b, n):
                    act.wait_ge(s_eg, NU * b + n + 1)
                    act.activation(eg[:, n % 2, :], bank[1 + n % 2][:, :], ACT.Silu).then_inc(s_es, 1)

                def tail(b, step):
                    if step == 0:
                        act.wait_ge(s_t1, b + 1)
                        act.activation(l1[:, :], bank[7][:, :], ACT.Identity, bias=bias[:, 3:4]).then_inc(s_t1c, 1)
                    elif step == 1:
                        act.wait_ge(s_t2, b + 1)
                        act.activation(tg[:, :], bank[7][:, :], ACT.Silu, bias=bias[:, 4:5]).then_inc(s_t2c, 1)
                    elif step == 2:
                        act.wait_ge(s_t3c, b + 1)
                        act.activation(t3[:, :], t2[:, :], ACT.Copy, scale=mods[:, 5, bass.ds(b, 1)]).then_inc(s_t4, 1)

                def keep_sum(b):
                    act.wait_ge(s_ey, NU * b + NU)
                    act.activation(ys[:, :], bank[0][:, :], ACT.Copy).then_inc(s_yk, 1)

                def batch(b, u, first):
                    act.wait_ge(s_wt, b + 1)
                    act.activation(wTs[:, u, :], w_ps, ACT.Copy).then_inc(s_wtc, 1)
                    for n in range(NU):
                        gate(b, n)
                        if not first:
                            if n == 0:
                                keep_sum(b - 1)
                            if n == TAIL[0]:
                                tail(b - 1, 0)
                            if n == TAIL[1]:
                                tail(b - 1, 1)
                            if n == TAIL[2] + 1:
                                tail(b - 1, 2)

                pairs(act, batch)
                keep_sum(NB - 1)
                for step in range(3):
                    tail(NB - 1, step)

            @block.vector
            def _(dve):
                def hidden(b, n, free):
                    k = NU * b + n
                    dve.wait_ge(s_es, k + 1)
                    if n < E:
                        g = eg[:, n % 2, :]
                        dve.tensor_tensor(g, bank[3 + n % 2][:, :], g, ALU.mult).then_inc(s_eu, 1)
                        dve.wait_ge(s_eu, E * b + n + 1)
                        if free:
                            dve.wait_ge(s_ey, k - 1)
                        dve.tensor_tensor(ep[:, n % 2, :], bank[5 + n % 2][:, :], g, ALU.mult).then_inc(s_ep, 1)
                    else:
                        dve.wait_ge(s_ey, k - 1)
                        dve.tensor_tensor(ep[:, n % 2, :], bank[3 + n % 2][:, :], eg[:, n % 2, :],
                                          ALU.mult).then_inc(s_ep, 1)

                def tail(b, u, step):
                    if step == 2:
                        dve.wait_ge(s_t3, b + 1)
                        dve.scalar_tensor_tensor(out=t2[:, :], in0=bank[7][:, :], scalar=bias[:, 5:6], in1=tg[:, :],
                                                 op0=ALU.add, op1=ALU.mult).then_inc(s_t3c, 1)
                    else:
                        dve.wait_ge(s_t5, b + 1)
                        dve.wait_ge(s_out[u], stored(b, u))
                        dve.tensor_tensor(fin[:, u, :, :], bank[7][:, :].rearrange("p (i d) -> p i d", d=D),
                                          x_all[:, bass.ds(b * NT, NT), :], ALU.add).then_inc(s_fin, 1)

                def stored(b, u):
                    return 8 * (b - u)

                def batch(b, u, first):
                    for n in range(NU):
                        hidden(b, n, not first or n >= 2)
                        if not first and n == TAIL[2]:
                            tail(b - 1, 1 - u, 2)
                        if not first and n == TAIL[3]:
                            tail(b - 1, 1 - u, 3)

                pairs(dve, batch)
                tail(NB - 1, 1, 2)
                tail(NB - 1, 1, 3)
        ph.close()


def kernel(**inputs):
    import numpy as np
    import concourse.bacc as bacc
    from concourse.bass_utils import run_bass_kernel_spmd as run

    a = {k.removeprefix("L0_"): np.asarray(v) for k, v in inputs.items()}
    t = lambda m: np.ascontiguousarray(np.swapaxes(m, -1, -2))
    col = lambda v: np.ascontiguousarray(v.reshape(-1, 1))
    laid = {
        "x": a["attn_x"], "gate_wT": t(a["attn_gate_w"]), "q_w": a["attn_q_w"], "k_w": a["attn_k_w"],
        "v_wT": t(a["attn_v_w"]),
        "fmT": np.stack([np.tile(t(a[f"attn_fm{n}_w"]), (8, 8)) for n in ("q1", "q2", "k1", "k2")]),
        "norm_c": col(np.tile(a["attn_norm_w"], 8)), "o_wT": t(a["attn_o_w"]),
        "lin0": a["ffn_lin0_w"], "lin0_b": col(a["ffn_lin0_b"]), "s1w1": a["ffn_swi1_w1"], "s1b1": col(a["ffn_swi1_b1"]),
        "s1w2": a["ffn_swi1_w2"], "s1b2": col(a["ffn_swi1_b2"]), "fgateT": t(a["ffn_gate_w"]),
        "ew1": a["ffn_exp_w1"], "ew3": a["ffn_exp_w3"], "ew2": a["ffn_exp_w2"],
        "shw1": a["ffn_sh_w1"], "shw3": a["ffn_sh_w3"], "shw2": a["ffn_sh_w2"],
        "lin1": a["ffn_lin1_w"], "lin1_b": col(a["ffn_lin1_b"]), "s2w1": a["ffn_swi2_w1"], "s2b1": col(a["ffn_swi2_b1"]),
        "s2w2": a["ffn_swi2_w2"], "s2b2": col(a["ffn_swi2_b2"]), "cT": t(a["c"]), "wmod": a["wmod"],
    }
    nc = bacc.Bacc("TRN2", target_bir_lowering=False, num_devices=1)
    arrays, args = {}, {}
    for name, v in laid.items():
        arrays[f"in_{name}"] = np.ascontiguousarray(v)
        args[name] = nc.dram_tensor(f"in_{name}", v.shape, mybir.dt.from_np(v.dtype), kind="ExternalInput").ap()
    args["out"] = nc.dram_tensor("out_0", (NB, S, D), F32, kind="ExternalOutput").ap()
    adaln_block(nc, **args)
    r = run(nc, [arrays], core_ids=[0])
    return r.results[0]["out_0"]
```

```python
from contextlib import ExitStack

import concourse.bass as bass
from concourse import mybir

ALU = mybir.AluOpType
ACT = mybir.ActivationFunctionType
AX = mybir.AxisListType
F32 = mybir.dt.float32
BF16 = mybir.dt.bfloat16
U32 = mybir.dt.uint32

P = 128
D = 128
NB = 16
S = 512
NT = S // P
TILES = NB * NT
E = 8
TOPA = 2
TOPF = 4
CAP = 256
H = 8
DK = 16
C = 64
NCH = CAP // C
ROW = 2 * D
G = NB * E
SH = 2
EPS = 1e-5
FAR = 1.0e6
LOW = -1.0e30


def bcast(ap, shape):
    return ap.to_broadcast(shape) if hasattr(ap, "to_broadcast") else ap.broadcast_to(shape)


def past(eng, semaphore, value):
    if not isinstance(value, int) or value > 0:
        eng.wait_ge(semaphore, value)


def adaln_block(nc, x, gate_wT, q_w, k_w, v_wT, fmT, norm_c, o_wT, lin0, lin0_b, s1w1, s1b1, s1w2, s1b2, fgateT,
                ew1, ew3, ew2, shw1, shw3, shw2, lin1, lin1_b, s2w1, s2b1, s2w2, s2b2, cT, wmod, out):
    ctx = ExitStack()
    with ctx:
        def sb(name, shape, dt=F32):
            return ctx.enter_context(nc.sbuf_tensor(name, shape, dt))

        def sem(name):
            return ctx.enter_context(nc.semaphore(name))

        hs = nc.dram_tensor("routed_rows", [(G + 1) * CAP, ROW], F32, kind="Internal").ap()
        osd = nc.dram_tensor("attended_rows", [G * CAP, D], F32, kind="Internal").ap()

        bank = [ctx.enter_context(nc.psum_tensor(f"bank{i}", [P, 512], F32)) for i in range(8)]

        x_all = sb("x_all", [P, TILES, D])
        hq = sb("hq", [P, TILES, ROW])
        ident = sb("ident", [P, P])
        identb = sb("identb", [P, P], BF16)
        headm = sb("headm", [P, P])
        parity = sb("parity", [P, 2])
        causal = sb("causal", [P, C])
        tri = sb("tri", [P, P], BF16)
        ones = sb("ones", [P, P], BF16)
        sel24 = sb("sel24", [3 * E, E, P], BF16)
        eslot = sb("eslot", [P, E])
        erow = sb("erow", [P, NB, E])
        mods = sb("mods", [P, 6, NB])
        k1T = sb("k1T", [P, E, P])
        k2T = sb("k2T", [P, E, P])
        q1T = sb("q1T", [P, P])
        q2T = sb("q2T", [P, P])
        vT = sb("vT", [P, E, P])
        oT = sb("oT", [P, P])
        gA = sb("gA", [P, E])
        gF = sb("gF", [P, E])
        mat = sb("mat", [P, 6, P])
        bias = sb("bias", [P, 6])
        w1s = sb("w1s", [P, E + SH, P])
        w3s = sb("w3s", [P, E + SH, P])
        w2s = sb("w2s", [P, E + SH, P])
        stats = sb("stats", [P, TILES, 6])
        mean = sb("mean", [P, TILES])
        rstd = sb("rstd", [P, TILES])
        lg = sb("lg", [P, TILES, E])
        wslot = sb("wslot", [P, TILES, TOPA])
        idxs = sb("idxs", [P, TILES, TOPA], U32)
        idxg = sb("idxg", [P, TILES, TOPA], U32)
        w24 = sb("w24", [P, TILES, 3 * E], BF16)

        ph = ExitStack()
        zero = ph.enter_context(nc.sbuf_tensor("zero", [P, CAP * E // P * ROW], F32))
        kw_raw = ph.enter_context(nc.sbuf_tensor("kw_raw", [P, E, P], F32))
        q_raw = ph.enter_context(nc.sbuf_tensor("q_raw", [P, P], F32))
        fm = ph.enter_context(nc.sbuf_tensor("fm", [P, 4, P], F32))
        cT_s = ph.enter_context(nc.sbuf_tensor("cT_s", [P, NB], F32))
        wmod_s = ph.enter_context(nc.sbuf_tensor("wmod_s", [P, 6 * P], F32))
        normc = ph.enter_context(nc.sbuf_tensor("normc", [P, 1], F32))
        sgn = ph.enter_context(nc.sbuf_tensor("sgn", [P, NB], F32))
        xh = ph.enter_context(nc.sbuf_tensor("xh", [P, 2, NT, D], F32))
        hT = ph.enter_context(nc.sbuf_tensor("hT", [P, 2, S], F32))
        q1s = ph.enter_context(nc.sbuf_tensor("q1s", [P, 2, S], F32))
        qT = ph.enter_context(nc.sbuf_tensor("qT", [P, 2, S], F32))
        tw = [ph.enter_context(nc.sbuf_tensor(f"tw{i}", [P, TILES, E], F32)) for i in range(4)]
        ta = [ph.enter_context(nc.sbuf_tensor(f"ta{i}", [P, TILES], F32)) for i in range(3)]
        selp = ph.enter_context(nc.sbuf_tensor("selp", [P, TILES, E], F32))
        selb = ph.enter_context(nc.sbuf_tensor("selb", [P, TILES, E], BF16))

        MASKS = 18
        NW = 8 + 6 + 6 + 8

        s_x = [sem(f"x_loaded{i}") for i in range(4)]
        s_w = sem("weights_loaded")
        s_mask = sem("masks_made")
        s_pmask = sem("parity_made")
        s_zero = sem("zero_made")
        s_zfill = sem("rows_zeroed")
        s_silu = sem("c_silu")
        s_mod = sem("mod_product")
        s_fold = sem("kq_folded")
        s_wcopy = sem("folded_copied")
        s_bd = sem("features_masked")
        s_ch = sem("vector_chain")
        s_var = sem("variance_ready")
        s_sq = sem("deviation_ready")
        s_mods = sem("mods_ready")
        s_xh = sem("normalised")
        s_xT = sem("normalised_turned")
        s_hT = sem("modulated")
        s_qp = sem("q_products")
        s_q1 = sem("q1_copied")
        s_qf = sem("q_features")
        s_hb = sem("h_and_logits")
        s_hqh = sem("h_rows_kept")
        s_lg = sem("logits_kept")
        s_qb = sem("q_turned")
        s_hqq = sem("q_rows_kept")
        s_e0 = sem("exponent_in")
        s_e1 = sem("exponent_out")
        s_selb = sem("selection_ready")
        s_cnt = sem("counts_ready")

        def newton(dve, link, dev, var, y, t):
            link(dve.reciprocal(y, dev))
            link(dve.tensor_tensor(t, y, y, ALU.mult))
            link(dve.tensor_tensor(t, t, var, ALU.mult))
            link(dve.tensor_scalar(t, t, -0.5, 1.5, ALU.mult, ALU.add))
            link(dve.tensor_tensor(y, y, t, ALU.mult))

        def norm_stats(dve, link, var, t):
            link(dve.tensor_tensor(mean[:, :], stats[:, :, 1], stats[:, :, 4], ALU.add))
            link(dve.tensor_scalar(mean[:, :], mean[:, :], 0.5, None, ALU.mult))
            link(dve.tensor_tensor(t, stats[:, :, 1], stats[:, :, 4], ALU.subtract))
            link(dve.tensor_tensor(t, t, t, ALU.mult))
            link(dve.tensor_scalar(t, t, 0.25, EPS, ALU.mult, ALU.add))
            link(dve.tensor_tensor(var, stats[:, :, 2], stats[:, :, 5], ALU.add))
            link(dve.scalar_tensor_tensor(out=var, in0=var, scalar=1.0 / D, in1=t, op0=ALU.mult, op1=ALU.add))

        def pick(dve, link, left, first, t, m):
            link(dve.tensor_reduce(m, left, AX.X, ALU.max))
            mb = m.unsqueeze(2).to_broadcast([P, TILES, E])
            link(dve.tensor_tensor(t, left, mb, ALU.is_equal))
            link(dve.tensor_tensor(t, t, eslot[:, :].unsqueeze(1).to_broadcast([P, TILES, E]), ALU.mult))
            link(dve.tensor_reduce(m, t, AX.X, ALU.max))
            link(dve.tensor_tensor(first, t, mb, ALU.is_equal))

        with nc.Block() as block:
            @block.sync
            def _(sp):
                xv = x.rearrange("b (i p) d -> p (b i) d", p=P)
                q = TILES // 4
                for n in range(4):
                    sp.dma_start(x_all[:, n * q:(n + 1) * q, :], xv[:, n * q:(n + 1) * q, :]).then_inc(s_x[n], 16)
                    if n == 0:
                        for dst, src in ((cT_s[:, :], cT), (wmod_s[:, :], wmod), (q_raw[:, :], q_w),
                                         (fm[:, :, :], fmT.rearrange("f k c -> k f c")), (gA[:, :], gate_wT),
                                         (normc[:, :], norm_c), (kw_raw[:, :, :], k_w.rearrange("e k c -> k e c")),
                                         (oT[:, :], o_wT)):
                            sp.dma_start(dst, src).then_inc(s_w, 16)
                for n, src in enumerate((lin0, s1w1, s1w2, lin1, s2w1, s2w2)):
                    sp.dma_start(mat[:, n, :], src).then_inc(s_w, 16)
                for n, src in enumerate((lin0_b, s1b1, s1b2, lin1_b, s2b1, s2b2)):
                    sp.dma_start(bias[:, n:n + 1], src).then_inc(s_w, 16)
                for dst, src in ((gF[:, :], fgateT), (vT[:, :, :], v_wT.rearrange("e c k -> c e k")),
                                 (w1s[:, 0:E, :], ew1.rearrange("e d h -> d e h")),
                                 (w3s[:, 0:E, :], ew3.rearrange("e d h -> d e h")),
                                 (w2s[:, 0:E, :], ew2.rearrange("e h d -> h e d")),
                                 (w1s[:, E:E + SH, :], shw1.rearrange("d (s h) -> d s h", s=SH)),
                                 (w3s[:, E:E + SH, :], shw3.rearrange("d (s h) -> d s h", s=SH)),
                                 (w2s[:, E:E + SH, :], shw2.rearrange("(s h) d -> h s d", s=SH))):
                    sp.dma_start(dst, src).then_inc(s_w, 16)
                sp.wait_ge(s_w, 16 * NW)
                sp.wait_ge(s_zero, 1)
                zrow = CAP * E // P
                for b in range(NB):
                    sp.dma_start(hs[b * CAP * E:(b + 1) * CAP * E, :].rearrange("(p r) w -> p (r w)", r=zrow),
                                 zero[:, :]).then_inc(s_zfill, 16)
                sp.dma_start(hs[G * CAP:(G + 1) * CAP, :].rearrange("(p r) w -> p (r w)", p=P),
                             zero[:, 0:CAP // P * ROW]).then_inc(s_zfill, 16)
                sp.wait_ge(s_zfill, 16 * (NB + 1))

            @block.gpsimd
            def _(pool):
                made = [0]

                def link(ins):
                    made[0] += 1
                    ins.then_inc(s_mask, 1)
                    pool.wait_ge(s_mask, made[0])

                pool.memset(zero[:, :], 0.0).then_inc(s_zero, 1)
                link(pool.memset(ident[:, :], 0.0))
                link(pool.affine_select(out=ident[:, :], in_=ident[:, :], compare_op=ALU.not_equal, fill=1.0, base=0,
                                        pattern=[[-1, P]], channel_multiplier=1))
                link(pool.tensor_copy(identb[:, :], ident[:, :]))
                link(pool.memset(headm[:, :], 1.0))
                hv = headm[:, :].rearrange("p (h d) -> p h d", d=DK)
                link(pool.affine_select(out=hv, in_=hv, compare_op=ALU.is_ge, fill=0.0, base=0,
                                        pattern=[[-DK, H], [0, DK]], channel_multiplier=1))
                link(pool.affine_select(out=hv, in_=hv, compare_op=ALU.is_ge, fill=0.0, base=DK - 1,
                                        pattern=[[DK, H], [0, DK]], channel_multiplier=-1))
                link(pool.memset(causal[:, :], 1.0))
                link(pool.affine_select(out=causal[:, :], in_=causal[:, :], compare_op=ALU.is_ge, fill=0.0, base=C,
                                        pattern=[[1, C]], channel_multiplier=-1))
                link(pool.affine_select(out=causal[0:C, :], in_=causal[0:C, :], compare_op=ALU.is_ge, fill=0.0,
                                        base=0, pattern=[[1, C]], channel_multiplier=-1))
                link(pool.memset(tri[:, :], 1.0))
                link(pool.affine_select(out=tri[:, :], in_=tri[:, :], compare_op=ALU.is_ge, fill=0.0, base=0,
                                        pattern=[[-1, P]], channel_multiplier=1))
                link(pool.memset(ones[:, :], 1.0))
                link(pool.memset(sel24[:, :, :], 0.0))
                for part in range(3):
                    link(pool.affine_select(out=sel24[:, :, :], in_=sel24[:, :, :], compare_op=ALU.not_equal, fill=1.0,
                                            base=-part * E, pattern=[[-1, E], [0, P]], channel_multiplier=1))
                link(pool.iota(eslot[:, :], [[-1, E]], base=E, channel_multiplier=0,
                               allow_small_or_imprecise_dtypes=True))
                link(pool.iota(erow[:, :, :], [[E * CAP, NB], [CAP, E]], base=CAP, channel_multiplier=0,
                               allow_small_or_imprecise_dtypes=True))
                assert made[0] == MASKS

            @block.scalar
            def _(act):
                act.wait_ge(s_w, 16 * NW)
                act.activation(cT_s[:, :], cT_s[:, :], ACT.Silu).then_inc(s_silu, 1)
                act.wait_ge(s_fold, 1)
                act.activation(q1T[:, :], bank[7][:, 256:384], ACT.Copy).then_inc(s_wcopy, 1)
                act.activation(q2T[:, :], bank[7][:, 384:512], ACT.Copy).then_inc(s_wcopy, 1)
                for e in range(E):
                    act.wait_ge(s_fold, 2 + e)
                    act.activation(k1T[:, e, :], bank[e % 4][:, 0:P], ACT.Copy)
                    act.activation(k2T[:, e, :], bank[e % 4][:, P:2 * P], ACT.Copy).then_inc(s_wcopy, 1)
                act.wait_ge(s_var, 1)
                act.activation(ta[1][:, :], ta[0][:, :], ACT.Sqrt).then_inc(s_sq, 1)
                act.wait_ge(s_mods, 1)
                with act.Fori(0, NB // 2) as bb:
                    for u in range(2):
                        b = 2 * bb + u
                        act.wait_ge(s_xT, b + 1)
                        act.activation(hT[:, u, :], bank[u][:, :], ACT.Identity, bias=mods[:, 0, bass.ds(b, 1)],
                                       scale=mods[:, 1, bass.ds(b, 1)]).then_inc(s_hT, 1)
                        act.wait_ge(s_qp, b + 1)
                        act.activation(q1s[:, u, :], bank[2][:, :], ACT.Copy).then_inc(s_q1, 1)
                        act.wait_ge(s_hb, b + 1)
                        act.activation(hq[:, bass.ds(b * NT, NT), 0:D],
                                       bank[5][:, :].rearrange("p (i d) -> p i d", d=D), ACT.Copy).then_inc(s_hqh, 1)
                        act.wait_ge(s_qb, b + 1)
                        act.activation(hq[:, bass.ds(b * NT, NT), D:ROW],
                                       bank[6][:, :].rearrange("p (i d) -> p i d", d=D), ACT.Copy).then_inc(s_hqq, 1)
                act.wait_ge(s_e0, 1)
                act.activation(tw[2][:, :, :], tw[2][:, :, :], ACT.Exp).then_inc(s_e1, 1)

            @block.tensor
            def _(pe):
                pe.wait_ge(s_w, 16 * NW)
                pe.wait_ge(s_silu, 1)
                for j in range(6):
                    mm = pe.matmul(bank[7][:, j * NB:(j + 1) * NB], wmod_s[:, j * P:(j + 1) * P], cT_s[:, :],
                                   start=True, stop=True)
                mm.then_inc(s_mod, 1)
                pe.wait_ge(s_bd, 1)
                pe.wait_ge(s_mods, 1)
                mm = pe.matmul(bank[7][:, 256:512], q_raw[:, :], fm[:, 0:2, :].rearrange("p f c -> p (f c)"),
                               start=True, stop=True)
                mm.then_inc(s_fold, 1)
                for e in range(E):
                    if e >= 4:
                        pe.wait_ge(s_wcopy, 2 + e - 3)
                    pe.matmul(bank[e % 4][:, 0:2 * P], kw_raw[:, e, :], fm[:, 2:4, :].rearrange("p f c -> p (f c)"),
                              start=True, stop=True).then_inc(s_fold, 1)
                pe.wait_ge(s_wcopy, 2 + E)
                pe.wait_ge(s_mask, MASKS)
                with pe.Fori(0, NB // 2) as bb:
                    for u in range(2):
                        b = 2 * bb + u
                        pe.wait_ge(s_xh, b + 1)
                        for i in range(NT):
                            mm = pe.transpose(bank[u][:, i * P:(i + 1) * P], xh[:, u, i, :], ident[:, :])
                        mm.then_inc(s_xT, 1)
                        pe.wait_ge(s_hT, b + 1)
                        pe.wait_ge(s_qf, b)
                        pe.matmul(bank[2][:, :], q1T[:, :], hT[:, u, :], start=True, stop=True)
                        pe.matmul(bank[3][:, :], q2T[:, :], hT[:, u, :], start=True, stop=True).then_inc(s_qp, 1)
                        pe.wait_ge(s_lg, b)
                        pe.wait_ge(s_hqh, b)
                        for i in range(NT):
                            pe.matmul(bank[4][:, i * E:(i + 1) * E], hT[:, u, i * P:(i + 1) * P], gA[:, :],
                                      start=True, stop=True)
                        for i in range(NT):
                            mm = pe.transpose(bank[5][:, i * P:(i + 1) * P], hT[:, u, i * P:(i + 1) * P], ident[:, :])
                        mm.then_inc(s_hb, 1)
                        pe.wait_ge(s_qf, b + 1)
                        pe.wait_ge(s_hqq, b)
                        for i in range(NT):
                            mm = pe.transpose(bank[6][:, i * P:(i + 1) * P], qT[:, u, i * P:(i + 1) * P], ident[:, :])
                        mm.then_inc(s_qb, 1)
                pe.wait_ge(s_selb, 1)
                flat = selb[:, :, :].rearrange("p t e -> p (t e)")
                pe.matmul(bank[0][:, :], tri[:, :], flat, start=True, stop=True)
                pe.matmul(bank[1][:, :], ones[:, :], flat, start=True, stop=True).then_inc(s_cnt, 1)

            @block.vector
            def _(dve):
                count = [0]

                def link(ins):
                    count[0] += 1
                    ins.then_inc(s_ch, 1)
                    dve.wait_ge(s_ch, count[0])

                dve.wait_ge(s_w, 16 * NW)
                dve.wait_ge(s_mask, MASKS)
                for f in range(4):
                    ins = dve.tensor_tensor(fm[:, f, :], fm[:, f, :], headm[:, :], ALU.mult)
                ins.then_inc(s_bd, 1)
                for par in range(2):
                    link(dve.tensor_reduce(parity[:, par:par + 1],
                                           headm[:, :].rearrange("p (h r) -> p h r", r=2 * DK)[:, :, par * DK],
                                           AX.X, ALU.add))
                link(dve.tensor_scalar(oT[:, :], oT[:, :], normc[:, 0:1], None, ALU.mult))
                dve.wait_ge(s_mod, 1)
                link(dve.tensor_copy(mods[:, :, :], bank[7][:, 0:6 * NB].rearrange("p (j b) -> p j b", b=NB)))
                for j in (1, 4):
                    link(dve.tensor_scalar(mods[:, j, :], mods[:, j, :], 1.0, None, ALU.add))
                for j in (2, 5):
                    link(dve.tensor_scalar(sgn[:, :], mods[:, j, :], 0.0, 2.0, ALU.is_ge, ALU.mult))
                    link(dve.tensor_scalar(sgn[:, :], sgn[:, :], -1.0, None, ALU.add))
                    link(dve.tensor_tensor(mods[:, j, :], mods[:, j, :], sgn[:, :], ALU.mult))
                    link(dve.tensor_scalar(mods[:, j, :], mods[:, j, :], 0.25, None, ALU.max))
                    link(dve.tensor_tensor(mods[:, j, :], mods[:, j, :], sgn[:, :], ALU.mult))
                dve.sem_inc(s_mods, 1)
                q = TILES // 4
                base = count[0]
                for n in range(4):
                    dve.wait_ge(s_x[n], 16)
                    with dve.Fori(n * q // NT, (n + 1) * q // NT) as tt:
                        for i in range(NT):
                            dve.bn_stats(stats[:, NT * tt + i, :], x_all[:, NT * tt + i, :]).then_inc(s_ch, 1)
                count[0] = base + TILES
                dve.wait_ge(s_ch, count[0])
                norm_stats(dve, link, ta[0][:, :], ta[2][:, :])
                dve.sem_inc(s_var, 1)
                dve.wait_ge(s_sq, 1)
                newton(dve, link, ta[1][:, :], ta[0][:, :], rstd[:, :], ta[2][:, :])
                with dve.Fori(0, NB // 2) as bb:
                    for u in range(2):
                        b = 2 * bb + u
                        if u == 0:
                            dve.wait_ge(s_xT, 2 * bb)
                        for i in range(NT):
                            t = b * NT + i
                            ins = dve.tensor_scalar(xh[:, u, i, :], x_all[:, t, :], mean[:, bass.ds(t, 1)],
                                                    rstd[:, bass.ds(t, 1)], ALU.subtract, ALU.mult)
                        ins.then_inc(s_xh, 1)
                    for u in range(2):
                        b = 2 * bb + u
                        dve.wait_ge(s_hb, b + 1)
                        dve.tensor_copy(lg[:, bass.ds(b * NT, NT), :],
                                        bank[4][:, 0:NT * E].rearrange("p (i e) -> p i e", e=E)).then_inc(s_lg, 1)
                        dve.wait_ge(s_q1, b + 1)
                        dve.scalar_tensor_tensor(out=qT[:, u, :], in0=bank[3][:, :], scalar=DK ** -0.5,
                                                 in1=q1s[:, u, :], op0=ALU.mult, op1=ALU.mult).then_inc(s_qf, 1)
                dve.wait_ge(s_lg, NB)
                one, two, left, t = (v[:, :, :] for v in (tw[0], tw[1], tw[3], tw[2]))
                m = ta[0][:, :]
                pick(dve, link, lg[:, :, :], one, t, m)
                link(dve.scalar_tensor_tensor(out=left, in0=one, scalar=LOW, in1=lg[:, :, :], op0=ALU.mult, op1=ALU.add))
                pick(dve, link, left, two, t, m)
                link(dve.tensor_reduce(m, lg[:, :, :], AX.X, ALU.max))
                link(dve.tensor_tensor(t, lg[:, :, :], m.unsqueeze(2).to_broadcast([P, TILES, E]), ALU.subtract))
                dve.sem_inc(s_e0, 1)
                link(dve.tensor_tensor(left, one, two, ALU.add))
                link(dve.tensor_copy(selb[:, :, :], left))
                dve.sem_inc(s_selb, 1)
                dve.wait_ge(s_e1, 1)
                link(dve.tensor_tensor(t, t, left, ALU.mult))
                link(dve.tensor_reduce(m, t, AX.X, ALU.add))
                link(dve.reciprocal(ta[1][:, :], m))
                link(dve.tensor_tensor(t, t, ta[1][:, :].unsqueeze(2).to_broadcast([P, TILES, E]), ALU.mult))
                dve.wait_ge(s_cnt, 1)
                cnt = lg[:, :, :]
                cb = lg[:, :, :].rearrange("p (b i) e -> p b i e", i=NT)
                tot = left.rearrange("p (b i) e -> p b i e", i=NT)
                link(dve.tensor_copy(cnt, bank[0][:, :].rearrange("p (t e) -> p t e", e=E)))
                link(dve.tensor_copy(left, bank[1][:, :].rearrange("p (t e) -> p t e", e=E)))
                for i in range(NT - 2, -1, -1):
                    link(dve.tensor_tensor(cb[:, :, i, :], cb[:, :, i, :], tot[:, :, i + 1, :], ALU.add))
                    if i:
                        link(dve.tensor_tensor(tot[:, :, i, :], tot[:, :, i, :], tot[:, :, i + 1, :], ALU.add))
                keep = left
                link(dve.tensor_scalar(keep, cnt, float(CAP), None, ALU.is_le))
                for i in range(NT):
                    link(dve.tensor_tensor(cb[:, :, i, :], erow[:, :, :], cb[:, :, i, :], ALU.subtract))
                for s, oh in enumerate((one, two)):
                    link(dve.tensor_tensor(oh, oh, keep, ALU.mult))
                    kept, row = ta[1][:, :], ta[2][:, :]
                    link(dve.tensor_reduce(kept, oh, AX.X, ALU.add))
                    prod = selp[:, :, :]
                    link(dve.tensor_tensor(prod, oh, t, ALU.mult))
                    link(dve.tensor_reduce(wslot[:, :, s], prod, AX.X, ALU.add))
                    link(dve.tensor_tensor(prod, oh, cnt, ALU.mult))
                    link(dve.tensor_reduce(row, prod, AX.X, ALU.add))
                    link(dve.tensor_copy(idxg[:, :, s], row))
                    link(dve.tensor_scalar(kept, kept, -FAR, FAR, ALU.mult, ALU.add))
                    link(dve.tensor_tensor(row, row, kept, ALU.add))
                    link(dve.tensor_copy(idxs[:, :, s], row))

        ph.close()

        ph = ExitStack()

        def tb(name, shape, dt=F32):
            return ph.enter_context(nc.sbuf_tensor(name, shape, dt))

        RING = 4
        AHEAD = 2
        srow = tb("srow", [P, NT, ROW])
        sidx = tb("sidx", [P, NT * TOPA], U32)
        rows = tb("rows", [P, RING, 2, ROW])
        turned = tb("turned", [P, RING, 2, 2 * P])
        k1s = tb("k1s", [P, 2 * P])
        kx = tb("kx", [P, NCH, 2, C])
        kr = tb("kr", [P, NCH - 1, P])
        vx = tb("vx", [P, 2, NCH, 4, 2, DK])
        att = tb("att", [P, NCH, 4, C])
        qx = tb("qx", [P, 2, NCH, 4, C])
        oTs = tb("oTs", [P, 2 * P])
        st = tb("st", [P, 3, P])
        ob = tb("ob", [P, 2, 2, P])

        s_scat = sem("rows_scattered")
        s_ld = [sem(f"rows_loaded{i}") for i in range(RING)]
        s_t = sem("rows_turned")
        s_te = sem("turned_copied")
        s_qa = sem("q_split_upper")
        s_qd = sem("q_split_lower")
        s_k = sem("k_products")
        s_ke = sem("k1_copied")
        s_kf = sem("k_features")
        s_kt = sem("k_turned")
        s_kte = sem("k_rows_copied")
        s_v = sem("values_ready")
        s_ve = sem("values_copied")
        s_vz = sem("zeros_between")
        s_s = sem("scores_ready")
        s_a = sem("scores_masked")
        s_st = sem("states_ready")
        s_stm = sem("states_masked")
        s_ste = sem("states_summed")
        s_o = sem("attended")
        s_oc = sem("attended_copied")
        s_ot = sem("attended_turned")
        s_oe = sem("attended_rows_ready")
        s_os = [sem("attended_stored0"), sem("attended_stored1")]


        def batches(eng, batch):
            batch(0, False, True)
            with eng.Fori(1, NB - 1) as b:
                batch(b, False, False)
            batch(NB - 1, True, False)

        with nc.Block() as block:
            @block.gpsimd
            def _(pool):
                def scatter(b):
                    past(pool, s_scat, 16 * NT * TOPA * b)
                    pool.tensor_copy(srow[:, :, :], hq[:, bass.ds(b * NT, NT), :])
                    pool.tensor_copy(sidx[:, :], idxs[:, bass.ds(b * NT, NT), :]
                                     .rearrange("p i s -> p (i s)"))
                    pool.drain()
                    for i in range(NT):
                        for s in range(TOPA):
                            k = i * TOPA + s
                            pool.indirect_dma_start(hs, bass.IndirectOffsetOnAxis(sidx[:, k:k + 1], 0),
                                                    srow[:, i, :], None, bounds_check=G * CAP - 1,
                                                    oob_is_err=False).then_inc(s_scat, 16)

                pool.memset(vx[:, :, :, :, :, :], 0.0)
                pool.memset(qx[:, :, :, :, :], 0.0).then_inc(s_vz, 1)
                scatter(0)
                with pool.Fori(1, NB) as b:
                    scatter(b)
                pool.wait_ge(s_scat, 16 * NT * TOPA * NB)

            @block.sync
            def _(sp):
                hv = hs.rearrange("(g a p) w -> g p a w", a=2, p=P)
                ov = osd.rearrange("(g a p) d -> g p a d", a=2, p=P)

                def load(g, slot):
                    sp.dma_start(rows[:, slot, :, :], hv[g]).then_inc(s_ld[slot], 16)

                def batch(b, last, first):
                    for e in range(E):
                        g = b * E + e
                        if not last or e < E - AHEAD - RING:
                            sp.wait_ge(s_t, g + AHEAD + 1)
                            if e == E - AHEAD - RING:
                                sp.wait_ge(s_scat, 16 * NT * TOPA * (b + 2))
                            load(g + AHEAD + RING, (e + AHEAD) % RING)
                        sp.wait_ge(s_oe, g + 1)
                        sp.dma_start(ov[g], ob[:, e % 2, :, :]).then_inc(s_os[e % 2], 16)

                sp.wait_ge(s_scat, 16 * NT * TOPA)
                for e in range(RING):
                    load(e, e)
                for e in range(AHEAD):
                    sp.wait_ge(s_t, e + 1)
                    load(RING + e, e)
                batches(sp, batch)
                for i in range(2):
                    sp.wait_ge(s_os[i], 16 * G // 2)

            @block.scalar
            def _(act):
                def turn(n, e):
                    act.wait_ge(s_t, n + 1)
                    act.activation(turned[:, e % RING, :, :].rearrange("p a c -> p (a c)"), bank[2][:, :],
                                   ACT.Copy).then_inc(s_te, 1)

                def split_q(n, e):
                    for p in (0, 1):
                        r = slice(32 * p, 32 * p + 32)
                        ins = act.activation(qx[r, e % 2, :, p, :],
                                             turned[r, e % RING, 1, :].rearrange("r (n t) -> r n t", t=C), ACT.Copy)
                    ins.then_inc(s_qa, 1)

                def first_k(n):
                    act.wait_ge(s_k, n + 1)
                    past(act, s_kf, n)
                    act.activation(k1s[:, :], bank[5][:, 0:2 * P], ACT.Copy).then_inc(s_ke, 1)

                def keep_values(n, e):
                    act.wait_ge(s_v, n + 1)
                    for par in range(2):
                        r = slice(par * C, (par + 1) * C)
                        ins = act.activation(vx[r, e % 2, :, :, par, :],
                                             bank[6][r, 0:NCH * C].rearrange("r (n p d) -> r n p d", n=NCH, d=DK),
                                             ACT.Copy)
                    ins.then_inc(s_ve, 1)

                def keep_k(n):
                    act.wait_ge(s_kt, n + 1)
                    act.activation(kr[:, :, :].rearrange("p n c -> p (n c)"), bank[4][:, 0:3 * P],
                                   ACT.Copy).then_inc(s_kte, 1)

                def keep_outputs(g):
                    act.wait_ge(s_o, g + 1)
                    act.activation(oTs[:, :], bank[7][:, 0:2 * P], ACT.Copy).then_inc(s_oc, 1)

                def output_rows(g, b, e):
                    act.wait_ge(s_ot, g + 1)
                    past(act, s_os[e % 2], 16 * (b * (E // 2) + e // 2))
                    act.activation(ob[:, e % 2, :, :].rearrange("p a c -> p (a c)"), bank[4][:, 0:2 * P],
                                   ACT.Copy).then_inc(s_oe, 1)

                def batch(b, last, first):
                    for e in range(E):
                        g = b * E + e
                        follows = not last or e < E - 1
                        if e:
                            output_rows(g - 1, b, e - 1)
                        elif not first:
                            output_rows(g - 1, b - 1, E - 1)
                        if follows:
                            act.wait_ge(s_te, g + 2)
                            split_q(g + 1, e + 1)
                            first_k(g + 1)
                            keep_values(g + 1, e + 1)
                        keep_outputs(g)
                        if not last or e < E - AHEAD:
                            turn(g + AHEAD, e + AHEAD)
                        if follows:
                            keep_k(g + 1)

                for e in range(AHEAD):
                    turn(e, e)
                first_k(0)
                act.wait_ge(s_vz, 1)
                act.wait_ge(s_te, 1)
                split_q(0, 0)
                keep_values(0, 0)
                keep_k(0)
                batches(act, batch)
                output_rows(G - 1, NB - 1, E - 1)

            @block.tensor
            def _(pe):
                def turn(n, e, b):
                    pe.wait_ge(s_ld[e % RING], 16 * (b * (E // RING) + e // RING + 1))
                    for part in range(2):
                        for a in range(2):
                            mm = pe.transpose(bank[2][:, part * 2 * P + a * P:part * 2 * P + (a + 1) * P],
                                              rows[:, e % RING, a, part * D:(part + 1) * D], ident[:, :])
                    mm.then_inc(s_t, 1)

                def keys(n, e):
                    pe.wait_ge(s_te, n + 1)
                    hT2 = turned[:, e % RING, 0, :]
                    pe.matmul(bank[5][:, 0:2 * P], k1T[:, e % E, :], hT2, start=True, stop=True)
                    pe.matmul(bank[5][:, 2 * P:4 * P], k2T[:, e % E, :], hT2, start=True, stop=True).then_inc(s_k, 1)

                def values(n, e):
                    vh = vT[:, e % E, :].rearrange("c (p r d) -> c r p d", r=2, d=DK)
                    for n in range(NCH):
                        for par in range(2):
                            mm = pe.matmul(bank[6][par * C:(par + 1) * C, n * C:(n + 1) * C],
                                           turned[:, e % RING, 0, n * C:(n + 1) * C], vh[:, par], start=True, stop=True)
                    mm.then_inc(s_v, 1)

                def turn_k(n):
                    pe.wait_ge(s_kf, n + 1)
                    past(pe, s_oe, n - 1)
                    for m in range(NCH - 1):
                        mm = pe.transpose(bank[4][:, m * P:(m + 1) * P],
                                          kx[:, m, :, :].rearrange("p r t -> p (r t)"), ident[:, :])
                    mm.then_inc(s_kt, 1)

                def scores(g, e):
                    pe.wait_ge(s_kf, g + 1)
                    pe.wait_ge(s_qa, g + 1)
                    pe.wait_ge(s_qd, g + 1)
                    for n in range(NCH):
                        mm = pe.matmul(bank[n // 2][:, n % 2 * 4 * C:(n % 2 + 1) * 4 * C],
                                       kx[:, n, :, :].rearrange("p r t -> p (r t)"),
                                       qx[:, e % 2, n, :, :].rearrange("p h t -> p (h t)"), start=True, stop=True)
                        if n % 2:
                            mm.then_inc(s_s, 1)

                def states(g, e):
                    pe.wait_ge(s_kte, g + 1)
                    pe.wait_ge(s_ve, g + 1)
                    past(pe, s_oc, g)
                    for m in range(NCH - 1):
                        mm = pe.matmul(bank[7][:, m * P:(m + 1) * P], kr[:, m, :],
                                       vx[:, e % 2, m, :, :, :].rearrange("p h r d -> p (h r d)"),
                                       start=True, stop=True)
                    mm.then_inc(s_st, 1)

                def attend(g, e):
                    pe.wait_ge(s_a, 2 * (g + 1))
                    pe.wait_ge(s_ste, g + 1)
                    for n in (1, 2, 3, 0):
                        if n:
                            pe.matmul(bank[7][:, n * C:(n + 1) * C], st[:, n - 1, :],
                                      turned[:, e % RING, 1, n * C:(n + 1) * C], start=True, stop=True,
                                      skip_group_check=True)
                        for p in range(4):
                            mm = pe.matmul(bank[7][32 * p:32 * p + 32, n * C:(n + 1) * C],
                                           vx[:, e % 2, n, p, :, :].rearrange("p r d -> p (r d)"),
                                           att[:, n, p, :], start=(n == 0), stop=True,
                                           skip_group_check=True)
                    mm.then_inc(s_o, 1)

                def turn_outputs(g):
                    pe.wait_ge(s_oc, g + 1)
                    for a in range(2):
                        mm = pe.transpose(bank[4][:, a * P:(a + 1) * P], oTs[:, a * P:(a + 1) * P], ident[:, :])
                    mm.then_inc(s_ot, 1)

                def batch(b, last, first):
                    for e in range(E):
                        g = b * E + e
                        follows = not last or e < E - 1
                        scores(g, e)
                        states(g, e)
                        if e or not first:
                            turn_outputs(g - 1)
                        if follows:
                            keys(g + 1, e + 1)
                            values(g + 1, e + 1)
                        attend(g, e)
                        if not last or e < E - AHEAD:
                            turn(g + AHEAD, e + AHEAD, b)
                        if follows:
                            turn_k(g + 1)

                turn(0, 0, 0)
                pe.wait_ge(s_te, 1)
                turn(1, 1, 0)
                keys(0, 0)
                values(0, 0)
                turn_k(0)
                batches(pe, batch)
                turn_outputs(G - 1)

            @block.vector
            def _(dve):
                def k_features(n):
                    dve.wait_ge(s_ke, n + 1)
                    for par in range(2):
                        ins = dve.scalar_tensor_tensor(
                            out=kx[:, :, par, :], in0=bank[5][:, 2 * P:4 * P].rearrange("p (n t) -> p n t", t=C),
                            scalar=parity[:, par:par + 1], in1=k1s[:, :].rearrange("p (n t) -> p n t", t=C),
                            op0=ALU.mult, op1=ALU.mult)
                    ins.then_inc(s_kf, 1)

                def split_q(n, e):
                    dve.wait_ge(s_te, n + 1)
                    for p in (2, 3):
                        r = slice(32 * p, 32 * p + 32)
                        ins = dve.tensor_copy(qx[r, e % 2, :, p, :],
                                              turned[r, e % RING, 1, :].rearrange("r (n t) -> r n t", t=C))
                    ins.then_inc(s_qd, 1)

                def mask_scores(g, a):
                    dve.wait_ge(s_s, 2 * g + a + 1)
                    dve.tensor_tensor(att[:, 2 * a:2 * a + 2, :, :].rearrange("k n p t -> k (n p) t"),
                                      bank[a][:, :].rearrange("k (x t) -> k x t", t=C),
                                      causal[:, :].unsqueeze(1).to_broadcast([P, 8, C]), ALU.mult).then_inc(s_a, 1)

                def sum_states(g, step):
                    if step == 0:
                        dve.wait_ge(s_st, g + 1)
                        dve.tensor_tensor(st[:, :, :], bank[7][:, 0:3 * P].rearrange("p (n d) -> p n d", d=P),
                                          headm[:, :].unsqueeze(1).to_broadcast([P, 3, P]), ALU.mult).then_inc(s_stm, 1)
                    else:
                        dve.wait_ge(s_stm, 2 * g + step)
                        dve.tensor_tensor(st[:, step, :], st[:, step, :], st[:, step - 1, :],
                                          ALU.add).then_inc(s_stm if step == 1 else s_ste, 1)

                def batch(b, last, first):
                    for e in range(E):
                        g = b * E + e
                        mask_scores(g, 0)
                        mask_scores(g, 1)
                        sum_states(g, 0)
                        sum_states(g, 1)
                        sum_states(g, 2)
                        if not last or e < E - 1:
                            split_q(g + 1, e + 1)
                        if not last or e < E - 1:
                            k_features(g + 1)

                dve.wait_ge(s_vz, 1)
                split_q(0, 0)
                k_features(0)
                batches(dve, batch)
        ph.close()

        ph = ExitStack()
        gst = tb("gst", [P, 2, NT * TOPA, D])
        gidx = tb("gidx", [P, 2, NT * TOPA], U32)
        sqs = tb("sqs", [P, NT, D])
        ss = tb("ss", [P, NB * NT * H])
        dev = tb("dev", [P, NB * NT * H])
        rr = tb("rr", [P, NB * NT * H])
        tt = tb("tt", [P, NB * NT * H])
        on = tb("on", [P, 2, NT, D])
        onT = tb("onT", [P, 2, S])
        aT = tb("aT", [P, 2, S])

        s_g = [sem("rows_gathered0"), sem("rows_gathered1")]
        s_gm = sem("gathered_weighed")
        s_c1 = sem("combine_chain")
        s_v1 = sem("head_variance")
        s_v2 = sem("head_deviation")
        s_on = sem("heads_normalised")
        s_onT = sem("heads_turned")
        s_onc = sem("heads_copied")
        s_y = sem("projected")
        s_yc = sem("gated")
        s_yT = sem("gated_turned")
        s_x2 = sem("residual_added")
        s_v3 = sem("norm_variance")
        s_v4 = sem("norm_deviation")
        o_all = hq[:, :, 0:D]

        with nc.Block() as block:
            @block.gpsimd
            def _(pool):
                with pool.Fori(0, NB // 2) as bb:
                    for u in range(2):
                        b = 2 * bb + u
                        if u == 0:
                            pool.wait_ge(s_gm, 2 * bb)
                        pool.tensor_copy(gidx[:, u, :], idxg[:, bass.ds(b * NT, NT), :]
                                         .rearrange("p i s -> p (i s)"))
                        pool.drain()
                        for k in range(NT * TOPA):
                            pool.indirect_dma_start(gst[:, u, k, :], None, osd,
                                                    bass.IndirectOffsetOnAxis(gidx[:, u, k:k + 1], 0),
                                                    bounds_check=G * CAP - 1, oob_is_err=False).then_inc(s_g[u], 16)

            @block.scalar
            def _(act):
                act.wait_ge(s_v1, 1)
                act.activation(dev[:, :], ss[:, :], ACT.Sqrt).then_inc(s_v2, 1)
                with act.Fori(0, NB // 2) as bb:
                    for u in range(2):
                        b = 2 * bb + u
                        act.wait_ge(s_onT, b + 1)
                        act.activation(onT[:, u, :], bank[u][:, :], ACT.Copy).then_inc(s_onc, 1)
                        act.wait_ge(s_y, b + 1)
                        act.activation(aT[:, u, :], bank[2 + u][:, :], ACT.Copy,
                                       scale=mods[:, 2, bass.ds(b, 1)]).then_inc(s_yc, 1)
                act.wait_ge(s_v3, 1)
                act.activation(dev[:, 0:TILES], ss[:, 0:TILES], ACT.Sqrt).then_inc(s_v4, 1)

            @block.tensor
            def _(pe):
                with pe.Fori(0, NB // 2) as bb:
                    for u in range(2):
                        b = 2 * bb + u
                        pe.wait_ge(s_on, b + 1)
                        for i in range(NT):
                            mm = pe.transpose(bank[u][:, i * P:(i + 1) * P], on[:, u, i, :], ident[:, :])
                        mm.then_inc(s_onT, 1)
                        pe.wait_ge(s_onc, b + 1)
                        pe.matmul(bank[2 + u][:, :], oT[:, :], onT[:, u, :], start=True, stop=True).then_inc(s_y, 1)
                        pe.wait_ge(s_yc, b + 1)
                        if u == 0:
                            pe.wait_ge(s_x2, 2 * bb)
                        for i in range(NT):
                            mm = pe.transpose(bank[4 + u][:, i * P:(i + 1) * P], aT[:, u, i * P:(i + 1) * P],
                                              ident[:, :])
                        mm.then_inc(s_yT, 1)

            @block.vector
            def _(dve):
                count = [0]

                def link(ins):
                    count[0] += 1
                    ins.then_inc(s_c1, 1)
                    dve.wait_ge(s_c1, count[0])

                with dve.Fori(0, NB // 2) as bb:
                    for u in range(2):
                        b = 2 * bb + u
                        dve.wait_ge(s_g[u], 16 * NT * TOPA * (bb + 1))
                        w = wslot[:, bass.ds(b * NT, NT), :].rearrange("p i s -> p (i s)").unsqueeze(2)
                        dve.tensor_tensor(gst[:, u, :, :], gst[:, u, :, :], w.to_broadcast([P, NT * TOPA, D]),
                                          ALU.mult).then_inc(s_c1, 1)
                        dve.wait_ge(s_c1, 4 * b + 1)
                        gv = gst[:, u, :, :].rearrange("p (i s) d -> p i s d", s=TOPA)
                        o = o_all[:, bass.ds(b * NT, NT), :]
                        dve.tensor_tensor(o, gv[:, :, 0, :], gv[:, :, 1, :], ALU.add).then_inc(s_c1, 1)
                        dve.wait_ge(s_c1, 4 * b + 2)
                        dve.tensor_tensor(sqs[:, :, :], o, o, ALU.mult).then_inc(s_c1, 1)
                        dve.wait_ge(s_c1, 4 * b + 3)
                        dve.tensor_reduce(ss[:, bass.ds(b * NT * H, NT * H)],
                                          sqs[:, :, :].rearrange("p i (h d) -> p (i h) d", d=DK), AX.X,
                                          ALU.add).then_inc(s_c1, 1)
                        dve.wait_ge(s_c1, 4 * b + 4)
                        dve.sem_inc(s_gm, 1)
                count[0] = 4 * NB
                link(dve.tensor_scalar(ss[:, :], ss[:, :], 1.0 / DK, EPS, ALU.mult, ALU.add))
                dve.sem_inc(s_v1, 1)
                dve.wait_ge(s_v2, 1)
                newton(dve, link, dev[:, :], ss[:, :], rr[:, :], tt[:, :])

                def normalise(b, u):
                    o = o_all[:, bass.ds(b * NT, NT), :].rearrange("p i (h d) -> p i h d", d=DK)
                    r = rr[:, bass.ds(b * NT * H, NT * H)].rearrange("p (i h) -> p i h", h=H)
                    dve.tensor_tensor(on[:, u, :, :].rearrange("p i (h d) -> p i h d", d=DK), o,
                                      r.unsqueeze(3).to_broadcast([P, NT, H, DK]), ALU.mult).then_inc(s_on, 1)

                base = count[0]
                with dve.Fori(0, NB // 2) as bb:
                    dve.wait_ge(s_onT, 2 * bb)
                    for u in range(2):
                        normalise(2 * bb + u, u)
                    for u in range(2):
                        b = 2 * bb + u
                        dve.wait_ge(s_yT, b + 1)
                        xb = x_all[:, bass.ds(b * NT, NT), :]
                        dve.tensor_tensor(xb, bank[4 + u][:, :].rearrange("p (i d) -> p i d", d=D), xb,
                                          ALU.add).then_inc(s_x2, 1)
                        dve.wait_ge(s_x2, b + 1)
                        for i in range(NT):
                            dve.bn_stats(stats[:, NT * b + i, :], x_all[:, NT * b + i, :]).then_inc(s_c1, 1)
                count[0] = base + TILES
                dve.wait_ge(s_c1, count[0])
                norm_stats(dve, link, ss[:, 0:TILES], tt[:, 0:TILES])
                dve.sem_inc(s_v3, 1)
                dve.wait_ge(s_v4, 1)
                newton(dve, link, dev[:, 0:TILES], ss[:, 0:TILES], rstd[:, :], tt[:, 0:TILES])
        ph.close()

        ph = ExitStack()
        fxh = tb("fxh", [P, 2, NT, D])
        fhT = tb("fhT", [P, 2, S])
        l0 = tb("l0", [P, 2, S])
        sg = tb("sg", [P, 2, S])
        h2 = tb("h2", [P, 2, S])
        fw = [tb(f"fw{i}", [P, TILES, E]) for i in range(4)]
        fa = [tb(f"fa{i}", [P, TILES]) for i in range(2)]
        h_all = hq[:, :, D:ROW]

        s_fx = sem("ff_normalised")
        s_fT = sem("ff_turned")
        s_fh = sem("ff_modulated")
        s_l0 = sem("ff_linear")
        s_l0c = sem("ff_linear_copied")
        s_sw = sem("ff_glu_products")
        s_sg = sem("ff_glu_gate")
        s_h2 = sem("ff_hidden")
        s_rl = sem("router_products")
        s_rlc = sem("router_copied")
        s_hk = sem("ff_hidden_kept")
        s_c2 = sem("router_chain")
        s_x0 = sem("router_exponent_in")
        s_x1 = sem("router_exponent_out")

        with nc.Block() as block:
            @block.scalar
            def _(act):
                with act.Fori(0, NB // 2) as bb:
                    for u in range(2):
                        b = 2 * bb + u
                        act.wait_ge(s_fT, b + 1)
                        act.activation(fhT[:, u, :], bank[u][:, :], ACT.Identity, bias=mods[:, 3, bass.ds(b, 1)],
                                       scale=mods[:, 4, bass.ds(b, 1)]).then_inc(s_fh, 1)
                        act.wait_ge(s_l0, b + 1)
                        act.activation(l0[:, u, :], bank[2][:, :], ACT.Identity,
                                       bias=bias[:, 0:1]).then_inc(s_l0c, 1)
                        act.wait_ge(s_sw, 2 * b + 1)
                        act.activation(sg[:, u, :], bank[3][:, :], ACT.Silu, bias=bias[:, 1:2]).then_inc(s_sg, 1)
                act.wait_ge(s_x0, 1)
                act.activation(fw[2][:, :, :], fw[2][:, :, :], ACT.Exp).then_inc(s_x1, 1)

            @block.gpsimd
            def _(pool):
                with pool.Fori(0, NB // 2) as bb:
                    for u in range(2):
                        b = 2 * bb + u
                        pool.wait_ge(s_h2, b + 1)
                        pool.tensor_copy(h_all[:, bass.ds(b * NT, NT), :],
                                         h2[:, u, :].rearrange("p (i d) -> p i d", d=D)).then_inc(s_hk, 1)

            @block.tensor
            def _(pe):
                with pe.Fori(0, NB // 2) as bb:
                    for u in range(2):
                        b = 2 * bb + u
                        pe.wait_ge(s_fx, b + 1)
                        for i in range(NT):
                            mm = pe.transpose(bank[u][:, i * P:(i + 1) * P], fxh[:, u, i, :], ident[:, :])
                        mm.then_inc(s_fT, 1)
                        pe.wait_ge(s_fh, b + 1)
                        pe.matmul(bank[2][:, :], mat[:, 0, :], fhT[:, u, :], start=True, stop=True).then_inc(s_l0, 1)
                        pe.wait_ge(s_l0c, b + 1)
                        pe.matmul(bank[3][:, :], mat[:, 1, :], l0[:, u, :], start=True, stop=True).then_inc(s_sw, 1)
                        pe.wait_ge(s_h2, b)
                        pe.matmul(bank[4][:, :], mat[:, 2, :], l0[:, u, :], start=True, stop=True).then_inc(s_sw, 1)
                        pe.wait_ge(s_h2, b + 1)
                        pe.wait_ge(s_rlc, b)
                        for i in range(NT):
                            mm = pe.matmul(bank[5][:, i * E:(i + 1) * E], h2[:, u, i * P:(i + 1) * P], gF[:, :],
                                           start=True, stop=True)
                        mm.then_inc(s_rl, 1)

            @block.vector
            def _(dve):
                count = [0]

                def link(ins):
                    count[0] += 1
                    ins.then_inc(s_c2, 1)
                    dve.wait_ge(s_c2, count[0])

                with dve.Fori(0, NB // 2) as bb:
                    dve.wait_ge(s_fT, 2 * bb)
                    for u in range(2):
                        for i in range(NT):
                            t = (2 * bb + u) * NT + i
                            ins = dve.tensor_scalar(fxh[:, u, i, :], x_all[:, t, :], mean[:, bass.ds(t, 1)],
                                                    rstd[:, bass.ds(t, 1)], ALU.subtract, ALU.mult)
                        ins.then_inc(s_fx, 1)
                    for u in range(2):
                        b = 2 * bb + u
                        dve.wait_ge(s_sg, b + 1)
                        dve.wait_ge(s_sw, 2 * b + 2)
                        if u == 0:
                            dve.wait_ge(s_hk, 2 * bb)
                        dve.scalar_tensor_tensor(out=h2[:, u, :], in0=bank[4][:, :], scalar=bias[:, 2:3],
                                                 in1=sg[:, u, :], op0=ALU.add, op1=ALU.mult).then_inc(s_h2, 1)
                        dve.wait_ge(s_rl, b + 1)
                        dve.tensor_copy(lg[:, bass.ds(b * NT, NT), :],
                                        bank[5][:, 0:NT * E].rearrange("p (i e) -> p i e", e=E)).then_inc(s_rlc, 1)
                dve.wait_ge(s_rlc, NB)
                left, one, t, w = (v[:, :, :] for v in fw)
                m = fa[0][:, :]
                for k in range(TOPF):
                    src = lg[:, :, :] if k == 0 else left
                    pick(dve, link, src, one, t, m)
                    link(dve.scalar_tensor_tensor(out=left, in0=one, scalar=LOW, in1=src, op0=ALU.mult, op1=ALU.add))
                    if k == 0:
                        link(dve.tensor_copy(w, one))
                    else:
                        link(dve.tensor_tensor(w, w, one, ALU.add))
                link(dve.tensor_reduce(m, lg[:, :, :], AX.X, ALU.max))
                link(dve.tensor_tensor(t, lg[:, :, :], m.unsqueeze(2).to_broadcast([P, TILES, E]), ALU.subtract))
                dve.sem_inc(s_x0, 1)
                dve.wait_ge(s_x1, 1)
                link(dve.tensor_tensor(w, w, t, ALU.mult))
                link(dve.tensor_reduce(m, w, AX.X, ALU.add))
                link(dve.reciprocal(fa[1][:, :], m))
                link(dve.tensor_tensor(w, w, fa[1][:, :].unsqueeze(2).to_broadcast([P, TILES, E]), ALU.mult))
                for part in range(3):
                    piece = w24[:, :, part * E:(part + 1) * E]
                    link(dve.tensor_copy(piece, w))
                    if part < 2:
                        link(dve.tensor_tensor(w, w, piece, ALU.subtract))
        ph.close()

        ph = ExitStack()
        wst = tb("wst", [P, 2, NT, 3 * E], BF16)
        wTs = tb("wTs", [3 * E, 2, S], BF16)
        eg = tb("eg", [P, 2, S])
        ep = tb("ep", [P, 2, S])
        ys = tb("ys", [P, S])
        l1 = tb("l1", [P, S])
        tg = tb("tg", [P, S])
        t2 = tb("t2", [P, S])
        t3 = tb("t3", [P, S])
        fin = tb("fin", [P, 2, NT, D])
        TAIL = (2, 4, 6, 8)
        NU = E + SH

        s_ws = sem("weights_staged")
        s_wt = sem("weights_turned")
        s_wtc = sem("weights_copied")
        s_eg = sem("expert_products")
        s_es = sem("expert_gate")
        s_eu = sem("expert_gated")
        s_ep = sem("expert_hidden")
        s_ey = sem("expert_sum_parts")
        s_yk = sem("expert_sum_copied")
        s_t1 = sem("tail_linear")
        s_t1c = sem("tail_linear_copied")
        s_t2 = sem("tail_gate_product")
        s_t2c = sem("tail_gate")
        s_t3 = sem("tail_up_product")
        s_t3c = sem("tail_hidden")
        s_t4 = sem("tail_scaled")
        s_t5 = sem("tail_turned")
        s_fin = sem("result_ready")
        s_out = [sem("result_stored0"), sem("result_stored1")]

        w_ps = bank[7][0:3 * E, 0:S // 2].bitcast(BF16)

        with nc.Block() as block:
            def pairs(eng, batch):
                for u in range(2):
                    batch(u, u, u == 0)
                with eng.Fori(1, NB // 2) as bb:
                    for u in range(2):
                        batch(2 * bb + u, u, False)

            @block.gpsimd
            def _(pool):
                def batch(b, u, first):
                    if u == 0:
                        pool.wait_ge(s_wt, b)
                    pool.tensor_copy(wst[:, u, :, :], w24[:, bass.ds(b * NT, NT), :]).then_inc(s_ws, 1)

                pairs(pool, batch)

            @block.sync
            def _(sp):
                ov = out.rearrange("b (i p) d -> b p i d", p=P)

                def batch(b, u):
                    sp.wait_ge(s_fin, b + 1)
                    sp.dma_start(ov[b], fin[:, u, :, :]).then_inc(s_out[u], 16)

                with sp.Fori(0, NB // 2) as bb:
                    for u in range(2):
                        batch(2 * bb + u, u)
                for u in range(2):
                    sp.wait_ge(s_out[u], 16 * (NB // 2))

            @block.tensor
            def _(pe):
                def turn_weights(b, u, first):
                    pe.wait_ge(s_ws, b + 1)
                    if not first or u:
                        pe.wait_ge(s_fin, b - 1)
                        pe.wait_ge(s_wtc, b)
                    for i in range(NT):
                        mm = pe.transpose(w_ps[:, i * P:(i + 1) * P], wst[:, u, i, :], identb[:, :])
                    mm.then_inc(s_wt, 1)

                def up(b, u, n, free):
                    k = NU * b + n
                    r = h_all[:, bass.ds(b * NT, NT), :]
                    if free:
                        pe.wait_ge(s_ep, k - 1)
                    pe.matmul(bank[1 + n % 2][:, :], w1s[:, n, :], r, start=True, stop=True)
                    mm = pe.matmul(bank[3 + n % 2][:, :], w3s[:, n, :], r, start=True, stop=True)
                    if n < E:
                        pe.wait_ge(s_wtc, b + 1)
                        mm = pe.matmul(bank[5 + n % 2][:, :], sel24[:, n, :], wTs[:, u, :], start=True, stop=True)
                    mm.then_inc(s_eg, 1)

                def down(b, n):
                    pe.wait_ge(s_ep, NU * b + n + 1)
                    pe.matmul(bank[0][:, :], w2s[:, n, :], ep[:, n % 2, :], start=(n == 0),
                              stop=(n == NU - 1)).then_inc(s_ey, 1)

                def tail(b, step):
                    if step == 0:
                        pe.wait_ge(s_yk, b + 1)
                        pe.matmul(bank[7][:, :], mat[:, 3, :], ys[:, :], start=True, stop=True).then_inc(s_t1, 1)
                    elif step == 1:
                        pe.wait_ge(s_t1c, b + 1)
                        pe.matmul(bank[7][:, :], mat[:, 4, :], l1[:, :], start=True, stop=True).then_inc(s_t2, 1)
                    elif step == 2:
                        pe.wait_ge(s_t2c, b + 1)
                        pe.matmul(bank[7][:, :], mat[:, 5, :], l1[:, :], start=True, stop=True).then_inc(s_t3, 1)
                    else:
                        pe.wait_ge(s_t4, b + 1)
                        for i in range(NT):
                            mm = pe.transpose(bank[7][:, i * P:(i + 1) * P], t3[:, i * P:(i + 1) * P], ident[:, :])
                        mm.then_inc(s_t5, 1)

                def batch(b, u, first):
                    turn_weights(b, u, first)
                    for n in range(NU):
                        up(b, u, n, not first or n >= 2)
                        if n:
                            if n == 1 and not first:
                                pe.wait_ge(s_yk, b)
                            down(b, n - 1)
                        elif not first:
                            down(b - 1, NU - 1)
                        if n in TAIL and not first:
                            tail(b - 1, TAIL.index(n))

                pairs(pe, batch)
                down(NB - 1, NU - 1)
                for step in range(4):
                    tail(NB - 1, step)

            @block.scalar
            def _(act):
                def gate(b, n):
                    act.wait_ge(s_eg, NU * b + n + 1)
                    act.activation(eg[:, n % 2, :], bank[1 + n % 2][:, :], ACT.Silu).then_inc(s_es, 1)

                def tail(b, step):
                    if step == 0:
                        act.wait_ge(s_t1, b + 1)
                        act.activation(l1[:, :], bank[7][:, :], ACT.Identity, bias=bias[:, 3:4]).then_inc(s_t1c, 1)
                    elif step == 1:
                        act.wait_ge(s_t2, b + 1)
                        act.activation(tg[:, :], bank[7][:, :], ACT.Silu, bias=bias[:, 4:5]).then_inc(s_t2c, 1)
                    elif step == 2:
                        act.wait_ge(s_t3c, b + 1)
                        act.activation(t3[:, :], t2[:, :], ACT.Copy, scale=mods[:, 5, bass.ds(b, 1)]).then_inc(s_t4, 1)

                def keep_sum(b):
                    act.wait_ge(s_ey, NU * b + NU)
                    act.activation(ys[:, :], bank[0][:, :], ACT.Copy).then_inc(s_yk, 1)

                def batch(b, u, first):
                    act.wait_ge(s_wt, b + 1)
                    act.activation(wTs[:, u, :], w_ps, ACT.Copy).then_inc(s_wtc, 1)
                    for n in range(NU):
                        gate(b, n)
                        if not first:
                            if n == 0:
                                keep_sum(b - 1)
                            if n == TAIL[0]:
                                tail(b - 1, 0)
                            if n == TAIL[1]:
                                tail(b - 1, 1)
                            if n == TAIL[2] + 1:
                                tail(b - 1, 2)

                pairs(act, batch)
                keep_sum(NB - 1)
                for step in range(3):
                    tail(NB - 1, step)

            @block.vector
            def _(dve):
                def hidden(b, n, free):
                    k = NU * b + n
                    dve.wait_ge(s_es, k + 1)
                    if n < E:
                        g = eg[:, n % 2, :]
                        dve.tensor_tensor(g, bank[3 + n % 2][:, :], g, ALU.mult).then_inc(s_eu, 1)
                        dve.wait_ge(s_eu, E * b + n + 1)
                        if free:
                            dve.wait_ge(s_ey, k - 1)
                        dve.tensor_tensor(ep[:, n % 2, :], bank[5 + n % 2][:, :], g, ALU.mult).then_inc(s_ep, 1)
                    else:
                        dve.wait_ge(s_ey, k - 1)
                        dve.tensor_tensor(ep[:, n % 2, :], bank[3 + n % 2][:, :], eg[:, n % 2, :],
                                          ALU.mult).then_inc(s_ep, 1)

                def tail(b, u, step):
                    if step == 2:
                        dve.wait_ge(s_t3, b + 1)
                        dve.scalar_tensor_tensor(out=t2[:, :], in0=bank[7][:, :], scalar=bias[:, 5:6], in1=tg[:, :],
                                                 op0=ALU.add, op1=ALU.mult).then_inc(s_t3c, 1)
                    else:
                        dve.wait_ge(s_t5, b + 1)
                        dve.wait_ge(s_out[u], stored(b, u))
                        dve.tensor_tensor(fin[:, u, :, :], bank[7][:, :].rearrange("p (i d) -> p i d", d=D),
                                          x_all[:, bass.ds(b * NT, NT), :], ALU.add).then_inc(s_fin, 1)

                def stored(b, u):
                    return 8 * (b - u)

                def batch(b, u, first):
                    for n in range(NU):
                        hidden(b, n, not first or n >= 2)
                        if not first and n == TAIL[2]:
                            tail(b - 1, 1 - u, 2)
                        if not first and n == TAIL[3]:
                            tail(b - 1, 1 - u, 3)

                pairs(dve, batch)
                tail(NB - 1, 1, 2)
                tail(NB - 1, 1, 3)
        ph.close()


def kernel(**inputs):
    import numpy as np
    import concourse.bacc as bacc
    from concourse.bass_utils import run_bass_kernel_spmd as run

    a = {k.removeprefix("L0_"): np.asarray(v) for k, v in inputs.items()}
    t = lambda m: np.ascontiguousarray(np.swapaxes(m, -1, -2))
    col = lambda v: np.ascontiguousarray(v.reshape(-1, 1))
    laid = {
        "x": a["attn_x"], "gate_wT": t(a["attn_gate_w"]), "q_w": a["attn_q_w"], "k_w": a["attn_k_w"],
        "v_wT": t(a["attn_v_w"]),
        "fmT": np.stack([np.tile(t(a[f"attn_fm{n}_w"]), (8, 8)) for n in ("q1", "q2", "k1", "k2")]),
        "norm_c": col(np.tile(a["attn_norm_w"], 8)), "o_wT": t(a["attn_o_w"]),
        "lin0": a["ffn_lin0_w"], "lin0_b": col(a["ffn_lin0_b"]), "s1w1": a["ffn_swi1_w1"], "s1b1": col(a["ffn_swi1_b1"]),
        "s1w2": a["ffn_swi1_w2"], "s1b2": col(a["ffn_swi1_b2"]), "fgateT": t(a["ffn_gate_w"]),
        "ew1": a["ffn_exp_w1"], "ew3": a["ffn_exp_w3"], "ew2": a["ffn_exp_w2"],
        "shw1": a["ffn_sh_w1"], "shw3": a["ffn_sh_w3"], "shw2": a["ffn_sh_w2"],
        "lin1": a["ffn_lin1_w"], "lin1_b": col(a["ffn_lin1_b"]), "s2w1": a["ffn_swi2_w1"], "s2b1": col(a["ffn_swi2_b1"]),
        "s2w2": a["ffn_swi2_w2"], "s2b2": col(a["ffn_swi2_b2"]), "cT": t(a["c"]), "wmod": a["wmod"],
    }
    nc = bacc.Bacc("TRN2", target_bir_lowering=False, num_devices=1)
    arrays, args = {}, {}
    for name, v in laid.items():
        arrays[f"in_{name}"] = np.ascontiguousarray(v)
        args[name] = nc.dram_tensor(f"in_{name}", v.shape, mybir.dt.from_np(v.dtype), kind="ExternalInput").ap()
    args["out"] = nc.dram_tensor("out_0", (NB, S, D), F32, kind="ExternalOutput").ap()
    adaln_block(nc, **args)
    r = run(nc, [arrays], core_ids=[0])
    return r.results[0]["out_0"]
```

```python
from contextlib import ExitStack

import concourse.bass as bass
from concourse import mybir

ALU = mybir.AluOpType
ACT = mybir.ActivationFunctionType
AX = mybir.AxisListType
F32 = mybir.dt.float32
F32R = mybir.dt.float32r
BF16 = mybir.dt.bfloat16
U32 = mybir.dt.uint32
I32 = mybir.dt.int32

P = 128
D = 128
NB = 16
S = 512
NT = S // P
TILES = NB * NT
E = 8
TOPA = 2
TOPF = 4
CAP = 256
H = 8
DK = 16
C = 64
NCH = CAP // C
ROW = 2 * D
G = NB * E
SH = 2
EPS = 1e-5
FAR = 1.0e6
LOW = -1.0e30
ZW = 1024


def bcast(ap, shape):
    return ap.to_broadcast(shape) if hasattr(ap, "to_broadcast") else ap.broadcast_to(shape)


def past(eng, semaphore, value):
    if not isinstance(value, int) or value > 0:
        eng.wait_ge(semaphore, value)


def adaln_block(nc, x, gate_wT, q_w, k_w, v_wT, fmT, norm_c, o_wT, lin0, lin0_b, s1w1, s1b1, s1w2, s1b2, fgateT,
                ew1, ew3, ew2, shw1, shw3, shw2, lin1, lin1_b, s2w1, s2b1, s2w2, s2b2, cT, wmod, out):
    ctx = ExitStack()
    with ctx:
        def sb(name, shape, dt=F32):
            return ctx.enter_context(nc.sbuf_tensor(name, shape, dt))

        def sem(name):
            return ctx.enter_context(nc.semaphore(name))

        hs = nc.dram_tensor("routed_rows", [G * CAP, ROW], F32, kind="Internal").ap()
        halves = hs.rearrange("r (k d) -> (r k) d", k=2)

        bank = [ctx.enter_context(nc.psum_tensor(f"bank{i}", [P, 512], F32)) for i in range(8)]

        PASSES = ((0, 0), (1, 0), (0, 1))

        x_all = sb("x_all", [P, TILES, D])
        hq = sb("hq", [P, TILES, ROW])
        ident = sb("ident", [P, P])
        identb = sb("identb", [P, P], BF16)
        headm = sb("headm", [P, P])
        parity = sb("parity", [P, 2])
        causal = sb("causal", [P, C])
        tri = sb("tri", [P, P], BF16)
        ones = sb("ones", [P, P], BF16)
        sel24 = sb("sel24", [3 * E, E, P], BF16)
        eslot = sb("eslot", [P, E])
        erow = sb("erow", [P, NB, E])
        mods = sb("mods", [P, 6, NB])
        gF = sb("gF", [P, E])
        mat = sb("mat", [P, 6, P])
        bias = sb("bias", [P, 6])
        w1s = sb("w1s", [P, E + SH, P])
        w3s = sb("w3s", [P, E + SH, P])
        w2s = sb("w2s", [P, E + SH, P])
        lg = sb("lg", [P, TILES, E])
        picked = sb("picked", [P, TILES, E], BF16)
        wslot = sb("wslot", [P, TILES, TOPA])
        idxs = sb("idxs", [P, TILES, TOPA], U32)
        idxg = sb("idxg", [P, TILES, TOPA], U32)

        pa = ExitStack()

        def pb(name, shape, dt=F32):
            return pa.enter_context(nc.sbuf_tensor(name, shape, dt))

        kp = pb("kp", [P, 2, 2, E, P], F32R)
        vT = pb("vT", [P, E, P])
        oT = pb("oT", [P, P])
        gA = pb("gA", [P, E])

        ph = ExitStack()
        zero = ph.enter_context(nc.sbuf_tensor("zero", [P, 1, ZW], F32))
        stats = ph.enter_context(nc.sbuf_tensor("stats", [P, TILES, 6], F32))
        mean = ph.enter_context(nc.sbuf_tensor("mean", [P, TILES], F32))
        rstd = ph.enter_context(nc.sbuf_tensor("rstd", [P, TILES], F32))
        q1T = ph.enter_context(nc.sbuf_tensor("q1T", [P, P], F32))
        q2T = ph.enter_context(nc.sbuf_tensor("q2T", [P, P], F32))
        k1T = ph.enter_context(nc.sbuf_tensor("k1T", [P, E, P], F32))
        k2T = ph.enter_context(nc.sbuf_tensor("k2T", [P, E, P], F32))
        kw_raw = ph.enter_context(nc.sbuf_tensor("kw_raw", [P, E, P], F32))
        q_raw = ph.enter_context(nc.sbuf_tensor("q_raw", [P, P], F32))
        fm = ph.enter_context(nc.sbuf_tensor("fm", [P, 4, P], F32))
        cT_s = ph.enter_context(nc.sbuf_tensor("cT_s", [P, NB], F32))
        wmod_s = ph.enter_context(nc.sbuf_tensor("wmod_s", [P, 6 * P], F32))
        normc = ph.enter_context(nc.sbuf_tensor("normc", [P, 1], F32))
        sgn = ph.enter_context(nc.sbuf_tensor("sgn", [P, NB], F32))
        xh = ph.enter_context(nc.sbuf_tensor("xh", [P, 2, NT, D], F32))
        hT = ph.enter_context(nc.sbuf_tensor("hT", [P, 2, S], F32))
        q1s = ph.enter_context(nc.sbuf_tensor("q1s", [P, 2, S], F32))
        qT = ph.enter_context(nc.sbuf_tensor("qT", [P, 2, S], F32))
        tw = [ph.enter_context(nc.sbuf_tensor(f"tw{i}", [P, TILES, E], F32)) for i in range(4)]
        ta = [ph.enter_context(nc.sbuf_tensor(f"ta{i}", [P, TILES], F32)) for i in range(3)]
        selp = ph.enter_context(nc.sbuf_tensor("selp", [P, TILES, E], F32))
        selb = ph.enter_context(nc.sbuf_tensor("selb", [P, TILES, E], BF16))

        MASKS = 18
        NW0, NW1 = 7, 1 + 6 + 6 + 8
        EARLY = 2
        PARTS = ((0, EARLY * NT), (EARLY * NT, TILES))

        s_x = [sem(f"x_loaded{i}") for i in range(4)]
        s_w0 = sem("routing_weights_loaded")
        s_w1 = sem("other_weights_loaded")
        s_mask = sem("masks_made")
        s_zero = sem("zero_made")
        s_z = [sem("first_rows_zeroed"), sem("other_rows_zeroed")]
        s_silu = sem("c_silu")
        s_mod = sem("mod_product")
        s_fold = sem("kq_folded")
        s_wcopy = sem("folded_copied")
        s_bd = sem("features_masked")
        s_ch = sem("vector_chain")
        s_var = sem("variance_ready")
        s_sq = sem("deviation_ready")
        s_mods = sem("mods_ready")
        s_xh = sem("normalised")
        s_xT = sem("normalised_turned")
        s_hT = sem("modulated")
        s_qp = sem("q_products")
        s_q1 = sem("q1_copied")
        s_qf = sem("q_features")
        s_lgp = sem("logit_products")
        s_hb = sem("h_turned")
        s_hqh = sem("h_rows_kept")
        s_lg = sem("logits_kept")
        s_qb = sem("q_turned")
        s_hqq = sem("q_rows_kept")
        s_e0 = sem("exponent_in")
        s_e1 = sem("exponent_out")
        s_selb = sem("selection_ready")
        s_cnt = sem("counts_ready")
        s_routed = sem("tiles_routed")
        s_scat = sem("rows_scattered")

        def scatter_tile(pool, rows_of, places):
            pool.indirect_dma_start(hs, bass.IndirectOffsetOnAxis(places, 0), rows_of, None,
                                    bounds_check=G * CAP - 1, oob_is_err=False).then_inc(s_scat, 16)

        def newton(dve, link, dev, var, y, t):
            link(dve.reciprocal(y, dev))
            link(dve.tensor_tensor(t, y, y, ALU.mult))
            link(dve.tensor_tensor(t, t, var, ALU.mult))
            link(dve.tensor_scalar(t, t, -0.5, 1.5, ALU.mult, ALU.add))
            link(dve.tensor_tensor(y, y, t, ALU.mult))

        def norm_stats(dve, link, var, t):
            link(dve.tensor_tensor(mean[:, :], stats[:, :, 1], stats[:, :, 4], ALU.add))
            link(dve.tensor_scalar(mean[:, :], mean[:, :], 0.5, None, ALU.mult))
            link(dve.tensor_tensor(t, stats[:, :, 1], stats[:, :, 4], ALU.subtract))
            link(dve.tensor_tensor(t, t, t, ALU.mult))
            link(dve.tensor_scalar(t, t, 0.25, EPS, ALU.mult, ALU.add))
            link(dve.tensor_tensor(var, stats[:, :, 2], stats[:, :, 5], ALU.add))
            link(dve.scalar_tensor_tensor(out=var, in0=var, scalar=1.0 / D, in1=t, op0=ALU.mult, op1=ALU.add))

        def pick(dve, link, left, first, t, m):
            n = left.shape[1]
            link(dve.tensor_reduce(m, left, AX.X, ALU.max))
            mb = m.unsqueeze(2).to_broadcast([P, n, E])
            link(dve.tensor_tensor(t, left, mb, ALU.is_equal))
            link(dve.tensor_tensor(t, t, eslot[:, :].unsqueeze(1).to_broadcast([P, n, E]), ALU.mult))
            link(dve.tensor_reduce(m, t, AX.X, ALU.max))
            link(dve.tensor_tensor(first, t, mb, ALU.is_equal))

        def choose_next(dve, link, k, tiles, left, one, t, m):
            src = lg[:, tiles, :] if k == 0 else left
            pick(dve, link, src, one, t, m)
            if k < TOPF - 1:
                link(dve.scalar_tensor_tensor(out=left, in0=one, scalar=LOW, in1=src, op0=ALU.mult, op1=ALU.add))
            if k == 0:
                link(dve.tensor_copy(picked[:, tiles, :], one))
            else:
                link(dve.tensor_tensor(picked[:, tiles, :], picked[:, tiles, :], one, ALU.add))

        with nc.Block() as block:
            @block.sync
            def _(sp):
                xv = x.rearrange("b (i p) d -> p (b i) d", p=P)
                q = TILES // 4
                for n in range(4):
                    sp.dma_start(x_all[:, n * q:(n + 1) * q, :], xv[:, n * q:(n + 1) * q, :]).then_inc(s_x[n], 16)
                    if n == 0:
                        for dst, src in ((cT_s[:, :], cT), (wmod_s[:, :], wmod), (q_raw[:, :], q_w),
                                         (fm[:, :, :], fmT.rearrange("f k c -> k f c")), (gA[:, :], gate_wT),
                                         (normc[:, :], norm_c), (kw_raw[:, :, :], k_w.rearrange("e k c -> k e c"))):
                            sp.dma_start(dst, src).then_inc(s_w0, 16)
                zr = CAP * E * ROW // (P * ZW)

                def zero_rows(b):
                    sp.dma_start(hs[b * CAP * E:(b + 1) * CAP * E, :].rearrange("(p r) w -> p (r w)", p=P)
                                 .rearrange("p (r w) -> p r w", w=ZW),
                                 zero[:, :, :].to_broadcast([P, zr, ZW])).then_inc(s_z[b >= EARLY], 16)

                sp.wait_ge(s_zero, 1)
                for b in range(EARLY):
                    zero_rows(b)
                for n, src in enumerate((lin0, s1w1, s1w2, lin1, s2w1, s2w2)):
                    sp.dma_start(mat[:, n, :], src).then_inc(s_w1, 16)
                for n, src in enumerate((lin0_b, s1b1, s1b2, lin1_b, s2b1, s2b2)):
                    sp.dma_start(bias[:, n:n + 1], src).then_inc(s_w1, 16)
                for dst, src in ((oT[:, :], o_wT), (gF[:, :], fgateT), (vT[:, :, :], v_wT.rearrange("e c k -> c e k")),
                                 (w1s[:, 0:E, :], ew1.rearrange("e d h -> d e h")),
                                 (w3s[:, 0:E, :], ew3.rearrange("e d h -> d e h")),
                                 (w2s[:, 0:E, :], ew2.rearrange("e h d -> h e d")),
                                 (w1s[:, E:E + SH, :], shw1.rearrange("d (s h) -> d s h", s=SH)),
                                 (w3s[:, E:E + SH, :], shw3.rearrange("d (s h) -> d s h", s=SH)),
                                 (w2s[:, E:E + SH, :], shw2.rearrange("(s h) d -> h s d", s=SH))):
                    sp.dma_start(dst, src).then_inc(s_w1, 16)
                for b in range(EARLY, NB):
                    zero_rows(b)
                sp.wait_ge(s_z[0], 16 * EARLY)
                sp.wait_ge(s_z[1], 16 * (NB - EARLY))

            def steps(eng, step):
                for i in range(2):
                    step(i, i, i)
                with eng.Fori(1, NB // 2 - 1) as ii:
                    for u in range(2):
                        step(2 * ii + u, u, 2)
                for i in range(NB - 2, NB + 1):
                    step(i, i % 2, i)

            @block.gpsimd
            def _(pool):
                made = [0]

                def link(ins):
                    made[0] += 1
                    ins.then_inc(s_mask, 1)
                    pool.wait_ge(s_mask, made[0])

                pool.memset(zero[:, :, :], 0.0).then_inc(s_zero, 1)
                link(pool.memset(ident[:, :], 0.0))
                link(pool.affine_select(out=ident[:, :], in_=ident[:, :], compare_op=ALU.not_equal, fill=1.0, base=0,
                                        pattern=[[-1, P]], channel_multiplier=1))
                link(pool.tensor_copy(identb[:, :], ident[:, :]))
                link(pool.memset(headm[:, :], 1.0))
                hv = headm[:, :].rearrange("p (h d) -> p h d", d=DK)
                link(pool.affine_select(out=hv, in_=hv, compare_op=ALU.is_ge, fill=0.0, base=0,
                                        pattern=[[-DK, H], [0, DK]], channel_multiplier=1))
                link(pool.affine_select(out=hv, in_=hv, compare_op=ALU.is_ge, fill=0.0, base=DK - 1,
                                        pattern=[[DK, H], [0, DK]], channel_multiplier=-1))
                link(pool.memset(causal[:, :], 1.0))
                link(pool.affine_select(out=causal[:, :], in_=causal[:, :], compare_op=ALU.is_ge, fill=0.0, base=C,
                                        pattern=[[1, C]], channel_multiplier=-1))
                link(pool.affine_select(out=causal[0:C, :], in_=causal[0:C, :], compare_op=ALU.is_ge, fill=0.0,
                                        base=0, pattern=[[1, C]], channel_multiplier=-1))
                link(pool.memset(tri[:, :], 1.0))
                link(pool.affine_select(out=tri[:, :], in_=tri[:, :], compare_op=ALU.is_ge, fill=0.0, base=0,
                                        pattern=[[-1, P]], channel_multiplier=1))
                link(pool.memset(ones[:, :], 1.0))
                link(pool.memset(sel24[:, :, :], 0.0))
                for part in range(3):
                    link(pool.affine_select(out=sel24[:, :, :], in_=sel24[:, :, :], compare_op=ALU.not_equal, fill=1.0,
                                            base=-part * E, pattern=[[-1, E], [0, P]], channel_multiplier=1))
                link(pool.iota(eslot[:, :], [[-1, E]], base=E, channel_multiplier=0,
                               allow_small_or_imprecise_dtypes=True))
                link(pool.iota(erow[:, :, :], [[E * CAP, NB], [CAP, E]], base=CAP, channel_multiplier=0,
                               allow_small_or_imprecise_dtypes=True))
                assert made[0] == MASKS
                pool.wait_ge(s_wcopy, 2 + E)
                for m, k in enumerate((k1T, k2T)):
                    pool.tensor_copy(kp[:, 0, m, :, :], k[:, :, :])
                pool.drain()
                for m, k in enumerate((k1T, k2T)):
                    pool.tensor_tensor(kp[:, 1, m, :, :], k[:, :, :], kp[:, 0, m, :, :], ALU.subtract)
                pool.wait_ge(s_z[0], 16 * EARLY)
                pool.wait_ge(s_hqh, NB)
                pool.wait_ge(s_hqq, NB)
                pool.wait_ge(s_routed, 1)
                for b in range(EARLY):
                    past(pool, s_scat, 16 * NT * TOPA * b)
                    for t in range(b * NT, (b + 1) * NT):
                        for s in range(TOPA):
                            scatter_tile(pool, hq[:, t, :], idxs[:, t, s:s + 1])

            @block.scalar
            def _(act):
                act.wait_ge(s_w0, 16 * NW0)
                act.activation(cT_s[:, :], cT_s[:, :], ACT.Silu).then_inc(s_silu, 1)
                act.wait_ge(s_fold, 1)
                act.activation(q1T[:, :], bank[6][:, 0:P], ACT.Copy).then_inc(s_wcopy, 1)
                act.activation(q2T[:, :], bank[6][:, P:2 * P], ACT.Copy).then_inc(s_wcopy, 1)
                for e in range(E):
                    act.wait_ge(s_fold, 2 + e)
                    act.activation(k1T[:, e, :], bank[e % 4][:, 0:P], ACT.Copy)
                    act.activation(k2T[:, e, :], bank[e % 4][:, P:2 * P], ACT.Copy).then_inc(s_wcopy, 1)
                act.wait_ge(s_var, 1)
                act.activation(ta[1][:, :], ta[0][:, :], ACT.Sqrt).then_inc(s_sq, 1)
                act.wait_ge(s_mods, 1)

                def step(i, u, at):
                    if at < NB:
                        act.wait_ge(s_xT, i + 1)
                        act.activation(hT[:, u, :], bank[0][:, :], ACT.Identity, bias=mods[:, 0, bass.ds(i, 1)],
                                       scale=mods[:, 1, bass.ds(i, 1)]).then_inc(s_hT, 1)
                    if at:
                        act.wait_ge(s_hb, i)
                        act.activation(hq[:, bass.ds((i - 1) * NT, NT), 0:D],
                                       bank[6][:, :].rearrange("p (i d) -> p i d", d=D), ACT.Copy).then_inc(s_hqh, 1)
                    if at < NB:
                        act.wait_ge(s_qp, i + 1)
                        past(act, s_qf, i - 1)
                        act.activation(q1s[:, u, :], bank[2 + 2 * u][:, :], ACT.Copy).then_inc(s_q1, 1)
                    if at:
                        act.wait_ge(s_qb, i)
                        act.activation(hq[:, bass.ds((i - 1) * NT, NT), D:ROW],
                                       bank[7][:, :].rearrange("p (i d) -> p i d", d=D), ACT.Copy).then_inc(s_hqq, 1)

                steps(act, step)
                for n, (lo, hi) in enumerate(PARTS):
                    act.wait_ge(s_e0, n + 1)
                    act.activation(tw[2][:, lo:hi, :], tw[2][:, lo:hi, :], ACT.Exp).then_inc(s_e1, 1)

            @block.tensor
            def _(pe):
                pe.wait_ge(s_w0, 16 * NW0)
                pe.wait_ge(s_silu, 1)
                for j in range(6):
                    mm = pe.matmul(bank[7][:, j * NB:(j + 1) * NB], wmod_s[:, j * P:(j + 1) * P], cT_s[:, :],
                                   start=True, stop=True)
                mm.then_inc(s_mod, 1)
                pe.wait_ge(s_bd, 1)
                mm = pe.matmul(bank[6][:, 0:2 * P], q_raw[:, :], fm[:, 0:2, :].rearrange("p f c -> p (f c)"),
                               start=True, stop=True)
                mm.then_inc(s_fold, 1)
                for e in range(E):
                    if e >= 4:
                        pe.wait_ge(s_wcopy, 2 + e - 3)
                    pe.matmul(bank[e % 4][:, 0:2 * P], kw_raw[:, e, :], fm[:, 2:4, :].rearrange("p f c -> p (f c)"),
                              start=True, stop=True).then_inc(s_fold, 1)
                pe.wait_ge(s_wcopy, 2 + E)
                pe.wait_ge(s_mask, MASKS)
                pe.wait_ge(s_mods, 1)

                def step(i, u, at):
                    if at < NB:
                        pe.wait_ge(s_xh, i + 1)
                        past(pe, s_hT, i)
                        for k in range(NT):
                            mm = pe.transpose(bank[0][:, k * P:(k + 1) * P], xh[:, u, k, :], ident[:, :])
                        mm.then_inc(s_xT, 1)
                    if at:
                        past(pe, s_lg, i - 1)
                        for k in range(NT):
                            mm = pe.matmul(bank[1][:, k * E:(k + 1) * E], hT[:, 1 - u, k * P:(k + 1) * P], gA[:, :],
                                           start=True, stop=True)
                        mm.then_inc(s_lgp, 1)
                        past(pe, s_hqh, i - 1)
                        for k in range(NT):
                            mm = pe.transpose(bank[6][:, k * P:(k + 1) * P], hT[:, 1 - u, k * P:(k + 1) * P],
                                              ident[:, :])
                        mm.then_inc(s_hb, 1)
                    if at < NB:
                        pe.wait_ge(s_hT, i + 1)
                        past(pe, s_qf, i - 1)
                        pe.matmul(bank[2 + 2 * u][:, :], q1T[:, :], hT[:, u, :], start=True, stop=True)
                        pe.matmul(bank[3 + 2 * u][:, :], q2T[:, :], hT[:, u, :], start=True,
                                  stop=True).then_inc(s_qp, 1)
                    if at:
                        pe.wait_ge(s_qf, i)
                        past(pe, s_hqq, i - 1)
                        for k in range(NT):
                            mm = pe.transpose(bank[7][:, k * P:(k + 1) * P], qT[:, 1 - u, k * P:(k + 1) * P],
                                              ident[:, :])
                        mm.then_inc(s_qb, 1)

                steps(pe, step)
                pe.wait_ge(s_hT, NB)
                for n, (lo, hi) in enumerate(PARTS):
                    pe.wait_ge(s_selb, n + 1)
                    flat = selb[:, lo:hi, :].rearrange("p t e -> p (t e)")
                    pe.matmul(bank[0][:, lo * E:hi * E], tri[:, :], flat, start=True, stop=True)
                    pe.matmul(bank[1][:, lo * E:hi * E], ones[:, :], flat, start=True, stop=True).then_inc(s_cnt, 1)

            @block.vector
            def _(dve):
                count = [0]

                def link(ins):
                    count[0] += 1
                    ins.then_inc(s_ch, 1)
                    dve.wait_ge(s_ch, count[0])

                def stats_of(n):
                    q = TILES // 4
                    dve.wait_ge(s_x[n], 16)
                    with dve.Fori(n * q // NT, (n + 1) * q // NT) as tt:
                        for i in range(NT):
                            dve.bn_stats(stats[:, NT * tt + i, :], x_all[:, NT * tt + i, :]).then_inc(s_ch, 1)
                    count[0] += q

                stats_of(0)
                dve.wait_ge(s_mask, MASKS)
                dve.wait_ge(s_w0, 16 * NW0)
                for f in range(4):
                    ins = dve.tensor_tensor(fm[:, f, :], fm[:, f, :], headm[:, :], ALU.mult)
                ins.then_inc(s_bd, 1)
                stats_of(1)
                dve.wait_ge(s_mod, 1)
                link(dve.tensor_copy(mods[:, :, :], bank[7][:, 0:6 * NB].rearrange("p (j b) -> p j b", b=NB)))
                for j in (1, 4):
                    link(dve.tensor_scalar(mods[:, j, :], mods[:, j, :], 1.0, None, ALU.add))
                for j in (2, 5):
                    link(dve.tensor_scalar(sgn[:, :], mods[:, j, :], 0.0, 2.0, ALU.is_ge, ALU.mult))
                    link(dve.tensor_scalar(sgn[:, :], sgn[:, :], -1.0, None, ALU.add))
                    link(dve.tensor_tensor(mods[:, j, :], mods[:, j, :], sgn[:, :], ALU.mult))
                    link(dve.tensor_scalar(mods[:, j, :], mods[:, j, :], 0.25, None, ALU.max))
                    link(dve.tensor_tensor(mods[:, j, :], mods[:, j, :], sgn[:, :], ALU.mult))
                dve.sem_inc(s_mods, 1)
                stats_of(2)
                stats_of(3)
                dve.wait_ge(s_ch, count[0])
                norm_stats(dve, link, ta[0][:, :], ta[2][:, :])
                dve.sem_inc(s_var, 1)
                dve.wait_ge(s_sq, 1)
                newton(dve, link, ta[1][:, :], ta[0][:, :], rstd[:, :], ta[2][:, :])

                def normalise(b, u):
                    past(dve, s_xT, b - 1)
                    for k in range(NT):
                        t = b * NT + k
                        ins = dve.tensor_scalar(xh[:, u, k, :], x_all[:, t, :], mean[:, bass.ds(t, 1)],
                                                rstd[:, bass.ds(t, 1)], ALU.subtract, ALU.mult)
                    ins.then_inc(s_xh, 1)

                def step(i, u, at):
                    if at < NB - 1:
                        normalise(i + 1, 1 - u)
                    if at:
                        dve.wait_ge(s_lgp, i)
                        dve.tensor_copy(lg[:, bass.ds((i - 1) * NT, NT), :],
                                        bank[1][:, 0:NT * E].rearrange("p (i e) -> p i e", e=E)).then_inc(s_lg, 1)
                    if at < NB:
                        dve.wait_ge(s_q1, i + 1)
                        past(dve, s_qb, i - 1)
                        dve.scalar_tensor_tensor(out=qT[:, u, :], in0=bank[3 + 2 * u][:, :], scalar=DK ** -0.5,
                                                 in1=q1s[:, u, :], op0=ALU.mult, op1=ALU.mult).then_inc(s_qf, 1)

                normalise(0, 0)
                steps(dve, step)
                for par in range(2):
                    link(dve.tensor_reduce(parity[:, par:par + 1],
                                           headm[:, :].rearrange("p (h r) -> p h r", r=2 * DK)[:, :, par * DK],
                                           AX.X, ALU.add))
                dve.wait_ge(s_w1, 16 * NW1)
                link(dve.tensor_scalar(oT[:, :], oT[:, :], normc[:, 0:1], None, ALU.mult))
                dve.wait_ge(s_lg, NB)
                def route(n, lo, hi):
                    tiles, size = slice(lo, hi), hi - lo
                    one, two, left, t, prod, cnt = (v[:, tiles, :] for v in (tw[0], tw[1], tw[3], tw[2], selp, lg))
                    m, kept, row = (v[:, tiles] for v in ta)
                    pick(dve, link, cnt, one, t, m)
                    link(dve.scalar_tensor_tensor(out=left, in0=one, scalar=LOW, in1=cnt, op0=ALU.mult, op1=ALU.add))
                    pick(dve, link, left, two, t, m)
                    link(dve.tensor_reduce(m, cnt, AX.X, ALU.max))
                    link(dve.tensor_tensor(t, cnt, m.unsqueeze(2).to_broadcast([P, size, E]), ALU.subtract))
                    dve.sem_inc(s_e0, 1)
                    link(dve.tensor_tensor(left, one, two, ALU.add))
                    link(dve.tensor_copy(selb[:, tiles, :], left))
                    dve.sem_inc(s_selb, 1)
                    dve.wait_ge(s_e1, n + 1)
                    link(dve.tensor_tensor(t, t, left, ALU.mult))
                    link(dve.tensor_reduce(m, t, AX.X, ALU.add))
                    link(dve.reciprocal(kept, m))
                    link(dve.tensor_tensor(t, t, kept.unsqueeze(2).to_broadcast([P, size, E]), ALU.mult))
                    dve.wait_ge(s_cnt, n + 1)
                    cb = cnt.rearrange("p (b i) e -> p b i e", i=NT)
                    tot = left.rearrange("p (b i) e -> p b i e", i=NT)
                    columns = slice(lo * E, hi * E)
                    link(dve.tensor_copy(cnt, bank[0][:, columns].rearrange("p (t e) -> p t e", e=E)))
                    link(dve.tensor_copy(left, bank[1][:, columns].rearrange("p (t e) -> p t e", e=E)))
                    for i in range(NT - 2, -1, -1):
                        link(dve.tensor_tensor(cb[:, :, i, :], cb[:, :, i, :], tot[:, :, i + 1, :], ALU.add))
                        if i:
                            link(dve.tensor_tensor(tot[:, :, i, :], tot[:, :, i, :], tot[:, :, i + 1, :], ALU.add))
                    keep = left
                    link(dve.tensor_scalar(keep, cnt, float(CAP), None, ALU.is_le))
                    for i in range(NT):
                        link(dve.tensor_tensor(cb[:, :, i, :], erow[:, lo // NT:hi // NT, :], cb[:, :, i, :],
                                               ALU.subtract))
                    for s, oh in enumerate((one, two)):
                        link(dve.tensor_tensor(oh, oh, keep, ALU.mult))
                        link(dve.tensor_reduce(kept, oh, AX.X, ALU.add))
                        link(dve.tensor_tensor(prod, oh, t, ALU.mult))
                        link(dve.tensor_reduce(wslot[:, tiles, s], prod, AX.X, ALU.add))
                        link(dve.tensor_tensor(prod, oh, cnt, ALU.mult))
                        link(dve.tensor_reduce(row, prod, AX.X, ALU.add))
                        link(dve.tensor_scalar(idxg[:, tiles, s], row, 2.0, None, ALU.mult))
                        link(dve.tensor_scalar(kept, kept, -FAR, FAR, ALU.mult, ALU.add))
                        link(dve.tensor_tensor(row, row, kept, ALU.add))
                        link(dve.tensor_copy(idxs[:, tiles, s], row))
                    dve.sem_inc(s_routed, 1)

                for n, (lo, hi) in enumerate(PARTS):
                    route(n, lo, hi)

        ph.close()

        ph = ExitStack()

        def tb(name, shape, dt=F32):
            return ph.enter_context(nc.sbuf_tensor(name, shape, dt))

        RING = 4
        AHEAD = 2
        srow = tb("srow", [P, NT, ROW])
        sidx = tb("sidx", [P, NT * TOPA], U32)
        rows = tb("rows", [P, RING, 2, ROW])
        hparts = tb("hparts", [P, 2, 2, 2 * P], F32R)
        turned = tb("turned", [P, RING, 2, 2 * P])
        k1s = tb("k1s", [P, 2 * P])
        kx = tb("kx", [P, NCH, 2, C])
        kr = tb("kr", [P, NCH - 1, P])
        vx = tb("vx", [P, 2, NCH, 4, 2, DK])
        att = tb("att", [P, NCH, 4, C])
        qx = tb("qx", [P, 2, NCH, 4, C])
        oTs = tb("oTs", [P, 2 * P])
        st = tb("st", [P, 3, P])
        ob = tb("ob", [P, 2, 2, P])

        s_ld = [sem(f"rows_loaded{i}") for i in range(RING)]
        s_t = sem("rows_turned")
        s_te = sem("turned_copied")
        s_tl = sem("turned_low_part")
        s_qa = sem("q_split_upper")
        s_qd = sem("q_split_lower")
        s_k = sem("k_products")
        s_ke = sem("k1_copied")
        s_kf = sem("k_features")
        s_kt = sem("k_turned")
        s_kte = sem("k_rows_copied")
        s_v = sem("values_ready")
        s_ve = sem("values_copied")
        s_vz = sem("zeros_between")
        s_s = sem("scores_ready")
        s_a = sem("scores_masked")
        s_st = sem("states_ready")
        s_stm = sem("states_masked")
        s_ste = sem("states_summed")
        s_o = sem("attended")
        s_oc = sem("attended_copied")
        s_ot = sem("attended_turned")
        s_oe = sem("attended_rows_ready")
        s_os = [sem("attended_stored0"), sem("attended_stored1")]

        gst = tb("gst", [P, NT * TOPA, D])
        gidx = tb("gidx", [P, NT * TOPA], U32)
        NV = NT * H + NT
        var = tb("var", [P, NV])
        inv = tb("inv", [P, NV])
        tmp = tb("tmp", [P, NV])
        jt = tb("jt", [P, S])
        jh = tb("jh", [P, S])
        jm = tb("jm", [P, S])
        js = tb("js", [P, S])
        h2 = tb("h2", [P, S])
        bst = tb("bst", [P, NT, 6])
        mv = tb("mv", [P, NT, 2])

        s_g = sem("rows_gathered")
        s_cc = sem("combine_chain")
        s_on = sem("heads_normalised")
        s_onT = sem("heads_turned")
        s_onc = sem("heads_copied")
        s_y = sem("projected")
        s_yc = sem("gated")
        s_yT = sem("gated_turned")
        s_x2 = sem("residual_added")
        s_ne = sem("norm_variance")
        s_nc = sem("deviation_chain")
        s_fx = sem("ff_normalised")
        s_fT = sem("ff_turned")
        s_fh = sem("ff_modulated")
        s_l0 = sem("ff_linear")
        s_l0c = sem("ff_linear_copied")
        s_w1 = sem("ff_gate_product")
        s_sg = sem("ff_gate")
        s_w2 = sem("ff_up_product")
        s_h2 = sem("ff_hidden")
        s_rl = sem("router_products")
        s_rlc = sem("router_copied")
        s_hk = sem("ff_hidden_kept")
        s_rk = sem("router_choices")
        h_all = hq[:, :, D:ROW]

        LAG = 3

        def rounds(eng, batch, end):
            for b in range(LAG + 1):
                batch(b, b)
            with eng.Fori(LAG + 1, NB - 2) as b:
                batch(b, LAG + 1)
            for b in range(NB - 2, end):
                batch(b, b)

        CHOICES = ((NB + 1, 0), (NB + 1, 1), (NB + 1, 3), (NB + 2, 3))
        CHOSEN = (NB - 2) * NT

        def there(at):
            return 0 <= at < NB


        with nc.Block() as block:
            @block.gpsimd
            def _(pool):
                def scatter(b):
                    pool.wait_ge(s_scat, 16 * NT * TOPA * b)
                    pool.tensor_copy(srow[:, :, :], hq[:, bass.ds(b * NT, NT), :])
                    pool.tensor_copy(sidx[:, :], idxs[:, bass.ds(b * NT, NT), :]
                                     .rearrange("p i s -> p (i s)"))
                    pool.drain()
                    for i in range(NT):
                        for s in range(TOPA):
                            k = i * TOPA + s
                            scatter_tile(pool, srow[:, i, :], sidx[:, k:k + 1])

                def gather(b):
                    for i in range(2):
                        pool.wait_ge(s_os[i], 16 * (E // 2) * (b + 1))
                    past(pool, s_onT, b)
                    pool.tensor_copy(gidx[:, :], idxg[:, bass.ds(b * NT, NT), :].rearrange("p i s -> p (i s)"))
                    pool.drain()
                    for k in range(NT * TOPA):
                        pool.indirect_dma_start(gst[:, k, :], None, halves,
                                                bass.IndirectOffsetOnAxis(gidx[:, k:k + 1], 0),
                                                bounds_check=2 * G * CAP - 1, oob_is_err=False).then_inc(s_g, 16)

                def batch(b, at):
                    if there(at - 1):
                        gather(b - 1)
                    if there(at + EARLY):
                        scatter(b + EARLY)
                    if there(at - 3):
                        pool.wait_ge(s_h2, b - 2)
                        pool.tensor_copy(h_all[:, bass.ds((b - 3) * NT, NT), :],
                                         h2[:, :].rearrange("p (i d) -> p i d", d=D)).then_inc(s_hk, 1)

                rounds(pool, batch, NB + LAG)
                pool.wait_ge(s_scat, 16 * NT * TOPA * NB)

            @block.sync
            def _(sp):
                hv = hs.rearrange("(g a p) w -> g p a w", a=2, p=P)
                ov = hs[:, 0:D].rearrange("(g a p) d -> g p a d", a=2, p=P)

                def load(g, slot):
                    sp.dma_start(rows[:, slot, :, :], hv[g]).then_inc(s_ld[slot], 16)

                def batch(b, at):
                    last = at == NB - 1
                    for e in range(E):
                        g = b * E + e
                        if not last or e < E - AHEAD - RING:
                            sp.wait_ge(s_t, g + AHEAD + 1)
                            if e == E - AHEAD - RING:
                                sp.wait_ge(s_scat, 16 * NT * TOPA * (b + 2))
                            load(g + AHEAD + RING, (e + AHEAD) % RING)
                        sp.wait_ge(s_oe, g + 1)
                        sp.dma_start(ov[g], ob[:, e % 2, :, :]).then_inc(s_os[e % 2], 16)

                sp.wait_ge(s_scat, 16 * NT * TOPA)
                for e in range(RING):
                    load(e, e)
                for e in range(AHEAD):
                    sp.wait_ge(s_t, e + 1)
                    load(RING + e, e)
                rounds(sp, batch, NB)
                for i in range(2):
                    sp.wait_ge(s_os[i], 16 * G // 2)

            @block.scalar
            def _(act):
                def turn(n, e):
                    act.wait_ge(s_t, n + 1)
                    act.activation(hparts[:, e % 2, 0, :], bank[2][:, 0:2 * P], ACT.Copy)
                    act.activation(turned[:, e % RING, :, :].rearrange("p a c -> p (a c)"), bank[2][:, :],
                                   ACT.Copy).then_inc(s_te, 1)

                def split_q(n, e):
                    for p in (0, 1):
                        r = slice(32 * p, 32 * p + 32)
                        ins = act.activation(qx[r, e % 2, :, p, :],
                                             turned[r, e % RING, 1, :].rearrange("r (n t) -> r n t", t=C), ACT.Copy)
                    ins.then_inc(s_qa, 1)

                def first_k(n):
                    act.wait_ge(s_k, n + 1)
                    past(act, s_kf, n)
                    act.activation(k1s[:, :], bank[5][:, 0:2 * P], ACT.Copy).then_inc(s_ke, 1)

                def keep_values(n, e):
                    act.wait_ge(s_v, n + 1)
                    for par in range(2):
                        r = slice(par * C, (par + 1) * C)
                        ins = act.activation(vx[r, e % 2, :, :, par, :],
                                             bank[6][r, 0:NCH * C].rearrange("r (n p d) -> r n p d", n=NCH, d=DK),
                                             ACT.Copy)
                    ins.then_inc(s_ve, 1)

                def keep_k(n):
                    act.wait_ge(s_kt, n + 1)
                    act.activation(kr[:, :, :].rearrange("p n c -> p (n c)"), bank[4][:, 0:3 * P],
                                   ACT.Copy).then_inc(s_kte, 1)

                def keep_outputs(g):
                    act.wait_ge(s_o, g + 1)
                    act.activation(oTs[:, :], bank[7][:, 0:2 * P], ACT.Copy).then_inc(s_oc, 1)

                def output_rows(g, b, e):
                    act.wait_ge(s_ot, g + 1)
                    past(act, s_os[e % 2], 16 * (b * (E // 2) + e // 2))
                    act.activation(ob[:, e % 2, :, :].rearrange("p a c -> p (a c)"), bank[4][:, 0:2 * P],
                                   ACT.Copy).then_inc(s_oe, 1)

                def step(b, at, e):
                    if e == 0 and there(at - 2):
                        act.wait_ge(s_onT, b - 1)
                        act.activation(jt[:, :], bank[3][:, :], ACT.Copy).then_inc(s_onc, 1)
                    elif e == 1 and there(at - 2):
                        act.wait_ge(s_y, b - 1)
                        act.activation(jm[:, :], bank[3][:, :], ACT.Copy,
                                       scale=mods[:, 2, bass.ds(b - 2, 1)]).then_inc(s_yc, 1)
                    elif e == 3 and there(at - 3):
                        act.wait_ge(s_l0, b - 2)
                        act.activation(jm[:, :], bank[3][:, :], ACT.Identity, bias=bias[:, 0:1]).then_inc(s_l0c, 1)
                    elif e == 4 and there(at - 3):
                        act.wait_ge(s_w1, b - 2)
                        act.activation(js[:, :], bank[3][:, :], ACT.Silu, bias=bias[:, 1:2]).then_inc(s_sg, 1)
                    elif e == 7 and there(at - 2):
                        act.wait_ge(s_fT, b - 1)
                        act.activation(jh[:, :], bank[3][:, :], ACT.Identity, bias=mods[:, 3, bass.ds(b - 2, 1)],
                                       scale=mods[:, 4, bass.ds(b - 2, 1)]).then_inc(s_fh, 1)

                def batch(b, at):
                    last = at == NB - 1
                    for e in range(E):
                        g = b * E + e
                        follows = not last or e < E - 1
                        if e == 0 and there(at - 1):
                            output_rows(g - 1, b - 1, E - 1)
                        elif e and there(at):
                            output_rows(g - 1, b, e - 1)
                        step(b, at, e)
                        if not there(at):
                            continue
                        if follows:
                            act.wait_ge(s_te, g + 2)
                            split_q(g + 1, e + 1)
                            first_k(g + 1)
                            keep_values(g + 1, e + 1)
                        keep_outputs(g)
                        if not last or e < E - AHEAD:
                            turn(g + AHEAD, e + AHEAD)
                        if follows:
                            keep_k(g + 1)

                act.activation(js[:, 0:1], bias[:, 1:2], ACT.Silu)
                for e in range(AHEAD):
                    turn(e, e)
                first_k(0)
                act.wait_ge(s_vz, 1)
                act.wait_ge(s_te, 1)
                split_q(0, 0)
                keep_values(0, 0)
                keep_k(0)
                rounds(act, batch, NB + LAG)

            @block.tensor
            def _(pe):
                def turn(n, e, b):
                    pe.wait_ge(s_ld[e % RING], 16 * (b * (E // RING) + e // RING + 1))
                    for part in range(2):
                        for a in range(2):
                            mm = pe.transpose(bank[2][:, part * 2 * P + a * P:part * 2 * P + (a + 1) * P],
                                              rows[:, e % RING, a, part * D:(part + 1) * D], ident[:, :])
                    mm.then_inc(s_t, 1)

                def keys(n, e):
                    pe.wait_ge(s_te, n + 1)
                    pe.wait_ge(s_tl, n + 1)
                    for m in range(2):
                        for wk, hk in PASSES:
                            mm = pe.matmul(bank[5][:, 2 * m * P:2 * (m + 1) * P], kp[:, wk, m, e % E, :],
                                           hparts[:, e % 2, hk, :], start=(wk + hk == 0), stop=(hk == 1))
                    mm.then_inc(s_k, 1)

                def values(n, e):
                    vh = vT[:, e % E, :].rearrange("c (p r d) -> c r p d", r=2, d=DK)
                    for par in range(2):
                        for n in range(NCH):
                            mm = pe.matmul(bank[6][par * C:(par + 1) * C, n * C:(n + 1) * C],
                                           turned[:, e % RING, 0, n * C:(n + 1) * C], vh[:, par], start=True, stop=True)
                    mm.then_inc(s_v, 1)

                def turn_k(n):
                    pe.wait_ge(s_kf, n + 1)
                    past(pe, s_oe, n - 1)
                    for m in range(NCH - 1):
                        mm = pe.transpose(bank[4][:, m * P:(m + 1) * P],
                                          kx[:, m, :, :].rearrange("p r t -> p (r t)"), ident[:, :])
                    mm.then_inc(s_kt, 1)

                def scores(g, e):
                    pe.wait_ge(s_kf, g + 1)
                    pe.wait_ge(s_qa, g + 1)
                    pe.wait_ge(s_qd, g + 1)
                    for n in range(NCH):
                        mm = pe.matmul(bank[n // 2][:, n % 2 * 4 * C:(n % 2 + 1) * 4 * C],
                                       kx[:, n, :, :].rearrange("p r t -> p (r t)"),
                                       qx[:, e % 2, n, :, :].rearrange("p h t -> p (h t)"), start=True, stop=True)
                        if n % 2:
                            mm.then_inc(s_s, 1)

                def states(g, e):
                    pe.wait_ge(s_kte, g + 1)
                    pe.wait_ge(s_ve, g + 1)
                    past(pe, s_oc, g)
                    for m in range(NCH - 1):
                        mm = pe.matmul(bank[7][:, m * P:(m + 1) * P], kr[:, m, :],
                                       vx[:, e % 2, m, :, :, :].rearrange("p h r d -> p (h r d)"),
                                       start=True, stop=True)
                    mm.then_inc(s_st, 1)

                def attend(g, e):
                    pe.wait_ge(s_a, 2 * (g + 1))
                    pe.wait_ge(s_ste, g + 1)
                    for n in range(1, NCH):
                        pe.matmul(bank[7][:, n * C:(n + 1) * C], st[:, n - 1, :],
                                  turned[:, e % RING, 1, n * C:(n + 1) * C], start=(n == 1), stop=True,
                                  skip_group_check=True)
                    for n in range(NCH):
                        for p in range(4):
                            mm = pe.matmul(bank[7][32 * p:32 * p + 32, n * C:(n + 1) * C],
                                           vx[:, e % 2, n, p, :, :].rearrange("p r d -> p (r d)"),
                                           att[:, n, p, :], start=False, stop=True, skip_group_check=True)
                    mm.then_inc(s_o, 1)

                def turn_outputs(g):
                    pe.wait_ge(s_oc, g + 1)
                    for a in range(2):
                        mm = pe.transpose(bank[4][:, a * P:(a + 1) * P], oTs[:, a * P:(a + 1) * P], ident[:, :])
                    mm.then_inc(s_ot, 1)

                def turn_job(src):
                    for i in range(NT):
                        mm = pe.transpose(bank[3][:, i * P:(i + 1) * P], src[:, i, :], ident[:, :])
                    return mm

                def by_tile(src):
                    return src[:, :].rearrange("p (i d) -> p i d", d=D)

                def product(w, src):
                    return pe.matmul(bank[3][:, :], w, src, start=True, stop=True)

                def step(b, at, e):
                    if e == 0 and there(at - 2):
                        pe.wait_ge(s_on, b - 1)
                        past(pe, s_fh, b - 2)
                        turn_job(gst[:, :, :].rearrange("p (i s) d -> p s i d", s=TOPA)[:, 1]).then_inc(s_onT, 1)
                    elif e == 1 and there(at - 2):
                        pe.wait_ge(s_onc, b - 1)
                        product(oT[:, :], jt[:, :]).then_inc(s_y, 1)
                    elif e == 2 and there(at - 2):
                        pe.wait_ge(s_yc, b - 1)
                        turn_job(by_tile(jm)).then_inc(s_yT, 1)
                    elif e == 3 and there(at - 3):
                        if there(at - 2):
                            pe.wait_ge(s_x2, b - 1)
                        pe.wait_ge(s_fh, b - 2)
                        product(mat[:, 0, :], jh[:, :]).then_inc(s_l0, 1)
                    elif e == 4 and there(at - 3):
                        pe.wait_ge(s_l0c, b - 2)
                        product(mat[:, 1, :], jm[:, :]).then_inc(s_w1, 1)
                    elif e == 5 and there(at - 3):
                        pe.wait_ge(s_sg, b - 2)
                        product(mat[:, 2, :], jm[:, :]).then_inc(s_w2, 1)
                    elif e == 6 and there(at - 3):
                        pe.wait_ge(s_h2, b - 2)
                        for i in range(NT):
                            mm = pe.matmul(bank[3][:, i * E:(i + 1) * E], h2[:, i * P:(i + 1) * P], gF[:, :],
                                           start=True, stop=True)
                        mm.then_inc(s_rl, 1)
                    elif e == 7 and there(at - 2):
                        pe.wait_ge(s_fx, b - 1)
                        if there(at - 3):
                            pe.wait_ge(s_rlc, b - 2)
                        else:
                            pe.wait_ge(s_x2, b - 1)
                        turn_job(by_tile(js)).then_inc(s_fT, 1)

                def batch(b, at):
                    last = at == NB - 1
                    for e in range(E):
                        g = b * E + e
                        follows = not last or e < E - 1
                        if there(at):
                            scores(g, e)
                            states(g, e)
                        if (e and there(at)) or (e == 0 and there(at - 1)):
                            turn_outputs(g - 1)
                        step(b, at, e)
                        if not there(at):
                            continue
                        if follows:
                            keys(g + 1, e + 1)
                            values(g + 1, e + 1)
                        attend(g, e)
                        if not last or e < E - AHEAD:
                            turn(g + AHEAD, e + AHEAD, b)
                        if follows:
                            turn_k(g + 1)

                turn(0, 0, 0)
                pe.wait_ge(s_te, 1)
                turn(1, 1, 0)
                keys(0, 0)
                values(0, 0)
                turn_k(0)
                rounds(pe, batch, NB + LAG)

            @block.vector
            def _(dve):
                def k_features(n):
                    dve.wait_ge(s_ke, n + 1)
                    for par in range(2):
                        ins = dve.scalar_tensor_tensor(
                            out=kx[:, :, par, :], in0=bank[5][:, 2 * P:4 * P].rearrange("p (n t) -> p n t", t=C),
                            scalar=parity[:, par:par + 1], in1=k1s[:, :].rearrange("p (n t) -> p n t", t=C),
                            op0=ALU.mult, op1=ALU.mult)
                    ins.then_inc(s_kf, 1)

                def low_h(n, e):
                    dve.wait_ge(s_te, n + 1)
                    dve.tensor_tensor(hparts[:, e % 2, 1, :], turned[:, e % RING, 0, :], hparts[:, e % 2, 0, :],
                                      ALU.subtract).then_inc(s_tl, 1)

                def split_q(n, e):
                    dve.wait_ge(s_te, n + 1)
                    for p in (2, 3):
                        r = slice(32 * p, 32 * p + 32)
                        ins = dve.tensor_copy(qx[r, e % 2, :, p, :],
                                              turned[r, e % RING, 1, :].rearrange("r (n t) -> r n t", t=C))
                    ins.then_inc(s_qd, 1)

                def mask_scores(g, a):
                    dve.wait_ge(s_s, 2 * g + a + 1)
                    dve.tensor_tensor(att[:, 2 * a:2 * a + 2, :, :].rearrange("k n p t -> k (n p) t"),
                                      bank[a][:, :].rearrange("k (x t) -> k x t", t=C),
                                      causal[:, :].unsqueeze(1).to_broadcast([P, 8, C]), ALU.mult).then_inc(s_a, 1)

                def sum_states(g, step):
                    if step == 0:
                        dve.wait_ge(s_st, g + 1)
                        dve.tensor_tensor(st[:, :, :], bank[7][:, 0:3 * P].rearrange("p (n d) -> p n d", d=P),
                                          headm[:, :].unsqueeze(1).to_broadcast([P, 3, P]), ALU.mult).then_inc(s_stm, 1)
                    else:
                        dve.wait_ge(s_stm, 2 * g + step)
                        dve.tensor_tensor(st[:, step, :], st[:, step, :], st[:, step - 1, :],
                                          ALU.add).then_inc(s_stm if step == 1 else s_ste, 1)

                COMBINE = 5
                CHAIN = 10

                def combine(b, e):
                    def link(n, ins):
                        ins.then_inc(s_cc, 1)
                        dve.wait_ge(s_cc, COMBINE * b + n)

                    gv = gst[:, :, :].rearrange("p (i s) d -> p i s d", s=TOPA)
                    o = gv[:, :, 0, :]
                    if e == 4:
                        dve.wait_ge(s_g, 16 * NT * TOPA * (b + 1))
                        w = wslot[:, bass.ds(b * NT, NT), :].rearrange("p i s -> p (i s)").unsqueeze(2)
                        link(1, dve.tensor_tensor(gst[:, :, :], gst[:, :, :], w.to_broadcast([P, NT * TOPA, D]),
                                                  ALU.mult))
                        link(2, dve.tensor_tensor(o, o, gv[:, :, 1, :], ALU.add))
                        link(3, dve.tensor_tensor(gv[:, :, 1, :], o, o, ALU.mult))
                    elif e == 5:
                        v = var[:, 0:NT * H]
                        link(4, dve.tensor_reduce(v.rearrange("p (i h) -> p i h", h=H),
                                                  gv[:, :, 1, :].rearrange("p i (h d) -> p i h d", d=DK), AX.X, ALU.add))
                        link(5, dve.tensor_scalar(v, v, 1.0 / DK, EPS, ALU.mult, ALU.add))
                    elif e == 7:
                        r = inv[:, 0:NT * H].rearrange("p (i h) -> p i h", h=H)
                        dve.tensor_tensor(gv[:, :, 1, :].rearrange("p i (h d) -> p i h d", d=DK),
                                          o.rearrange("p i (h d) -> p i h d", d=DK),
                                          r.unsqueeze(3).to_broadcast([P, NT, H, DK]), ALU.mult).then_inc(s_on, 1)

                def invert(b, at, e):
                    r = slice(0 if there(at - 1) else NT * H, NV if there(at - 2) else NT * H)
                    y, v, t = inv[:, r], var[:, r], tmp[:, r]

                    def link(n, ins):
                        ins.then_inc(s_nc, 1)
                        dve.wait_ge(s_nc, CHAIN * (b - 1) + n)

                    if e == 5:
                        link(1, dve.tensor_scalar(y.bitcast(I32), v.bitcast(I32), -0.5, float(0x5f3759df), ALU.mult,
                                                  ALU.add))
                    for k in ((0,) if e == 5 else (1, 2)):
                        link(3 * k + 2, dve.tensor_tensor(t, y, y, ALU.mult))
                        link(3 * k + 3, dve.scalar_tensor_tensor(out=t, in0=t, scalar=-0.5, in1=v, op0=ALU.mult,
                                                                 op1=ALU.mult))
                        link(3 * k + 4, dve.scalar_tensor_tensor(out=y, in0=t, scalar=1.5, in1=y, op0=ALU.add,
                                                                 op1=ALU.mult))

                def step(b, at, e):
                    if e == 2 and there(at - 2):
                        dve.wait_ge(s_yT, b - 1)
                        xb = x_all[:, bass.ds((b - 2) * NT, NT), :]
                        dve.tensor_tensor(xb, bank[3][:, :].rearrange("p (i d) -> p i d", d=D), xb,
                                          ALU.add).then_inc(s_x2, 1)
                        dve.drain()
                        for i in range(NT):
                            dve.bn_stats(bst[:, i, :], x_all[:, (b - 2) * NT + i, :])
                        dve.drain()
                        for i in range(NT):
                            dve.bn_aggr(mv[:, i, :], bst[:, i, :])
                        dve.drain()
                        dve.tensor_scalar(var[:, NT * H:NV], mv[:, :, 1], EPS, None, ALU.add).then_inc(s_ne, 1)
                        dve.wait_ge(s_ne, b - 1)
                    elif e == 5 and there(at - 3):
                        dve.wait_ge(s_w2, b - 2)
                        dve.wait_ge(s_sg, b - 2)
                        past(dve, s_hk, b - 3)
                        past(dve, s_rl, b - 3)
                        dve.scalar_tensor_tensor(out=h2[:, :], in0=bank[3][:, :], scalar=bias[:, 2:3], in1=js[:, :],
                                                 op0=ALU.add, op1=ALU.mult).then_inc(s_h2, 1)
                    elif e == 6:
                        if there(at - 3):
                            dve.wait_ge(s_rl, b - 2)
                            dve.tensor_copy(lg[:, bass.ds((b - 3) * NT, NT), :],
                                            bank[3][:, 0:NT * E].rearrange("p (i e) -> p i e", e=E)).then_inc(s_rlc, 1)
                        if there(at - 2):
                            past(dve, s_h2, b - 2)
                            for i in range(NT):
                                ins = dve.tensor_scalar(js[:, i * D:(i + 1) * D], x_all[:, (b - 2) * NT + i, :],
                                                        mv[:, i, 0:1], inv[:, NT * H + i:NT * H + i + 1], ALU.subtract,
                                                        ALU.mult)
                            ins.then_inc(s_fx, 1)

                choices = [0]

                def choose(k):
                    def link(ins):
                        choices[0] += 1
                        ins.then_inc(s_rk, 1)
                        dve.wait_ge(s_rk, choices[0])

                    left, one, t = (rows[:, i, :, :].rearrange("p a w -> p (a w)").rearrange("p (n e) -> p n e", e=E)
                                    [:, 0:CHOSEN] for i in range(3))
                    m = rows[:, 3, 0, 0:CHOSEN]
                    dve.wait_ge(s_rlc, NB - 2)
                    choose_next(dve, link, k, slice(0, CHOSEN), left, one, t, m)

                def batch(b, at):
                    last = at == NB - 1
                    for e in range(E):
                        g = b * E + e
                        if (at, e) in CHOICES:
                            choose(CHOICES.index((at, e)))
                        if there(at):
                            if not last or e < E - 1:
                                low_h(g + 1, e + 1)
                            mask_scores(g, 0)
                            mask_scores(g, 1)
                            sum_states(g, 0)
                            sum_states(g, 1)
                            sum_states(g, 2)
                            if not last or e < E - 1:
                                split_q(g + 1, e + 1)
                                k_features(g + 1)
                        if e == 5:
                            step(b, at, e)
                        if there(at - 1) and e >= 4:
                            combine(b - 1, e)
                        if e in (5, 6) and (there(at - 1) or there(at - 2)):
                            invert(b, at, e)
                        if e != 5:
                            step(b, at, e)

                dve.memset(vx[:, :, :, :, :, :], 0.0)
                dve.memset(qx[:, :, :, :, :], 0.0).then_inc(s_vz, 1)
                dve.wait_ge(s_vz, 1)
                split_q(0, 0)
                low_h(0, 0)
                k_features(0)
                rounds(dve, batch, NB + LAG)
        ph.close()

        pa.close()

        pf = ExitStack()
        w24 = pf.enter_context(nc.sbuf_tensor("w24", [P, TILES, 3 * E], BF16))
        hp = pf.enter_context(nc.sbuf_tensor("hp", [P, 2, 2, S], F32R))
        s_hl = sem("hidden_parts")

        def hidden_parts(pool, b, u):
            h = h_all[:, bass.ds(b * NT, NT), :]
            high, low = (hp[:, u, k, :].rearrange("p (i d) -> p i d", d=D) for k in range(2))
            pool.tensor_copy(high, h)
            pool.drain()
            pool.tensor_tensor(low, h, high, ALU.subtract).then_inc(s_hl, 1)

        w1p = pf.enter_context(nc.sbuf_tensor("w1p", [P, 2, E + SH, P], F32R))
        w3p = pf.enter_context(nc.sbuf_tensor("w3p", [P, 2, E + SH, P], F32R))
        w2p = pf.enter_context(nc.sbuf_tensor("w2p", [P, 2, E + SH, P], F32R))

        ph = ExitStack()
        fw = [tb(f"fw{i}", [P, TILES, E]) for i in range(4)]
        fa = [tb(f"fa{i}", [P, TILES]) for i in range(2)]

        s_c2 = sem("router_chain")
        s_x0 = sem("router_exponent_in")
        s_x1 = sem("router_exponent_out")
        s_wh = sem("high_parts")

        with nc.Block() as block:
            @block.gpsimd
            def _(pool):
                for n, (w, parts) in enumerate(((w1s, w1p), (w3s, w3p), (w2s, w2p))):
                    pool.wait_ge(s_wh, n + 1)
                    pool.tensor_tensor(parts[:, 1, :, :], w[:, :, :], parts[:, 0, :, :], ALU.subtract)
                for b in range(2):
                    hidden_parts(pool, b, b)

            @block.scalar
            def _(act):
                for w, parts in ((w1s, w1p), (w3s, w3p), (w2s, w2p)):
                    act.activation(parts[:, 0, :, :], w[:, :, :], ACT.Copy).then_inc(s_wh, 1)
                act.wait_ge(s_x0, 1)
                act.activation(fw[2][:, :, :], fw[2][:, :, :], ACT.Exp).then_inc(s_x1, 1)

            @block.vector
            def _(dve):
                count = [0]

                def link(ins):
                    count[0] += 1
                    ins.then_inc(s_c2, 1)
                    dve.wait_ge(s_c2, count[0])

                left, one, t, w = (v[:, :, :] for v in fw)
                m = fa[0][:, :]
                rest = slice(CHOSEN, TILES)
                for k in range(TOPF):
                    choose_next(dve, link, k, rest, left[:, rest], one[:, rest], t[:, rest], m[:, rest])
                link(dve.tensor_reduce(m, lg[:, :, :], AX.X, ALU.max))
                link(dve.tensor_tensor(t, lg[:, :, :], m.unsqueeze(2).to_broadcast([P, TILES, E]), ALU.subtract))
                dve.sem_inc(s_x0, 1)
                dve.wait_ge(s_x1, 1)
                link(dve.tensor_tensor(w, picked[:, :, :], t, ALU.mult))
                link(dve.tensor_reduce(m, w, AX.X, ALU.add))
                link(dve.reciprocal(fa[1][:, :], m))
                link(dve.tensor_tensor(w, w, fa[1][:, :].unsqueeze(2).to_broadcast([P, TILES, E]), ALU.mult))
                for part in range(3):
                    piece = w24[:, :, part * E:(part + 1) * E]
                    link(dve.tensor_copy(piece, w))
                    if part < 2:
                        link(dve.tensor_tensor(w, w, piece, ALU.subtract))
        ph.close()

        ph = ExitStack()
        wst = tb("wst", [P, 2, NT, 3 * E], BF16)
        wTs = tb("wTs", [3 * E, 2, S], BF16)
        eg = tb("eg", [P, 2, S])
        ep = tb("ep", [P, 2, S])
        epp = tb("epp", [P, 2, 2, S], F32R)
        ys = tb("ys", [P, S])
        l1 = tb("l1", [P, S])
        tg = tb("tg", [P, S])
        t2 = tb("t2", [P, S])
        t3 = tb("t3", [P, S])
        fin = tb("fin", [P, 2, NT, D])
        TAIL = (2, 4, 6, 8)
        NU = E + SH

        s_ws = sem("weights_staged")
        s_wt = sem("weights_turned")
        s_wtc = sem("weights_copied")
        s_eg = sem("expert_products")
        s_es = sem("expert_gate")
        s_eu = sem("expert_gated")
        s_ep = sem("expert_hidden")
        s_eh = sem("expert_hidden_high")
        s_el = sem("expert_hidden_low")
        s_ey = sem("expert_sum_parts")
        s_yk = sem("expert_sum_copied")
        s_t1 = sem("tail_linear")
        s_t1c = sem("tail_linear_copied")
        s_t2 = sem("tail_gate_product")
        s_t2c = sem("tail_gate")
        s_t3 = sem("tail_up_product")
        s_t3c = sem("tail_hidden")
        s_t4 = sem("tail_scaled")
        s_t5 = sem("tail_turned")
        s_fin = sem("result_ready")
        s_out = [sem("result_stored0"), sem("result_stored1")]

        w_ps = bank[7][0:3 * E, 0:S // 2].bitcast(BF16)

        with nc.Block() as block:
            def pairs(eng, batch):
                for u in range(2):
                    batch(u, u, u == 0)
                with eng.Fori(1, NB // 2) as bb:
                    for u in range(2):
                        batch(2 * bb + u, u, False)

            @block.gpsimd
            def _(pool):
                def batch(b, u, first):
                    if u == 0:
                        past(pool, s_wt, b)
                    pool.tensor_copy(wst[:, u, :, :], w24[:, bass.ds(b * NT, NT), :]).then_inc(s_ws, 1)
                    if not isinstance(b, int):
                        pool.wait_ge(s_eg, NU * (b - 1))
                        hidden_parts(pool, b, u)

                pairs(pool, batch)

            @block.sync
            def _(sp):
                ov = out.rearrange("b (i p) d -> b p i d", p=P)

                def batch(b, u):
                    sp.wait_ge(s_fin, b + 1)
                    sp.dma_start(ov[b], fin[:, u, :, :]).then_inc(s_out[u], 16)

                for u in range(2):
                    sp.sem_inc(s_out[u], 1)
                with sp.Fori(0, NB // 2) as bb:
                    for u in range(2):
                        batch(2 * bb + u, u)
                for u in range(2):
                    sp.wait_ge(s_out[u], 1 + 16 * (NB // 2))

            @block.tensor
            def _(pe):
                def turn_weights(b, u, first):
                    pe.wait_ge(s_ws, b + 1)
                    if not first or u:
                        past(pe, s_fin, b - 1)
                        pe.wait_ge(s_wtc, b)
                    for i in range(NT):
                        mm = pe.transpose(w_ps[:, i * P:(i + 1) * P], wst[:, u, i, :], identb[:, :])
                    mm.then_inc(s_wt, 1)

                def up(b, u, n, free):
                    k = NU * b + n
                    if n == 0:
                        pe.wait_ge(s_hl, b + 1)
                    if free:
                        pe.wait_ge(s_ep, k - 1)
                    for ps, w in ((bank[1 + n % 2], w1p), (bank[3 + n % 2], w3p)):
                        for wk, hk in PASSES:
                            mm = pe.matmul(ps[:, :], w[:, wk, n, :], hp[:, u, hk, :], start=(wk + hk == 0),
                                           stop=(hk == 1))
                    if n < E:
                        pe.wait_ge(s_wtc, b + 1)
                        mm = pe.matmul(bank[5 + n % 2][:, :], sel24[:, n, :], wTs[:, u, :], start=True, stop=True)
                    mm.then_inc(s_eg, 1)

                def down(b, n):
                    pe.wait_ge(s_el, NU * b + n + 1)
                    for wk, hk in PASSES:
                        mm = pe.matmul(bank[0][:, :], w2p[:, wk, n, :], epp[:, n % 2, hk, :],
                                       start=(n + wk + hk == 0), stop=(n == NU - 1 and hk == 1))
                    mm.then_inc(s_ey, 1)

                def tail(b, step):
                    if step == 0:
                        pe.wait_ge(s_yk, b + 1)
                        pe.matmul(bank[7][:, :], mat[:, 3, :], ys[:, :], start=True, stop=True).then_inc(s_t1, 1)
                    elif step == 1:
                        pe.wait_ge(s_t1c, b + 1)
                        pe.matmul(bank[7][:, :], mat[:, 4, :], l1[:, :], start=True, stop=True).then_inc(s_t2, 1)
                    elif step == 2:
                        pe.wait_ge(s_t2c, b + 1)
                        pe.matmul(bank[7][:, :], mat[:, 5, :], l1[:, :], start=True, stop=True).then_inc(s_t3, 1)
                    else:
                        pe.wait_ge(s_t4, b + 1)
                        for i in range(NT):
                            mm = pe.transpose(bank[7][:, i * P:(i + 1) * P], t3[:, i * P:(i + 1) * P], ident[:, :])
                        mm.then_inc(s_t5, 1)

                def batch(b, u, first):
                    turn_weights(b, u, first)
                    for n in range(NU):
                        up(b, u, n, not first or n >= 2)
                        if n >= 2:
                            if n == 2 and not first:
                                pe.wait_ge(s_yk, b)
                            down(b, n - 2)
                        elif not first:
                            down(b - 1, NU - 2 + n)
                        if n in TAIL and not first:
                            tail(b - 1, TAIL.index(n))

                pairs(pe, batch)
                for n in (NU - 2, NU - 1):
                    down(NB - 1, n)
                for step in range(4):
                    tail(NB - 1, step)

            @block.scalar
            def _(act):
                def gate(b, n):
                    act.wait_ge(s_eg, NU * b + n + 1)
                    act.activation(eg[:, n % 2, :], bank[1 + n % 2][:, :], ACT.Silu).then_inc(s_es, 1)

                def tail(b, step):
                    if step == 0:
                        act.wait_ge(s_t1, b + 1)
                        act.activation(l1[:, :], bank[7][:, :], ACT.Identity, bias=bias[:, 3:4]).then_inc(s_t1c, 1)
                    elif step == 1:
                        act.wait_ge(s_t2, b + 1)
                        act.activation(tg[:, :], bank[7][:, :], ACT.Silu, bias=bias[:, 4:5]).then_inc(s_t2c, 1)
                    elif step == 2:
                        act.wait_ge(s_t3c, b + 1)
                        act.activation(t3[:, :], t2[:, :], ACT.Copy, scale=mods[:, 5, bass.ds(b, 1)]).then_inc(s_t4, 1)

                def high_part(b, n, free):
                    k = NU * b + n
                    act.wait_ge(s_ep, k + 1)
                    if free:
                        act.wait_ge(s_ey, k - 1)
                    act.activation(epp[:, n % 2, 0, :], ep[:, n % 2, :], ACT.Copy).then_inc(s_eh, 1)

                def keep_sum(b):
                    act.wait_ge(s_ey, NU * b + NU)
                    act.activation(ys[:, :], bank[0][:, :], ACT.Copy).then_inc(s_yk, 1)

                def batch(b, u, first):
                    act.wait_ge(s_wt, b + 1)
                    act.activation(wTs[:, u, :], w_ps, ACT.Copy).then_inc(s_wtc, 1)
                    for n in range(NU):
                        gate(b, n)
                        if n:
                            high_part(b, n - 1, not first or n > 2)
                        elif not first:
                            high_part(b - 1, NU - 1, True)
                        if not first:
                            if n == 1:
                                keep_sum(b - 1)
                            if n == TAIL[0]:
                                tail(b - 1, 0)
                            if n == TAIL[1]:
                                tail(b - 1, 1)
                            if n == TAIL[2] + 1:
                                tail(b - 1, 2)

                pairs(act, batch)
                high_part(NB - 1, NU - 1, True)
                keep_sum(NB - 1)
                for step in range(3):
                    tail(NB - 1, step)

            @block.vector
            def _(dve):
                def low_part(b, n, free):
                    k = NU * b + n
                    dve.wait_ge(s_eh, k + 1)
                    if free:
                        dve.wait_ge(s_ey, k - 1)
                    dve.tensor_tensor(epp[:, n % 2, 1, :], ep[:, n % 2, :], epp[:, n % 2, 0, :],
                                      ALU.subtract).then_inc(s_el, 1)

                def hidden(b, n, first):
                    k = NU * b + n
                    free = not first or n >= 2
                    dve.wait_ge(s_es, k + 1)
                    g = eg[:, n % 2, :]
                    if n < E:
                        dve.tensor_tensor(g, bank[3 + n % 2][:, :], g, ALU.mult).then_inc(s_eu, 1)
                    if n:
                        low_part(b, n - 1, not first or n > 2)
                    elif not first:
                        low_part(b - 1, NU - 1, True)
                    if free:
                        dve.wait_ge(s_el, k - 1)
                    if n < E:
                        dve.wait_ge(s_eu, E * b + n + 1)
                        dve.tensor_tensor(ep[:, n % 2, :], bank[5 + n % 2][:, :], g, ALU.mult).then_inc(s_ep, 1)
                    else:
                        dve.tensor_tensor(ep[:, n % 2, :], bank[3 + n % 2][:, :], g, ALU.mult).then_inc(s_ep, 1)

                def tail(b, u, step):
                    if step == 2:
                        dve.wait_ge(s_t3, b + 1)
                        dve.scalar_tensor_tensor(out=t2[:, :], in0=bank[7][:, :], scalar=bias[:, 5:6], in1=tg[:, :],
                                                 op0=ALU.add, op1=ALU.mult).then_inc(s_t3c, 1)
                    else:
                        dve.wait_ge(s_t5, b + 1)
                        dve.wait_ge(s_out[u], stored(b, u))
                        dve.tensor_tensor(fin[:, u, :, :], bank[7][:, :].rearrange("p (i d) -> p i d", d=D),
                                          x_all[:, bass.ds(b * NT, NT), :], ALU.add).then_inc(s_fin, 1)

                def stored(b, u):
                    return 1 + 8 * (b - u)

                def batch(b, u, first):
                    for n in range(NU):
                        hidden(b, n, first)
                        if not first and n == TAIL[2]:
                            tail(b - 1, 1 - u, 2)
                        if not first and n == TAIL[3]:
                            tail(b - 1, 1 - u, 3)

                pairs(dve, batch)
                low_part(NB - 1, NU - 1, True)
                tail(NB - 1, 1, 2)
                tail(NB - 1, 1, 3)
        ph.close()
        pf.close()


def kernel(**inputs):
    import numpy as np
    import concourse.bacc as bacc
    from concourse.bass_utils import run_bass_kernel_spmd as run

    a = {k.removeprefix("L0_"): np.asarray(v) for k, v in inputs.items()}
    t = lambda m: np.ascontiguousarray(np.swapaxes(m, -1, -2))
    col = lambda v: np.ascontiguousarray(v.reshape(-1, 1))
    laid = {
        "x": a["attn_x"], "gate_wT": t(a["attn_gate_w"]), "q_w": a["attn_q_w"], "k_w": a["attn_k_w"],
        "v_wT": t(a["attn_v_w"]),
        "fmT": np.stack([np.tile(t(a[f"attn_fm{n}_w"]), (8, 8)) for n in ("q1", "q2", "k1", "k2")]),
        "norm_c": col(np.tile(a["attn_norm_w"], 8)), "o_wT": t(a["attn_o_w"]),
        "lin0": a["ffn_lin0_w"], "lin0_b": col(a["ffn_lin0_b"]), "s1w1": a["ffn_swi1_w1"], "s1b1": col(a["ffn_swi1_b1"]),
        "s1w2": a["ffn_swi1_w2"], "s1b2": col(a["ffn_swi1_b2"]), "fgateT": t(a["ffn_gate_w"]),
        "ew1": a["ffn_exp_w1"], "ew3": a["ffn_exp_w3"], "ew2": a["ffn_exp_w2"],
        "shw1": a["ffn_sh_w1"], "shw3": a["ffn_sh_w3"], "shw2": a["ffn_sh_w2"],
        "lin1": a["ffn_lin1_w"], "lin1_b": col(a["ffn_lin1_b"]), "s2w1": a["ffn_swi2_w1"], "s2b1": col(a["ffn_swi2_b1"]),
        "s2w2": a["ffn_swi2_w2"], "s2b2": col(a["ffn_swi2_b2"]), "cT": t(a["c"]), "wmod": a["wmod"],
    }
    nc = bacc.Bacc("TRN2", target_bir_lowering=False, num_devices=1)
    arrays, args = {}, {}
    for name, v in laid.items():
        arrays[f"in_{name}"] = np.ascontiguousarray(v)
        args[name] = nc.dram_tensor(f"in_{name}", v.shape, mybir.dt.from_np(v.dtype), kind="ExternalInput").ap()
    args["out"] = nc.dram_tensor("out_0", (NB, S, D), F32, kind="ExternalOutput").ap()
    adaln_block(nc, **args)
    r = run(nc, [arrays], core_ids=[0])
    return r.results[0]["out_0"]
```
